# Optimizing a Trainium2 kernel written in Bass

```python
import numpy as np
import jax
import jax.numpy as jnp

def _softmax(x, axis=-1):
    return jax.nn.softmax(x, axis=axis)

def _gelu(x):
    return jax.nn.gelu(x, approximate=True)

def _silu(x):
    return jax.nn.silu(x)

def _sigmoid(x):
    return jax.nn.sigmoid(x)

def _layernorm(x, axis=-1, eps=1e-05):
    m = jnp.mean(x, axis=axis, keepdims=True)
    v = jnp.var(x, axis=axis, keepdims=True)
    return (x - m) / jnp.sqrt(v + eps)

def _scatter_add(tgt, idx, src, axis=0):
    return tgt.at[idx].add(src)

def _segment_sum(src, seg, n):
    return jax.ops.segment_sum(src, seg, n)
kernel_name = 'mk_xattn_ffn_d2_seqx_r8_6012ba'

def setup_inputs(seed: int=0):
    np.random.seed(seed)
    _w = jnp.asarray

    def _rec_inputs():
        import jax
        import jax.numpy as jnp
        _rk = jax.random.key(seed)
        x = -0.0003929 + 0.9999 * jax.random.normal(jax.random.fold_in(_rk, 1), (16, 56, 256), jnp.float32)
        _lenS = 56 - jax.random.randint(jax.random.fold_in(_rk, 7), (16,), 0, max(1, 56 // 4) + 1, jnp.int32)
        _lenS2 = 1500 - jax.random.randint(jax.random.fold_in(_rk, 8), (16,), 0, max(1, 1500 // 4) + 1, jnp.int32)
        _ctx_1024P = jax.random.normal(jax.random.fold_in(_rk, 11), (16, 16, 128), jnp.float32)
        _ctx_1024c = jax.random.dirichlet(jax.random.fold_in(_rk, 511), 0.3 * jnp.ones((16,), jnp.float32), (16, 1500))
        _ctx_1024t = jnp.einsum('bsk,bkd->bsd', _ctx_1024c, _ctx_1024P)
        _ctx_1024t = _ctx_1024t * jax.lax.rsqrt(jnp.mean(jnp.square(_ctx_1024t)) + 1e-12) * 0.953939
        ctx_1024 = -0.000494167 + 1.00018 * (_ctx_1024t + 0.3 * jax.random.normal(jax.random.fold_in(_rk, 611), (16, 1500, 128), jnp.float32))
        _validS = jnp.arange(56)[None, :] < _lenS[:, None]
        _validS2 = jnp.arange(1500)[None, :] < _lenS2[:, None]
        _causal = jnp.tril(jnp.ones((56, 56), dtype=bool))
        mask_BxS2_bf1 = jnp.ones((16, 1500), dtype=bool)
        return (x, ctx_1024, mask_BxS2_bf1)
    x, ctx_1024, mask_BxS2_bf1 = _rec_inputs()

    def _L0_xattn_setup():
        import jax, jax.numpy as jnp
        import numpy as np
        N_HEADS = 16
        N_KV_HEADS = 8
        HEAD_DIM = 128
        D_TEXT = 256
        D_VISION = 128
        GROUPS = N_HEADS // N_KV_HEADS
        key = jax.random.key(seed)
        ks = jax.random.split(key, 6)
        B, T_text, T_vis = (4, 256, 72)
        text_hidden = jax.random.normal(ks[0], (B, T_text, D_TEXT), dtype=jnp.float32)
        vision_tokens = jax.random.normal(ks[1], (B, T_vis, D_VISION), dtype=jnp.float32)
        vision_mask = jnp.ones((B, T_vis), dtype=bool)
        s = 0.02
        Wq = jax.random.normal(ks[2], (D_TEXT, N_HEADS * HEAD_DIM), dtype=jnp.float32) * s
        Wk = jax.random.normal(ks[3], (D_VISION, N_KV_HEADS * HEAD_DIM), dtype=jnp.float32) * s
        Wv = jax.random.normal(ks[4], (D_VISION, N_KV_HEADS * HEAD_DIM), dtype=jnp.float32) * s
        Wo = jax.random.normal(ks[5], (N_HEADS * HEAD_DIM, D_TEXT), dtype=jnp.float32) * s
        return {'text_hidden': text_hidden, 'vision_tokens': vision_tokens, 'vision_mask': vision_mask, 'Wq': Wq, 'Wk': Wk, 'Wv': Wv, 'Wo': Wo}
    _L0_xattn_all = _L0_xattn_setup()
    _L0_xattn_in = {k: v for k, v in _L0_xattn_all.items() if k in ('Wq', 'Wk', 'Wv', 'Wo')}
    del _L0_xattn_all

    def _L0_ffn_setup():
        import math
        import jax, jax.numpy as jnp
        import numpy as np
        DIM = 256
        RANK = 8
        B, T = (4, 512)

        def _orthogonal(key, n):
            a = jax.random.normal(key, (n, n), dtype=jnp.float32)
            q, r = jnp.linalg.qr(a)
            q = q * jnp.sign(jnp.diagonal(r))[None, :]
            return q
        key = jax.random.key(seed)
        kx, kf = jax.random.split(key)
        x = jax.random.normal(kx, (B, T, DIM), dtype=jnp.float32)
        fkeys = jax.random.split(kf, RANK)
        factors = jnp.stack([_orthogonal(fkeys[r], DIM) * (r + 1) ** (-0.5) for r in range(RANK)])
        bias = jnp.zeros((DIM,), dtype=jnp.float32)
        return {'x': x, 'factors': factors, 'bias': bias}
    _L0_ffn_all = _L0_ffn_setup()
    _L0_ffn_in = {k: v for k, v in _L0_ffn_all.items() if k in ('factors', 'bias')}
    del _L0_ffn_all

    def _L1_xattn_setup():
        import jax, jax.numpy as jnp
        import numpy as np
        EPS = 1e-05

        def rmsnorm(x, g, eps=EPS):
            var = jnp.mean(jnp.square(x), axis=-1, keepdims=True)
            return x * jax.lax.rsqrt(var + eps) * g
        key = jax.random.key(seed)
        ks = jax.random.split(key, 8)
        B, Sq, Skv = (2, 512, 64)
        dim, cdim, H, D = (256, 128, 16, 128)
        inner = H * D
        s = lambda f: 1.0 / np.sqrt(f)
        return {'hidden_states': jax.random.normal(ks[0], (B, Sq, dim), jnp.float32), 'encoder_hidden_states': jax.random.normal(ks[1], (B, Skv, cdim), jnp.float32), 'Wq': jax.random.normal(ks[2], (dim, inner), jnp.float32) * s(dim), 'Wk': jax.random.normal(ks[3], (cdim, inner), jnp.float32) * s(cdim), 'Wv': jax.random.normal(ks[4], (cdim, inner), jnp.float32) * s(cdim), 'Wo': jax.random.normal(ks[5], (inner, dim), jnp.float32) * s(inner), 'gq': jnp.ones((D,), jnp.float32), 'gk': jnp.ones((D,), jnp.float32)}
    _L1_xattn_all = _L1_xattn_setup()
    _L1_xattn_in = {k: v for k, v in _L1_xattn_all.items() if k in ('Wq', 'Wk', 'Wv', 'Wo', 'gq', 'gk')}
    del _L1_xattn_all

    def _L1_ffn_setup():
        import jax, jax.numpy as jnp
        import numpy as np
        TOP_K = 4
        key = jax.random.key(seed)
        ks = jax.random.split(key, 8)
        B, S, D, E, H, HS = (2, 256, 256, 16, 128, 512)
        scaled = lambda k, shape, fan: jax.random.normal(k, shape, jnp.float32) * fan ** (-0.5)
        return {'x': jax.random.normal(ks[0], (B, S, D), jnp.float32), 'w_router': scaled(ks[1], (D, E), D), 'we1': scaled(ks[2], (E, D, H), D), 'we3': scaled(ks[3], (E, D, H), D), 'we2': scaled(ks[4], (E, H, D), H), 'ws1': scaled(ks[5], (D, HS), D), 'ws3': scaled(ks[6], (D, HS), D), 'ws2': scaled(ks[7], (HS, D), HS)}
    _L1_ffn_all = _L1_ffn_setup()
    _L1_ffn_in = {k: v for k, v in _L1_ffn_all.items() if k in ('w_router', 'we1', 'we3', 'we2', 'ws1', 'ws3', 'ws2')}
    del _L1_ffn_all
    return {'x': x, 'ctx_1024': ctx_1024, 'mask_BxS2_bf1': mask_BxS2_bf1, 'L0_xattn_Wq': _L0_xattn_in['Wq'], 'L0_xattn_Wk': _L0_xattn_in['Wk'], 'L0_xattn_Wv': _L0_xattn_in['Wv'], 'L0_xattn_Wo': _L0_xattn_in['Wo'], 'L0_ffn_factors': _L0_ffn_in['factors'], 'L0_ffn_bias': _L0_ffn_in['bias'], 'L1_xattn_Wq': _L1_xattn_in['Wq'], 'L1_xattn_Wk': _L1_xattn_in['Wk'], 'L1_xattn_Wv': _L1_xattn_in['Wv'], 'L1_xattn_Wo': _L1_xattn_in['Wo'], 'L1_xattn_gq': _L1_xattn_in['gq'], 'L1_xattn_gk': _L1_xattn_in['gk'], 'L1_ffn_w_router': _L1_ffn_in['w_router'], 'L1_ffn_we1': _L1_ffn_in['we1'], 'L1_ffn_we3': _L1_ffn_in['we3'], 'L1_ffn_we2': _L1_ffn_in['we2'], 'L1_ffn_ws1': _L1_ffn_in['ws1'], 'L1_ffn_ws3': _L1_ffn_in['ws3'], 'L1_ffn_ws2': _L1_ffn_in['ws2']}

def reference(x, ctx_1024, mask_BxS2_bf1, L0_xattn_Wq, L0_xattn_Wk, L0_xattn_Wv, L0_xattn_Wo, L0_ffn_factors, L0_ffn_bias, L1_xattn_Wq, L1_xattn_Wk, L1_xattn_Wv, L1_xattn_Wo, L1_xattn_gq, L1_xattn_gk, L1_ffn_w_router, L1_ffn_we1, L1_ffn_we3, L1_ffn_we2, L1_ffn_ws1, L1_ffn_ws3, L1_ffn_ws2):
    import jax
    import jax.numpy as jnp

    def _L0_xattn_ref(text_hidden, vision_tokens, vision_mask, Wq, Wk, Wv, Wo):
        import jax, jax.numpy as jnp
        import numpy as np
        N_HEADS = 16
        N_KV_HEADS = 8
        HEAD_DIM = 128
        D_TEXT = 256
        D_VISION = 128
        GROUPS = N_HEADS // N_KV_HEADS
        B, T_text, _ = text_hidden.shape
        T_vis = vision_tokens.shape[1]
        scale = jnp.float32(np.sqrt(HEAD_DIM))
        q = (text_hidden @ Wq).reshape(B, T_text, N_HEADS, HEAD_DIM).transpose(0, 2, 1, 3)
        k = (vision_tokens @ Wk).reshape(B, T_vis, N_KV_HEADS, HEAD_DIM).transpose(0, 2, 1, 3)
        v = (vision_tokens @ Wv).reshape(B, T_vis, N_KV_HEADS, HEAD_DIM).transpose(0, 2, 1, 3)
        k = jnp.repeat(k, GROUPS, axis=1)
        v = jnp.repeat(v, GROUPS, axis=1)
        scores = jnp.einsum('bhtd,bhsd->bhts', q, k) / scale
        mask = vision_mask[:, None, None, :]
        scores = jnp.where(mask, scores, -jnp.inf)
        attn = jax.nn.softmax(scores, axis=-1)
        attn = jnp.nan_to_num(attn, nan=0.0)
        out = jnp.einsum('bhts,bhsd->bhtd', attn, v)
        out = out.transpose(0, 2, 1, 3).reshape(B, T_text, N_HEADS * HEAD_DIM)
        return out @ Wo

    def _L0_ffn_ref(x, factors, bias):
        import math
        import jax, jax.numpy as jnp
        import numpy as np
        DIM = 256
        RANK = 8
        B, T = (4, 512)

        def _orthogonal(key, n):
            a = jax.random.normal(key, (n, n), dtype=jnp.float32)
            q, r = jnp.linalg.qr(a)
            q = q * jnp.sign(jnp.diagonal(r))[None, :]
            return q
        rank = factors.shape[0]
        mixed = jnp.einsum('btd,rde->bte', x, factors)
        mixed = mixed / math.sqrt(rank) + bias
        return mixed

    def _L1_xattn_ref(hidden_states, encoder_hidden_states, Wq, Wk, Wv, Wo, gq, gk):
        import jax, jax.numpy as jnp
        import numpy as np
        EPS = 1e-05

        def rmsnorm(x, g, eps=EPS):
            var = jnp.mean(jnp.square(x), axis=-1, keepdims=True)
            return x * jax.lax.rsqrt(var + eps) * g
        B, Sq, _ = hidden_states.shape
        Skv = encoder_hidden_states.shape[1]
        D = gq.shape[0]
        H = Wq.shape[1] // D
        scale = 1.0 / np.sqrt(D)
        q = (hidden_states @ Wq).reshape(B, Sq, H, D)
        k = (encoder_hidden_states @ Wk).reshape(B, Skv, H, D)
        v = (encoder_hidden_states @ Wv).reshape(B, Skv, H, D)
        q = rmsnorm(q, gq)
        k = rmsnorm(k, gk)
        scores = jnp.einsum('bqhd,bkhd->bhqk', q, k) * scale
        attn = jax.nn.softmax(scores, axis=-1)
        out = jnp.einsum('bhqk,bkhd->bqhd', attn, v)
        out = out.reshape(B, Sq, H * D)
        return out @ Wo

    def _L1_ffn_ref(x, w_router, we1, we3, we2, ws1, ws3, ws2):
        import jax, jax.numpy as jnp
        import numpy as np
        TOP_K = 4
        B, S, D = x.shape
        T = B * S
        E = w_router.shape[1]
        xt = x.reshape(T, D)
        probs = jax.nn.softmax(xt @ w_router, axis=-1)
        top_w, top_i = jax.lax.top_k(probs, TOP_K)
        top_w = top_w / jnp.sum(top_w, axis=-1, keepdims=True)
        cw = jnp.zeros((T, E), xt.dtype).at[jnp.arange(T)[:, None], top_i].add(top_w)
        g = jax.nn.silu(jnp.einsum('td,edh->teh', xt, we1)) * jnp.einsum('td,edh->teh', xt, we3)
        g = g * cw[:, :, None]
        moe_out = jnp.einsum('teh,ehd->td', g, we2)
        shared = jax.nn.silu(xt @ ws1) * (xt @ ws3) @ ws2
        k = TOP_K
        out = shared / (k + 1) + moe_out * (k / (k + 1))
        return out.reshape(B, S, D)
    x = x + _L0_xattn_ref(_layernorm(x, axis=-1), ctx_1024, mask_BxS2_bf1, L0_xattn_Wq, L0_xattn_Wk, L0_xattn_Wv, L0_xattn_Wo)
    x = x + _L0_ffn_ref(_layernorm(x, axis=-1), L0_ffn_factors, L0_ffn_bias)
    x = x + _L1_xattn_ref(_layernorm(x, axis=-1), ctx_1024, L1_xattn_Wq, L1_xattn_Wk, L1_xattn_Wv, L1_xattn_Wo, L1_xattn_gq, L1_xattn_gk)
    x = x + _L1_ffn_ref(_layernorm(x, axis=-1), L1_ffn_w_router, L1_ffn_we1, L1_ffn_we3, L1_ffn_we2, L1_ffn_ws1, L1_ffn_ws3, L1_ffn_ws2)
    return x

_drawn_inputs = setup_inputs


def setup_inputs(seed=0):
    import zlib

    import numpy as np

    out = dict(_drawn_inputs(seed))
    spreads = {'L0_ffn_bias': (0.0, 0.1), 'L1_xattn_gq': (1.0, 0.2), 'L1_xattn_gk': (1.0, 0.2)}
    factors = {'L0_xattn_Wq': 8.0, 'L0_xattn_Wk': 8.0}
    for name, (base, spread) in spreads.items():
        noise = np.random.default_rng([zlib.crc32(name.encode()), seed]).standard_normal(out[name].shape)
        drawn = base * np.exp(spread * noise) if base else spread * noise
        out[name] = jnp.asarray(drawn.astype(out[name].dtype))
    for name, factor in factors.items():
        out[name] = (out[name] * factor).astype(out[name].dtype)
    return out
```

```python
from collections import namedtuple
from contextlib import ExitStack

import concourse.bass as bass
from concourse import mybir

F32 = mybir.dt.float32
F32R = mybir.dt.float32r
U8 = mybir.dt.uint8
ALU = mybir.AluOpType
ACT = mybir.ActivationFunctionType
AX = mybir.AxisListType

B, QS, D = 16, 56, 256
S, C = 1500, 128
H, HD, G0 = 16, 128, 8
KT, NT = 125, 12
QW, HALF = H * QS, H * QS // 2
TT, NTT = 112, 8
KC = D // 128
RANK, E, HS = 8, 16, 512
NEXP = E + HS // 128
TOPK = 4
LN_EPS = 1e-5
RMS_EPS = 1e-5
MASKED = 30000.0
SCALE = float(HD) ** -0.5
MC, NMC = 500, 3
QBLK = 8
NG = 4
DVE_G = 3

STEPS = ["MMMMMA"] * 3 + ["MMMNNA"] * 3 + ["NNNNNA"] * 2 + ["TNNNNNA"] + ["NNNNNA"] * 3
SIDE = "".join(STEPS)
NSIDE = len(SIDE)
STEP_AT = [sum(len(x) for x in STEPS[:t]) for t in range(NT + 1)]
SIDE_V = sum(x != "A" for x in SIDE)
SIDE_A = SIDE.count("A")
assert (SIDE.count("M"), SIDE.count("N"), SIDE_A) == (QBLK * NMC, NT * DVE_G, NT) and NSIDE % 2 == 1


def need(eng, sem, value):
    if isinstance(value, int) and value <= 0:
        return
    eng.wait_ge(sem, value)


def side_number(k):
    return SIDE[:k].count(SIDE[k])


def side_done(s, batch, k):
    if SIDE[k] == "A":
        return s.side_act, SIDE_A * batch + SIDE[:k + 1].count("A")
    return s.side_dve, SIDE_V * batch + sum(x != "A" for x in SIDE[:k + 1])


def layer_norm_vector(dve, m, s):
    for j in range(NTT):
        dve.bn_stats(m.stats[:, j, :], m.x[:, j, :]).then_inc(s.ln_stats, 1)
    dve.wait_ge(s.ln_stats, NTT)
    for j in range(NTT):
        dve.bn_aggr(m.meanvar[:, j, :], m.stats[:, j, :]).then_inc(s.ln_aggr, 1)
    dve.wait_ge(s.ln_aggr, NTT)
    dve.tensor_scalar(m.vareps[:, :], m.meanvar[:, :, 1], LN_EPS, None, ALU.add).then_inc(s.ln_var, 1)
    dve.wait_ge(s.ln_std, 1)
    dve.reciprocal(m.rstd[:, :], m.std[:, :]).then_inc(s.ln_rstd, 1)
    dve.wait_ge(s.ln_rstd, 1)
    for j in range(NTT):
        dve.tensor_scalar(m.xn[:, j, :], m.x[:, j, :], m.meanvar[:, j, 0:1], m.rstd[:, j:j + 1],
                          ALU.subtract, ALU.mult).then_inc(s.xn, 1)


def layer_norm_scalar(act, m, s):
    act.wait_ge(s.ln_var, 1)
    act.activation(m.std[:, :], m.vareps[:, :], ACT.Sqrt).then_inc(s.ln_std, 1)


LN_SEMAPHORES = ["ln_stats", "ln_aggr", "ln_var", "ln_std", "ln_rstd", "xn"]


def semaphores(sem, tag, names):
    return namedtuple("Semaphores", names)(*[sem(f"{tag}_{n}") for n in names])


class Buffers:
    pass


class Banks:

    def __init__(self, jobs, sems, count=8):
        self.jobs, self.sems, self.count = jobs, sems, count

    def number(self, n):
        return sum(j[0] == self.jobs[n][0] for j in self.jobs[:n + 1])

    def wait_free(self, pe, n):
        if n >= self.count:
            pe.wait_ge(self.sems[self.jobs[n - self.count][0]], self.number(n - self.count))


def before_attention(nc, m, a, tag, sem):
    s = semaphores(sem, tag, LN_SEMAPHORES + ["ld_x", "ld_mask", "ld_const", "ld_w0", "ld_w1", "const", "ready", "on_act", "on_dve", "xnT",
                 "fold", "w_hi", "g_hi", "mcount"])
    jobs = [("act", "fold", i) for i in range(8)]
    jobs += [("dve", "gram", g) for g in range(DVE_G)]
    jobs += [("dve", "valid", 0)]
    jobs += [("act", "turn", i) for i in range(4)]
    jobs += [(("act", "dve")[i % 2], "query", i) for i in range(2 * H)]
    banks = Banks(jobs, {"act": s.on_act, "dve": s.on_dve})
    with ExitStack() as ctx:
        sb = lambda n, sh, dt: ctx.enter_context(nc.sbuf_tensor(f"{tag}_{n}", sh, dt))
        bk = [ctx.enter_context(nc.psum_tensor(f"{tag}_bk{i}", [128, 512], F32)) for i in range(8)]
        wqT = sb("wqT", [HD, H, D], F32)
        wkT0 = sb("wkT0", [HD, G0, C], F32)
        wkT1 = sb("wkT1", [HD, H, C], F32)
        wk1 = sb("wk1", [C, 512], F32)
        fold = sb("fold", [128, H, KC, C], F32)
        msum = sb("msum", [KT, B], F32)
        masku = sb("masku", [KT, B, NT], U8)
        maskf = sb("maskf", [KT, B, NT], F32)
        block = ctx.enter_context(nc.Block())

        @block.sync
        def _(sp):
            sp.dma_start(wqT[:, :, :], a.wqT0).then_inc(s.ld_w0, 16)
            sp.dma_start(wkT0[:, :, :], a.wkT0).then_inc(s.ld_w0, 16)
            sp.dma_start(m.x[:, :, :], a.x).then_inc(s.ld_x, 16)
            sp.dma_start(wkT1[:, :, :], a.wkT1).then_inc(s.ld_w1, 16)
            sp.dma_start(wk1[:, :], a.wk1).then_inc(s.ld_w1, 16)
            sp.dma_start(masku[:, :, :], a.mask_cols).then_inc(s.ld_mask, 16)
            sp.dma_start(m.ident[:, :], a.ident).then_inc(s.ld_const, 16)
            sp.dma_start(m.diag[:, :], a.diag).then_inc(s.ld_const, 16)

        @block.scalar
        def _(act):
            layer_norm_scalar(act, m, s)
            act.wait_ge(s.ld_w1, 32)
            act.activation(m.norm_hi[:, DVE_G * 512:], wk1[:, :], ACT.Copy).then_inc(s.w_hi, 1)
            for n, (who, kind, i) in enumerate(jobs):
                bank = bk[n % 8]
                if kind == "fold":
                    act.wait_ge(s.ready, n + 1)
                    act.activation(fold[:, 2 * i:2 * i + 2, :, :], bank[:, :], ACT.Copy, scale=SCALE).then_inc(s.on_act, 1)
                elif kind == "gram":
                    act.wait_ge(s.ready, n + 1)
                    act.activation(m.norm_hi[:, 512 * i:512 * i + 512], bank[:, :], ACT.Copy).then_inc(s.g_hi, 1)
                elif kind == "turn":
                    act.wait_ge(s.ready, n + 1)
                    act.activation(m.xnT[:, i // 2, HALF * (i % 2):HALF * (i % 2) + HALF], bank[:, 0:HALF],
                                   ACT.Copy).then_inc(s.on_act, 1)
                elif who == "act":
                    act.wait_ge(s.ready, n + 1)
                    h, half = i // 2, i % 2
                    act.activation(m.qs[:, 8 * half:8 * half + 8, h, :],
                                   bank[:, 0:HALF].rearrange("p (b q) -> p b q", q=QS), ACT.Copy).then_inc(s.on_act, 1)

        @block.vector
        def _(dve):
            dve.memset(m.ones[:, :], 1.0).then_inc(s.const, 1)
            dve.memset(m.ones8[:, :].bitcast(F32), 1.0).then_inc(s.const, 1)
            dve.memset(m.eps[:, :], RMS_EPS).then_inc(s.const, 1)
            dve.wait_ge(s.ld_x, 16)
            layer_norm_vector(dve, m, s)
            dve.wait_ge(s.ld_mask, 16)
            dve.tensor_scalar(m.mask_bias[:, :, :], masku[:, :, :], MASKED, -MASKED, ALU.mult, ALU.add).then_inc(s.const, 1)
            dve.tensor_copy(maskf[:, :, :], masku[:, :, :]).then_inc(s.mcount, 1)
            dve.wait_ge(s.mcount, 1)
            dve.tensor_reduce(msum[:, :], maskf[:, :, :], AX.X, ALU.add).then_inc(s.mcount, 1)
            dve.wait_ge(s.w_hi, 1)
            dve.tensor_tensor(m.norm_lo[:, DVE_G * 512:], wk1[:, :], m.norm_hi[:, DVE_G * 512:].bitcast(F32),
                              ALU.subtract).then_inc(s.const, 1)
            for n, (who, kind, i) in enumerate(jobs):
                bank = bk[n % 8]
                if who != "dve":
                    continue
                dve.wait_ge(s.ready, n + 1)
                if kind == "gram":
                    dve.wait_ge(s.g_hi, i + 1)
                    cols = slice(512 * i, 512 * i + 512)
                    dve.tensor_tensor(m.norm_lo[:, cols], bank[:, :], m.norm_hi[:, cols].bitcast(F32),
                                      ALU.subtract).then_inc(s.on_dve, 1)
                elif kind == "valid":
                    dve.tensor_scalar(m.valid[:, :], bank[:, 0:B], 1.0, None, ALU.min).then_inc(s.on_dve, 1)
                else:
                    h, half = i // 2, i % 2
                    dve.tensor_copy(m.qs[:, 8 * half:8 * half + 8, h, :],
                                    bank[:, 0:HALF].rearrange("p (b q) -> p b q", q=QS)).then_inc(s.on_dve, 1)

        @block.tensor
        def _(pe):
            for n, (who, kind, i) in enumerate(jobs):
                bank = bk[n % 8]
                banks.wait_free(pe, n)
                if kind == "fold":
                    if i == 0:
                        pe.wait_ge(s.ld_w0, 32)
                    for c in range(4):
                        h, kc = 2 * i + c // 2, c % 2
                        last = pe.matmul(bank[:, 128 * c:128 * c + 128], wqT[:, h, 128 * kc:128 * kc + 128],
                                         wkT0[:, h // 2, :], start=True, stop=True)
                elif kind == "gram":
                    if i == 0:
                        pe.wait_ge(s.ld_w1, 32)
                    for c in range(4):
                        h = 4 * i + c
                        last = pe.matmul(bank[:, 128 * c:128 * c + 128], wkT1[:, h, :], wkT1[:, h, :],
                                         start=True, stop=True)
                elif kind == "valid":
                    pe.wait_ge(s.mcount, 2)
                    pe.wait_ge(s.const, 1)
                    last = pe.matmul(bank[:, 0:B], m.ones[0:KT, :], msum[:, :], start=True, stop=True)
                elif kind == "turn":
                    if i == 0:
                        pe.wait_ge(s.ld_const, 32)
                        pe.wait_ge(s.xn, NTT)
                    for c in range(4):
                        j = 4 * (i % 2) + c
                        last = pe.transpose(bank[:, TT * c:TT * c + TT], m.xn[:, j, 128 * (i // 2):128 * (i // 2) + 128],
                                            m.ident[0:TT, 0:TT])
                else:
                    if i == 0:
                        pe.wait_ge(s.on_act, 12)
                    h, half = i // 2, i % 2
                    for kc in range(KC):
                        last = pe.matmul(bank[:, 0:HALF], fold[:, h, kc, :], m.xnT[:, kc, HALF * half:HALF * half + HALF],
                                         start=kc == 0, stop=kc == KC - 1)
                last.then_inc(s.ready, 1)


def attention(nc, m, a, tag, sem, first):
    names = ["ld_land", "ld_nat0", "ld_nat1", "ld_mask", "ctx_hi", "ctx_lo", "q_hi", "q_lo", "nat_hi", "xq", "mask_row",
             "scores", "scaled", "probs", "pv", "acc", "den", "inv", "o_raw", "o_done", "side_pe", "side_dve",
             "side_act", "negmax", "shift", "rk_pre", "dve_passed", "pool_passed"]
    s = semaphores(sem, tag, names)
    ld_nat = [s.ld_nat0, s.ld_nat1]
    consumed = s.probs if first else s.scaled
    with ExitStack() as ctx:
        sb = lambda n, sh, dt: ctx.enter_context(nc.sbuf_tensor(f"{tag}_{n}", sh, dt))
        psum = lambda n, sh: ctx.enter_context(nc.psum_tensor(f"{tag}_{n}", sh, F32))
        land = sb("land", [C, S], F32)
        chi = [sb(f"chi{i}", [C, S], F32R) for i in range(2)]
        clo = [sb(f"clo{i}", [C, S], F32R) for i in range(2)]
        nat = [sb(f"nat{i}", [KT, NT, C], F32) for i in range(2)]
        qhi = [sb(f"qhi{i}", [C, QW], F32R) for i in range(2)]
        qlo = [sb(f"qlo{i}", [C, QW], F32R) for i in range(2)]
        P = [sb(f"probs{i}", [KT, QW], F32) for i in range(3)]
        acc = [sb(f"acc{i}", [KT, QW], F32) for i in range(2)]
        inv = sb("inv", [128, QW], F32)
        if first:
            nathi = sb("nathi", [KT, NT, C], F32R)
            xq = sb("xq", [KT, NT, C], F32)
            masku = sb("masku", [TT, S], U8)
            mrow = sb("mrow", [TT, S], F32)
            mx = sb("mx", [TT, QBLK, NMC], F32)
            negmax = sb("negmax", [TT, QBLK], F32)
            shift = [sb(f"shift{i}", [QBLK, QW], F32R) for i in range(2)]
            msq = sb("msq", [KT, NT, 12], F32)
            msqa = sb("msqa", [KT, NT, 4], F32)
            side = [psum(f"side{i}", [128, 512]) for i in range(2)]
        else:
            scaled = [sb(f"scaled{i}", [KT, QW], F32) for i in range(2)]
        slots = psum("slots", [128, 2, 2, 512])
        psO = psum("psO", [128, 2, 512])
        block = ctx.enter_context(nc.Block())

        def slot_of(par, t):
            return par if t == 0 else (par + 1 + t) % 2

        def batches(eng, body):
            body(0, 0, True, True)
            body(1, 1, True, True)
            with eng.Fori(1, B // 2 - 1) as i:
                body(2 * i, 0, True, True)
                body(2 * i + 1, 1, True, True)
            body(B - 2, 0, True, False)
            body(B - 1, 1, False, False)

        @block.sync
        def _(sp):
            def load_land(b):
                need(sp, s.ctx_lo, b)
                sp.dma_start(land[:, :], a.ctxT[:, bass.ds(b, 1), :]).then_inc(s.ld_land, 16)

            def load_nat(b, par):
                need(sp, s.pv, NT * (b - 1))
                if first:
                    need(sp, s.xq, b - 1)
                sp.dma_start(nat[par][:, :, :], a.ctxN[bass.ds(b, 1), :, :, :]).then_inc(ld_nat[par], 16)

            def load_mask(b):
                need(sp, s.mask_row, b)
                sp.dma_start(masku[:, :], a.mask[bass.ds(b, 1), :].to_broadcast([TT, S])).then_inc(s.ld_mask, 16)

            def body(b, par, nxt, nxt2):
                if nxt:
                    load_nat(b + 1, 1 - par)
                if nxt2:
                    load_land(b + 2)
                    if first:
                        load_mask(b + 2)

            load_land(0)
            load_nat(0, 0)
            if first:
                load_mask(0)
            load_land(1)
            if first:
                load_mask(1)
            batches(sp, body)

        @block.scalar
        def _(act):
            def high_parts(b, par):
                act.wait_ge(s.ld_land, 16 * (b + 1))
                need(act, s.scores, NT * (b - 1))
                act.activation(chi[par][:, :], land[:, :], ACT.Copy).then_inc(s.ctx_hi, 1)
                act.activation(qhi[par][:, :], m.qs[:, bass.ds(b, 1), :, :].rearrange("p o h q -> p (o h q)"),
                               ACT.Copy).then_inc(s.q_hi, 1)

            def nat_high(b, par):
                act.wait_ge(ld_nat[par], 16 * (b // 2 + 1))
                need(act, s.xq, b)
                act.activation(nathi[:, :, :], nat[par][:, :, :], ACT.Copy).then_inc(s.nat_hi, 1)

            def norms(b, par, k):
                t = side_number(k)
                act.wait_ge(s.side_pe, NSIDE * b + k + 1)
                if t == 0:
                    need(act, s.rk_pre, 2 * b)
                bank = side[(k + par) % 2]
                for c in range(4):
                    sq = bank[0:KT, 128 * c:128 * c + 128]
                    last = act.activation(sq, sq, ACT.Square, accum_out=msqa[:, t, c:c + 1])
                last.then_inc(s.side_act, 1)

            def exp(b, par, t):
                if first:
                    act.wait_ge(s.scores, NT * b + t + 1)
                    src = slots[0:KT, slot_of(par, t), :, 0:HALF]
                else:
                    act.wait_ge(s.scaled, NT * b + t + 1)
                    src = scaled[t % 2][:, :].rearrange("p (a c) -> p a c", a=2)
                need(act, s.pv, NT * b + t - 2)
                need(act, s.acc, (NT - 1) * b + (max(1, t - 3) if t >= 3 else t - 2))
                dst = P[t % 3][:, :].rearrange("p (a c) -> p a c", a=2)
                if first:
                    bias = m.mask_bias[:, bass.ds(b, 1), t].rearrange("p o -> p o")
                    act.activation(dst, src, ACT.Exp, bias=bias).then_inc(s.probs, 1)
                else:
                    act.activation(dst, src, ACT.Exp).then_inc(s.probs, 1)

            def values_out(b):
                act.wait_ge(s.pv, NT * b + NT)
                dst = m.qs[:, bass.ds(b, 1), :, :].rearrange("p o (a h) q -> p (o a) (h q)", a=2)
                if first:
                    act.activation(dst, psO[:, :, 0:HALF], ACT.Copy, scale=m.valid[:, bass.ds(b, 1)]).then_inc(s.o_raw, 1)
                else:
                    act.activation(dst, psO[:, :, 0:HALF], ACT.Copy).then_inc(s.o_raw, 1)

            def body(b, par, nxt, nxt2):
                for t in range(NT):
                    if t < NT - 1:
                        exp(b, par, t + 1)
                    else:
                        if nxt2:
                            high_parts(b + 2, par)
                        if nxt:
                            exp(b + 1, 1 - par, 0)
                    if first and nxt:
                        if t == 1:
                            nat_high(b + 1, 1 - par)
                        for k in range(STEP_AT[t], STEP_AT[t + 1]):
                            if SIDE[k] == "A":
                                norms(b + 1, 1 - par, k)
                values_out(b)

            high_parts(0, 0)
            if first:
                nat_high(0, 0)
            act.wait_ge(s.ctx_lo, 1)
            high_parts(1, 1)
            if first:
                for k in range(NSIDE):
                    if SIDE[k] == "A":
                        norms(0, 0, k)
            exp(0, 0, 0)
            batches(act, body)

        @block.gpsimd
        def _(pool):
            def low_parts(b, par):
                pool.wait_ge(s.ctx_hi, b + 1)
                pool.tensor_tensor(clo[par][:, :], land[:, :], chi[par][:, :].bitcast(F32), ALU.subtract).then_inc(s.ctx_lo, 1)
                pool.wait_ge(s.q_hi, b + 1)
                pool.tensor_tensor(qlo[par][:, :], m.qs[:, bass.ds(b, 1), :, :].rearrange("p o h q -> p (o h q)"),
                                   qhi[par][:, :].bitcast(F32), ALU.subtract).then_inc(s.q_lo, 1)

            def mask_row(b):
                pool.wait_ge(s.ld_mask, 16 * (b + 1))
                if not (isinstance(b, int) and b == 0):
                    q, v = side_done(s, b - 1, SIDE.rindex("M"))
                    pool.wait_ge(q, v)
                pool.sem_inc(s.pool_passed, 1)
                pool.tensor_scalar(mrow[:, :], masku[:, :], MASKED, -MASKED, ALU.mult, ALU.add).then_inc(s.mask_row, 1)

            def add(b, par, t):
                pool.wait_ge(s.probs, NT * b + t + 1)
                if t == 1:
                    need(pool, s.den, b - 1)
                    pool.tensor_tensor(acc[par][:, :], P[0][:, :], P[1][:, :], ALU.add).then_inc(s.acc, 1)
                else:
                    pool.wait_ge(s.acc, (NT - 1) * b + t - 1)
                    pool.tensor_tensor(acc[par][:, :], acc[par][:, :], P[t % 3][:, :], ALU.add).then_inc(s.acc, 1)

            def body(b, par, nxt, nxt2):
                for t in range(1, NT):
                    add(b, par, t)
                    if t == 8 and first and nxt2:
                        mask_row(b + 2)
                if nxt2:
                    low_parts(b + 2, par)

            low_parts(0, 0)
            if first:
                mask_row(0)
            low_parts(1, 1)
            if first:
                mask_row(1)
            batches(pool, body)

        @block.vector
        def _(dve):
            def max_chunk(b, par, k):
                i = side_number(k)
                j, c = i // NMC, i % NMC
                dve.wait_ge(s.side_pe, NSIDE * b + k + 1)
                if i == 0:
                    dve.wait_ge(s.mask_row, b + 1)
                    need(dve, s.negmax, b)
                bank = side[(k + par) % 2][0:TT, 0:MC]
                dve.sem_inc(s.dve_passed, 1)
                dve.tensor_tensor_reduce(bank, bank, mrow[:, MC * c:MC * c + MC], 1.0, -3.0e38, ALU.add, ALU.max,
                                         mx[:, j, c:c + 1]).then_inc(s.side_dve, 1)
                if i == QBLK * NMC - 1:
                    q, v = side_done(s, b, k)
                    dve.wait_ge(q, v)
                    dve.tensor_reduce(negmax[:, :], mx[:, :, :], AX.X, ALU.max, negate=True).then_inc(s.negmax, 1)

            def spread_shift(b, par, k):
                dve.wait_ge(s.side_pe, NSIDE * b + k + 1)
                need(dve, s.scores, NT * (b - 1))
                src = side[(k + par) % 2][0:QBLK, 0:TT].unsqueeze(1).to_broadcast([QBLK, QBLK, TT])
                dve.tensor_tensor(shift[par][:, :].rearrange("p (j c) -> p j c", c=TT), src,
                                  m.diag[:, :].rearrange("p (j c) -> p j c", c=TT), ALU.mult).then_inc(s.side_dve, 1)

            def norms(b, par, k):
                i = side_number(k)
                t, g = i // DVE_G, i % DVE_G
                if i == 0:
                    dve.wait_ge(s.nat_hi, b + 1)
                    need(dve, s.side_dve, SIDE_V * b)
                    dve.scalar_tensor_tensor(xq[:, :, :], nat[par][:, :, :], 2.0, nathi[:, :, :].bitcast(F32),
                                             ALU.mult, ALU.subtract).then_inc(s.xq, 1)
                    dve.wait_ge(s.xq, b + 1)
                    need(dve, s.rk_pre, 2 * b)
                dve.wait_ge(s.side_pe, NSIDE * b + k + 1)
                bank = side[(k + par) % 2]
                for c in range(4):
                    u = bank[0:KT, 128 * c:128 * c + 128]
                    last = dve.tensor_tensor_reduce(u, u, xq[:, t, :], 1.0, 0.0, ALU.mult, ALU.add,
                                                    msq[:, t, 4 * g + c:4 * g + c + 1])
                last.then_inc(s.side_dve, 1)

            def side_job(b, par, k):
                {"M": max_chunk, "N": norms, "T": spread_shift}[SIDE[k]](b, par, k)

            def norms_out(b):
                dve.wait_ge(s.side_dve, SIDE_V * (b + 1))
                dve.wait_ge(s.side_act, SIDE_A * (b + 1))
                dst = m.rk[:, bass.ds(b, 1), :, :].rearrange("p o t h -> p (o t) h")
                dve.tensor_scalar(dst[:, :, 0:12], msq[:, :, :], 1.0 / HD, RMS_EPS, ALU.mult, ALU.add).then_inc(s.rk_pre, 1)
                dve.tensor_scalar(dst[:, :, 12:16], msqa[:, :, :], 1.0 / HD, RMS_EPS, ALU.mult, ALU.add).then_inc(s.rk_pre, 1)

            def scale_scores(b, par, t):
                dve.wait_ge(s.scores, NT * b + t + 1)
                need(dve, s.probs, NT * b + t - 1)
                src = slots[0:KT, slot_of(par, t), :, 0:HALF].rearrange("p a (h q) -> p a h q", q=QS)
                rk = m.rk[:, bass.ds(b, 1), t, :].rearrange("p o (a h) -> p (o a) h", a=2).unsqueeze(3)
                dve.tensor_tensor(scaled[t % 2][:, :].rearrange("p (a h q) -> p a h q", a=2, q=QS), src,
                                  rk.to_broadcast([KT, 2, H // 2, QS]), ALU.mult).then_inc(s.scaled, 1)

            def normalise(b, par):
                dve.wait_ge(s.den, b + 1)
                need(dve, s.o_done, b)
                dve.reciprocal(inv[:, :].rearrange("p (a c) -> p a c", a=2), slots[:, par, :, 0:HALF]).then_inc(s.inv, 1)
                dve.wait_ge(s.inv, b + 1)
                dve.wait_ge(s.o_raw, b + 1)
                o = m.qs[:, bass.ds(b, 1), :, :].rearrange("p o h q -> p (o h q)")
                dve.tensor_tensor(o, o, inv[:, :], ALU.mult).then_inc(s.o_done, 1)

            def body(b, par, nxt, nxt2):
                for t in range(NT):
                    if not first:
                        if t < NT - 1:
                            scale_scores(b, par, t + 1)
                        elif nxt:
                            scale_scores(b + 1, 1 - par, 0)
                    elif nxt:
                        for k in range(STEP_AT[t], STEP_AT[t + 1]):
                            if SIDE[k] != "A":
                                side_job(b + 1, 1 - par, k)
                if first and nxt:
                    norms_out(b + 1)
                normalise(b, par)

            if first:
                for k in range(NSIDE):
                    if SIDE[k] != "A":
                        side_job(0, 0, k)
                norms_out(0)
            else:
                scale_scores(0, 0, 0)
            batches(dve, body)

        @block.tensor
        def _(pe):
            def scores(b, par, t):
                slot = slot_of(par, t)
                if t == 0:
                    pe.wait_ge(s.ctx_lo, b + 1)
                    pe.wait_ge(s.q_lo, b + 1)
                    if first:
                        pe.wait_ge(*side_done(s, b, SIDE.index("T")))
                    need(pe, consumed, NT * b - 1)
                elif t == 1:
                    pe.wait_ge(consumed, NT * b + 1)
                elif t == 2:
                    need(pe, s.inv, b)
                else:
                    pe.wait_ge(consumed, NT * b + t - 1)
                keys = slice(KT * t, KT * t + KT)
                for a_ in range(2):
                    cols = slice(HALF * a_, HALF * a_ + HALF)
                    out = slots[0:KT, slot, a_, 0:HALF]
                    pe.matmul(out, clo[par][:, keys], qhi[par][:, cols], start=True, stop=False)
                    pe.matmul(out, chi[par][:, keys], qlo[par][:, cols], start=False, stop=False)
                    last = pe.matmul(out, chi[par][:, keys], qhi[par][:, cols], start=False, stop=not first)
                    if first:
                        last = pe.matmul(out, m.ones8[:, :], shift[par][:, cols], start=False, stop=True)
                last.then_inc(s.scores, 1)

            def values(b, par, t):
                pe.wait_ge(s.probs, NT * b + t + 1)
                if t == 0:
                    pe.wait_ge(ld_nat[par], 16 * (b // 2 + 1))
                    need(pe, s.o_raw, b)
                for a_ in range(2):
                    last = pe.matmul(psO[:, a_, 0:HALF], nat[par][:, t, :], P[t % 3][:, HALF * a_:HALF * a_ + HALF],
                                     start=t == 0, stop=t == NT - 1)
                last.then_inc(s.pv, 1)

            def sums(b, par):
                pe.wait_ge(s.acc, (NT - 1) * (b + 1))
                pe.wait_ge(consumed, NT * b + NT)
                for a_ in range(2):
                    last = pe.matmul(slots[:, par, a_, 0:HALF], m.ones[0:KT, :], acc[par][:, HALF * a_:HALF * a_ + HALF],
                                     start=True, stop=True)
                last.then_inc(s.den, 1)

            def side_job(b, par, k):
                kind, i = SIDE[k], side_number(k)
                bank = side[(k + par) % 2]
                if k == 0:
                    pe.wait_ge(s.ctx_hi, b + 1)
                    pe.wait_ge(s.q_hi, b + 1)
                if k >= 2:
                    pe.wait_ge(*side_done(s, b, k - 2))
                elif not (isinstance(b, int) and b == 0):
                    pe.wait_ge(*side_done(s, b - 1, k - 2 + NSIDE))
                if kind == "M":
                    j, c = i // NMC, i % NMC
                    last = pe.matmul(bank[0:TT, 0:MC], qhi[par][:, TT * j:TT * j + TT], chi[par][:, MC * c:MC * c + MC],
                                     start=True, stop=True)
                elif kind == "T":
                    pe.wait_ge(s.negmax, b + 1)
                    last = pe.transpose(bank[0:QBLK, 0:TT], negmax[:, :], m.ident[0:TT, 0:TT])
                else:
                    t, g = (i // DVE_G, i % DVE_G) if kind == "N" else (i, DVE_G)
                    keys, cols = slice(KT * t, KT * t + KT), slice(512 * g, 512 * g + 512)
                    if kind == "A":
                        if t == 0:
                            pe.wait_ge(s.ctx_lo, b + 1)
                        pe.matmul(bank[0:KT, :], clo[par][:, keys], m.norm_hi[:, cols], start=True, stop=False)
                    pe.matmul(bank[0:KT, :], chi[par][:, keys], m.norm_lo[:, cols], start=kind == "N", stop=False)
                    last = pe.matmul(bank[0:KT, :], chi[par][:, keys], m.norm_hi[:, cols], start=False, stop=True)
                last.then_inc(s.side_pe, 1)

            def body(b, par, nxt, nxt2):
                for t in range(NT):
                    if t < NT - 1:
                        scores(b, par, t + 1)
                    elif nxt:
                        scores(b + 1, 1 - par, 0)
                    jobs = range(STEP_AT[t], STEP_AT[t + 1]) if first and nxt else range(0)
                    for k in jobs[:len(jobs) // 2]:
                        side_job(b + 1, 1 - par, k)
                    values(b, par, t)
                    for k in jobs[len(jobs) // 2:]:
                        side_job(b + 1, 1 - par, k)
                sums(b, par)

            if first:
                for k in range(NSIDE):
                    side_job(0, 0, k)
            scores(0, 0, 0)
            batches(pe, body)


def between_layers(nc, m, a, tag, sem):
    s1 = semaphores(sem, tag + "1", LN_SEMAPHORES)
    s2 = semaphores(sem, tag + "2", LN_SEMAPHORES)
    s = semaphores(sem, tag, ["ld_wv", "ld_wo", "ld_fac", "ld_bias", "ld_wq", "ld_wk", "ld_g", "ready", "on_act", "on_dve", "fac",
                 "gain", "rk_std", "rk_inv", "q", "sq", "ms", "std", "rinv", "qn", "qf", "q_out", "bias"])
    jobs = [("act", "vo", i) for i in range(8)]
    jobs += [("act", "outT", i) for i in range(4)]
    jobs += [("dve", "out", i) for i in range(4)]
    jobs += [("act", "turn", i) for i in range(4)]
    jobs += [("dve", "ffn", j) for j in range(NTT)]
    jobs += [("act", "turn2", i) for i in range(4)]
    banks = Banks(jobs, {"act": s.on_act, "dve": s.on_dve})
    with ExitStack() as ctx:
        sb = lambda n, sh, dt: ctx.enter_context(nc.sbuf_tensor(f"{tag}_{n}", sh, dt))
        bk = [ctx.enter_context(nc.psum_tensor(f"{tag}_bk{i}", [128, 512], F32)) for i in range(8)]
        wvT = sb("wvT", [HD, G0, C], F32)
        wo = sb("wo", [HD, H, D], F32)
        vo = sb("vo", [C, H, D], F32)
        yT = m.xnT
        fac = sb("fac", [128, KC, RANK, D], F32)
        fsum = sb("fsum", [128, KC, D], F32)
        bias = sb("bias", [TT, D], F32)
        wq = sb("wq", [128, KC, H * HD], F32)
        wkT = sb("wkT", [HD, H, C], F32)
        gains = sb("gains", [HD, 2], F32)
        gain = sb("gain", [HD, 1], F32)
        sq = [sb(f"sq{i}", [HD, HALF], F32) for i in range(2)]
        std = [sb(f"std{i}", [HD, HALF], F32) for i in range(2)]
        qn = [sb(f"qn{i}", [HD, HALF], F32) for i in range(2)]
        block = ctx.enter_context(nc.Block())
        NQ = 2 * H
        first_q = len(jobs)

        @block.sync
        def _(sp):
            sp.dma_start(wvT[:, :, :], a.wvT0).then_inc(s.ld_wv, 16)
            sp.dma_start(wo[:, :, :], a.wo0).then_inc(s.ld_wo, 16)
            sp.dma_start(fac[:, :, :, :], a.factors).then_inc(s.ld_fac, 16)
            sp.dma_start(bias[:, :], a.bias.to_broadcast([TT, D])).then_inc(s.ld_bias, 16)
            sp.dma_start(wq[:, :, :], a.wq1).then_inc(s.ld_wq, 16)
            sp.dma_start(wkT[:, :, :], a.wkT1).then_inc(s.ld_wk, 16)
            sp.dma_start(gains[:, :], a.gains).then_inc(s.ld_g, 16)

        @block.scalar
        def _(act):
            for n, (who, kind, i) in enumerate(jobs):
                if kind == "turn" and i == 0:
                    layer_norm_scalar(act, m, s1)
                    act.activation(m.rk[:, :, :, :], m.rk[:, :, :, :], ACT.Sqrt).then_inc(s.rk_std, 1)
                if kind == "turn2" and i == 0:
                    layer_norm_scalar(act, m, s2)
                if who != "act":
                    continue
                bank = bk[n % 8]
                act.wait_ge(s.ready, n + 1)
                if kind == "vo":
                    act.activation(vo[:, 2 * i:2 * i + 2, :], bank[:, :], ACT.Copy).then_inc(s.on_act, 1)
                elif kind == "outT":
                    act.activation(yT[:, i // 2, HALF * (i % 2):HALF * (i % 2) + HALF], bank[:, 0:HALF],
                                   ACT.Copy).then_inc(s.on_act, 1)
                else:
                    act.activation(m.xnT[:, i // 2, HALF * (i % 2):HALF * (i % 2) + HALF], bank[:, 0:HALF],
                                   ACT.Copy).then_inc(s.on_act, 1)
            for n in range(NQ + 3):
                if n < NQ:
                    act.wait_ge(s.q, n + 1)
                    need(act, s.ms, n - 1)
                    act.activation(sq[n % 2][:, :], bk[n % 4][:, 0:HALF], ACT.Square).then_inc(s.sq, 1)
                if 1 <= n <= NQ:
                    act.wait_ge(s.ms, n)
                    need(act, s.rinv, n - 2)
                    act.activation(std[(n - 1) % 2][:, :], bk[4 + (n - 1) % 2][:, 0:HALF], ACT.Sqrt, bias=m.eps[:, 0:1],
                                   scale=1.0 / HD).then_inc(s.std, 1)
                if n >= 3:
                    k = n - 3
                    act.wait_ge(s.qf, k + 1)
                    act.activation(m.qs[:, 8 * (k % 2):8 * (k % 2) + 8, k // 2, :],
                                   bk[6 + k % 2][:, 0:HALF].rearrange("p (b q) -> p b q", q=QS), ACT.Copy).then_inc(s.q_out, 1)

        @block.vector
        def _(dve):
            dve.wait_ge(s.ld_fac, 16)
            dve.tensor_reduce(fsum[:, :, :], fac[:, :, :, :].rearrange("p k r d -> p k d r"), AX.X, ALU.add).then_inc(s.fac, 1)
            dve.wait_ge(s.ld_g, 16)
            dve.tensor_scalar(gain[:, :], gains[:, 0:1], gains[:, 1:2], SCALE, ALU.mult, ALU.mult).then_inc(s.gain, 1)
            for n, (who, kind, i) in enumerate(jobs):
                bank = bk[n % 8]
                if kind == "turn" and i == 0:
                    dve.wait_ge(s.on_dve, 4)
                    layer_norm_vector(dve, m, s1)
                    dve.wait_ge(s.ld_bias, 16)
                    dve.wait_ge(s1.xn, NTT)
                    dve.tensor_tensor(m.x[:, :, :], m.x[:, :, :], bias[:, :].unsqueeze(1).to_broadcast([TT, NTT, D]),
                                      ALU.add).then_inc(s.bias, 1)
                    dve.wait_ge(s.rk_std, 1)
                    dve.reciprocal(m.rk[:, :, :, :], m.rk[:, :, :, :]).then_inc(s.rk_inv, 1)
                if kind == "turn2" and i == 0:
                    dve.wait_ge(s.on_dve, 4 + NTT)
                    layer_norm_vector(dve, m, s2)
                if who != "dve":
                    continue
                dve.wait_ge(s.ready, n + 1)
                if kind == "out":
                    dve.tensor_tensor(m.x[:, 2 * i:2 * i + 2, :], bank[0:TT, :].rearrange("p (j d) -> p j d", d=D),
                                      m.x[:, 2 * i:2 * i + 2, :], ALU.add).then_inc(s.on_dve, 1)
                else:
                    if i == 0:
                        dve.wait_ge(s.bias, 1)
                    dve.scalar_tensor_tensor(m.x[:, i, :], bank[0:TT, 0:D], float(RANK) ** -0.5, m.x[:, i, :],
                                             ALU.mult, ALU.add).then_inc(s.on_dve, 1)
            dve.wait_ge(s.gain, 1)
            for n in range(NQ):
                dve.wait_ge(s.std, n + 1)
                need(dve, s.qf, n - 1)
                dve.reciprocal(qn[n % 2][:, :], std[n % 2][:, :]).then_inc(s.rinv, 1)
                dve.wait_ge(s.rinv, n + 1)
                dve.scalar_tensor_tensor(qn[n % 2][:, :], bk[n % 4][:, 0:HALF], gain[:, 0:1], qn[n % 2][:, :],
                                         ALU.mult, ALU.mult).then_inc(s.qn, 1)

        @block.tensor
        def _(pe):
            for n, (who, kind, i) in enumerate(jobs):
                bank = bk[n % 8]
                banks.wait_free(pe, n)
                if kind == "vo":
                    if i == 0:
                        pe.wait_ge(s.ld_wv, 16)
                        pe.wait_ge(s.ld_wo, 16)
                    for c in range(2):
                        last = pe.matmul(bank[:, D * c:D * c + D], wvT[:, i, :], wo[:, 2 * i + c, :], start=True, stop=True)
                elif kind == "outT":
                    if i == 0:
                        pe.wait_ge(s.on_act, 8)
                    for h in range(H):
                        last = pe.matmul(bank[:, 0:HALF], vo[:, h, 128 * (i // 2):128 * (i // 2) + 128],
                                         m.qs[:, 8 * (i % 2):8 * (i % 2) + 8, h, :], start=h == 0, stop=h == H - 1)
                elif kind == "out":
                    if i == 0:
                        pe.wait_ge(s.on_act, 12)
                    for c in range(4):
                        j = 2 * i + c // 2
                        last = pe.transpose(bank[0:TT, 128 * c:128 * c + 128], yT[:, c % 2, TT * j:TT * j + TT], m.ident[:, :])
                elif kind in ("turn", "turn2"):
                    if i == 0:
                        pe.wait_ge(s1.xn if kind == "turn" else s2.xn, NTT)
                    for c in range(4):
                        j = 4 * (i % 2) + c
                        last = pe.transpose(bank[:, TT * c:TT * c + TT], m.xn[:, j, 128 * (i // 2):128 * (i // 2) + 128],
                                            m.ident[0:TT, 0:TT])
                else:
                    if i == 0:
                        pe.wait_ge(s.on_act, 16)
                        pe.wait_ge(s.fac, 1)
                    for kc in range(KC):
                        last = pe.matmul(bank[0:TT, 0:D], m.xnT[:, kc, TT * i:TT * i + TT], fsum[:, kc, :],
                                         start=kc == 0, stop=kc == KC - 1)
                last.then_inc(s.ready, 1)
            pe.wait_ge(s.on_act, 20)
            pe.wait_ge(s.on_dve, 4 + NTT)
            pe.wait_ge(s.ld_wq, 16)
            pe.wait_ge(s.ld_wk, 16)
            for n in range(NQ + 3):
                if n < NQ:
                    need(pe, s.qn, n - 3)
                    for kc in range(KC):
                        last = pe.matmul(bk[n % 4][:, 0:HALF], wq[:, kc, HD * (n // 2):HD * (n // 2) + HD],
                                         m.xnT[:, kc, HALF * (n % 2):HALF * (n % 2) + HALF], start=kc == 0, stop=kc == KC - 1)
                    last.then_inc(s.q, 1)
                if 1 <= n <= NQ:
                    pe.wait_ge(s.sq, n)
                    need(pe, s.std, n - 2)
                    pe.matmul(bk[4 + (n - 1) % 2][:, 0:HALF], m.ones[:, :], sq[(n - 1) % 2][:, :],
                              start=True, stop=True).then_inc(s.ms, 1)
                if n >= 3:
                    k = n - 3
                    pe.wait_ge(s.qn, k + 1)
                    need(pe, s.q_out, k - 1)
                    pe.matmul(bk[6 + k % 2][:, 0:HALF], wkT[:, k // 2, :], qn[k % 2][:, :], start=True, stop=True).then_inc(s.qf, 1)


def after_attention(nc, m, a, out, tag, sem):
    s = semaphores(sem, tag, LN_SEMAPHORES + ["ld_wv", "ld_wo", "ld_r", "ready", "on_act", "on_dve", "logit", "exp", "rt", "cw", "st",
                 "ld_e0", "ld_e1", "h1", "h3", "silu", "hid", "y", "add", "cwe", "st_out"])
    jobs = [("act", "vo", i) for i in range(8)]
    jobs += [("act", "outT", i) for i in range(4)]
    jobs += [("dve", "out", i) for i in range(4)]
    jobs += [("act", "turn", i) for i in range(4)]
    jobs += [("dve", "route", 0)]
    banks = Banks(jobs, {"act": s.on_act, "dve": s.on_dve})
    with ExitStack() as ctx:
        sb = lambda n, sh, dt: ctx.enter_context(nc.sbuf_tensor(f"{tag}_{n}", sh, dt))
        bk = [ctx.enter_context(nc.psum_tensor(f"{tag}_bk{i}", [128, 512], F32)) for i in range(8)]
        wvT = sb("wvT", [HD, H, C], F32)
        wo = sb("wo", [HD, H, D], F32)
        vo = sb("vo", [C, H, D], F32)
        yT = m.xnT
        wr = sb("wr", [128, KC, E], F32)
        tri = sb("tri", [TT, E, E], F32)
        lmax = sb("lmax", [TT, NTT], F32)
        lsub = sb("lsub", [TT, NTT, E], F32)
        ex = sb("ex", [TT, NTT, E], F32)
        cmp = sb("cmp", [TT, NTT, E, E], F32)
        rank = [sb(f"rank{i}", [TT, NTT, E], F32) for i in range(2)]
        sel = sb("sel", [TT, NTT, E], F32)
        top = sb("top", [TT, NTT], F32)
        rtop = sb("rtop", [TT, NTT], F32)
        cw = sb("cw", [TT, NTT, NEXP], F32)
        cwe = [sb(f"cwe{i}", [TT, NTT], F32) for i in range(2)]
        we = [sb(f"we{i}", [128, 2 * KC * 128 + D], F32) for i in range(2)]
        silu = [sb(f"silu{i}", [128, HALF], F32) for i in range(2)]
        hid = [sb(f"hid{i}", [128, QW], F32) for i in range(2)]
        block = ctx.enter_context(nc.Block())

        def experts(eng, body):
            body(0, 0)
            body(1, 1)
            with eng.Fori(1, NEXP // 2) as i:
                body(2 * i, 0)
                body(2 * i + 1, 1)

        @block.sync
        def _(sp):
            sp.dma_start(wvT[:, :, :], a.wvT1).then_inc(s.ld_wv, 16)
            sp.dma_start(wo[:, :, :], a.wo1).then_inc(s.ld_wo, 16)
            sp.dma_start(wr[:, :, :], a.w_router).then_inc(s.ld_r, 16)
            sp.dma_start(tri[:, :, :], a.tri.to_broadcast([TT, E, E])).then_inc(s.ld_r, 16)

            def body(e, par):
                need(sp, s.y, 4 * (e - 1))
                sp.dma_start(we[par][:, :], a.experts[bass.ds(e, 1), :, :]).then_inc((s.ld_e0, s.ld_e1)[par], 16)

            experts(sp, body)
            sp.wait_ge(s.add, NTT * NEXP)
            sp.dma_start(out, m.x[:, :, :]).then_inc(s.st_out, 16)
            sp.wait_ge(s.st_out, 16)

        @block.scalar
        def _(act):
            for n, (who, kind, i) in enumerate(jobs):
                if kind == "turn" and i == 0:
                    layer_norm_scalar(act, m, s)
                if who != "act":
                    continue
                bank = bk[n % 8]
                act.wait_ge(s.ready, n + 1)
                if kind == "vo":
                    act.activation(vo[:, 2 * i:2 * i + 2, :], bank[:, :], ACT.Copy).then_inc(s.on_act, 1)
                elif kind == "outT":
                    act.activation(yT[:, i // 2, HALF * (i % 2):HALF * (i % 2) + HALF], bank[:, 0:HALF],
                                   ACT.Copy).then_inc(s.on_act, 1)
                else:
                    act.activation(m.xnT[:, i // 2, HALF * (i % 2):HALF * (i % 2) + HALF], bank[:, 0:HALF],
                                   ACT.Copy).then_inc(s.on_act, 1)
            act.wait_ge(s.logit, 2)
            act.activation(ex[:, :, :], lsub[:, :, :], ACT.Exp).then_inc(s.exp, 1)

            def body(e, par):
                for half in range(2):
                    act.wait_ge(s.h1, 2 * e + half + 1)
                    need(act, s.hid, 2 * e + half - 1)
                    act.activation(silu[half][:, :], bk[half][:, 0:HALF], ACT.Silu).then_inc(s.silu, 1)

            experts(act, body)

        @block.vector
        def _(dve):
            for n, (who, kind, i) in enumerate(jobs):
                bank = bk[n % 8]
                if kind == "turn" and i == 0:
                    dve.wait_ge(s.on_dve, 4)
                    layer_norm_vector(dve, m, s)
                if who != "dve":
                    continue
                dve.wait_ge(s.ready, n + 1)
                if kind == "out":
                    dve.tensor_tensor(m.x[:, 2 * i:2 * i + 2, :], bank[0:TT, :].rearrange("p (j d) -> p j d", d=D),
                                      m.x[:, 2 * i:2 * i + 2, :], ALU.add).then_inc(s.on_dve, 1)
                else:
                    lg = bank[0:TT, 0:NTT * E].rearrange("p (j e) -> p j e", e=E)
                    dve.tensor_reduce(lmax[:, :], lg, AX.X, ALU.max).then_inc(s.logit, 1)
                    dve.wait_ge(s.logit, 1)
                    dve.tensor_tensor(lsub[:, :, :], lg, lmax[:, :].unsqueeze(2).to_broadcast([TT, NTT, E]),
                                      ALU.subtract).then_inc(s.logit, 1)
            dve.wait_ge(s.exp, 1)
            dve.wait_ge(s.ld_r, 32)
            other = ex[:, :, :].unsqueeze(2).to_broadcast([TT, NTT, E, E])
            own = ex[:, :, :].unsqueeze(3).to_broadcast([TT, NTT, E, E])
            dve.tensor_tensor(cmp[:, :, :, :], other, own, ALU.is_gt).then_inc(s.rt, 1)
            dve.wait_ge(s.rt, 1)
            dve.tensor_reduce(rank[0][:, :, :], cmp[:, :, :, :], AX.X, ALU.add).then_inc(s.rt, 1)
            dve.wait_ge(s.rt, 2)
            dve.tensor_tensor(cmp[:, :, :, :], other, own, ALU.is_equal).then_inc(s.rt, 1)
            dve.wait_ge(s.rt, 3)
            dve.tensor_tensor(cmp[:, :, :, :], cmp[:, :, :, :], tri[:, :, :].unsqueeze(1).to_broadcast([TT, NTT, E, E]),
                              ALU.mult).then_inc(s.rt, 1)
            dve.wait_ge(s.rt, 4)
            dve.tensor_reduce(rank[1][:, :, :], cmp[:, :, :, :], AX.X, ALU.add).then_inc(s.rt, 1)
            dve.wait_ge(s.rt, 5)
            dve.tensor_tensor(rank[0][:, :, :], rank[0][:, :, :], rank[1][:, :, :], ALU.add).then_inc(s.rt, 1)
            dve.wait_ge(s.rt, 6)
            dve.scalar_tensor_tensor(sel[:, :, :], rank[0][:, :, :], TOPK - 0.5, ex[:, :, :], ALU.is_lt, ALU.mult).then_inc(s.rt, 1)
            dve.wait_ge(s.rt, 7)
            dve.tensor_reduce(top[:, :], sel[:, :, :], AX.X, ALU.add).then_inc(s.rt, 1)
            dve.wait_ge(s.rt, 8)
            dve.reciprocal(rtop[:, :], top[:, :]).then_inc(s.rt, 1)
            dve.wait_ge(s.rt, 9)
            dve.scalar_tensor_tensor(cw[:, :, 0:E], sel[:, :, :], TOPK / (TOPK + 1.0),
                                     rtop[:, :].unsqueeze(2).to_broadcast([TT, NTT, E]), ALU.mult, ALU.mult).then_inc(s.cw, 1)
            dve.memset(cw[:, :, E:NEXP], 1.0 / (TOPK + 1.0)).then_inc(s.cw, 1)
            dve.wait_ge(s.cw, 2)

            def body(e, par):
                for half in range(2):
                    dve.wait_ge(s.silu, 2 * e + half + 1)
                    dve.wait_ge(s.h3, 2 * e + half + 1)
                    need(dve, s.y, 4 * (e - 1))
                    dve.tensor_tensor(hid[par][:, HALF * half:HALF * half + HALF], bk[2 + half][:, 0:HALF], silu[half][:, :],
                                      ALU.mult).then_inc(s.hid, 1)
                need(dve, s.add, NTT * (e - 1))
                dve.tensor_copy(cwe[par][:, :], cw[:, :, bass.ds(e, 1)].rearrange("p j o -> p (j o)")).then_inc(s.cwe, 1)
                dve.wait_ge(s.cwe, e + 1)
                need(dve, s.add, NTT * e)
                for j in range(NTT):
                    dve.wait_ge(s.y, 4 * e + j // 2 + 1)
                    dve.scalar_tensor_tensor(m.x[:, j, :], bk[4 + j // 2][0:TT, D * (j % 2):D * (j % 2) + D],
                                             cwe[par][:, j:j + 1], m.x[:, j, :], ALU.mult, ALU.add).then_inc(s.add, 1)

            experts(dve, body)

        @block.tensor
        def _(pe):
            for n, (who, kind, i) in enumerate(jobs):
                bank = bk[n % 8]
                banks.wait_free(pe, n)
                if kind == "vo":
                    if i == 0:
                        pe.wait_ge(s.ld_wv, 16)
                        pe.wait_ge(s.ld_wo, 16)
                    for c in range(2):
                        last = pe.matmul(bank[:, D * c:D * c + D], wvT[:, 2 * i + c, :], wo[:, 2 * i + c, :], start=True, stop=True)
                elif kind == "outT":
                    if i == 0:
                        pe.wait_ge(s.on_act, 8)
                    for h in range(H):
                        last = pe.matmul(bank[:, 0:HALF], vo[:, h, 128 * (i // 2):128 * (i // 2) + 128],
                                         m.qs[:, 8 * (i % 2):8 * (i % 2) + 8, h, :], start=h == 0, stop=h == H - 1)
                elif kind == "out":
                    if i == 0:
                        pe.wait_ge(s.on_act, 12)
                    for c in range(4):
                        j = 2 * i + c // 2
                        last = pe.transpose(bank[0:TT, 128 * c:128 * c + 128], yT[:, c % 2, TT * j:TT * j + TT], m.ident[:, :])
                elif kind == "turn":
                    if i == 0:
                        pe.wait_ge(s.xn, NTT)
                    for c in range(4):
                        j = 4 * (i % 2) + c
                        last = pe.transpose(bank[:, TT * c:TT * c + TT], m.xn[:, j, 128 * (i // 2):128 * (i // 2) + 128],
                                            m.ident[0:TT, 0:TT])
                else:
                    pe.wait_ge(s.on_act, 16)
                    pe.wait_ge(s.ld_r, 32)
                    for j in range(NTT):
                        for kc in range(KC):
                            last = pe.matmul(bank[0:TT, E * j:E * j + E], m.xnT[:, kc, TT * j:TT * j + TT], wr[:, kc, :],
                                             start=kc == 0, stop=kc == KC - 1)
                last.then_inc(s.ready, 1)
            pe.wait_ge(s.logit, 2)

            def body(e, par):
                pe.wait_ge((s.ld_e0, s.ld_e1)[par], 16 * (e // 2 + 1))
                w = we[par]
                for half in range(2):
                    need(pe, s.silu, 2 * e + half - 1)
                    for kc in range(KC):
                        last = pe.matmul(bk[half][:, 0:HALF], w[:, 128 * kc:128 * kc + 128],
                                         m.xnT[:, kc, HALF * half:HALF * half + HALF], start=kc == 0, stop=kc == KC - 1)
                    last.then_inc(s.h1, 1)
                    need(pe, s.hid, 2 * e + half - 1)
                    for kc in range(KC):
                        last = pe.matmul(bk[2 + half][:, 0:HALF], w[:, 256 + 128 * kc:384 + 128 * kc],
                                         m.xnT[:, kc, HALF * half:HALF * half + HALF], start=kc == 0, stop=kc == KC - 1)
                    last.then_inc(s.h3, 1)
                for j in range(NTT):
                    if j % 2 == 0:
                        pe.wait_ge(s.hid, 2 * e + (1 if j < 4 else 2))
                        need(pe, s.add, NTT * (e - 1) + j + 2)
                    last = pe.matmul(bk[4 + j // 2][0:TT, D * (j % 2):D * (j % 2) + D], hid[par][:, TT * j:TT * j + TT],
                                     w[:, 512:512 + D], start=True, stop=True)
                    if j % 2 == 1:
                        last.then_inc(s.y, 1)

            experts(pe, body)


def build(nc, a, out):
    with ExitStack() as ctx:
        sb = lambda n, sh, dt: ctx.enter_context(nc.sbuf_tensor(n, sh, dt))
        sem = lambda n: ctx.enter_context(nc.semaphore(n))
        m = Buffers()
        m.x = sb("x", [TT, NTT, D], F32)
        m.qs = sb("qs", [128, B, H, QS], F32)
        m.rk = sb("rk", [KT, B, NT, H], F32)
        m.ident = sb("ident", [128, 128], F32)
        m.ones = sb("ones", [128, 128], F32)
        m.ones8 = sb("ones8", [QBLK, KT], F32R)
        m.diag = sb("diag", [QBLK, QW], F32)
        m.eps = sb("eps", [128, 1], F32)
        m.mask_bias = sb("mask_bias", [KT, B, NT], F32)
        m.valid = sb("valid", [128, B], F32)
        m.norm_hi = sb("norm_hi", [C, NG * 512], F32R)
        m.norm_lo = sb("norm_lo", [C, NG * 512], F32R)

        def with_norm_buffers(run, *args):
            with ExitStack() as inner:
                add = lambda n, sh: inner.enter_context(nc.sbuf_tensor(f"{args[0]}_{n}", sh, F32))
                m.xn, m.xnT = add("xn", [TT, NTT, D]), add("xnT", [128, KC, QW])
                m.stats, m.meanvar = add("stats", [TT, NTT, 6]), add("meanvar", [TT, NTT, 2])
                m.vareps, m.std, m.rstd = add("vareps", [TT, NTT]), add("std", [TT, NTT]), add("rstd", [TT, NTT])
                run(*args[1:])

        with_norm_buffers(before_attention, "pre", nc, m, a, "pre", sem)
        attention(nc, m, a, "l0", sem, True)
        with_norm_buffers(between_layers, "mid", nc, m, a, "mid", sem)
        attention(nc, m, a, "l1", sem, False)
        with_norm_buffers(after_attention, "post", nc, m, a, out, "post", sem)


def kernel(**inputs):
    import numpy as np
    import concourse.bacc as bacc
    from concourse import mybir as _mybir
    from concourse.bass_utils import run_bass_kernel_spmd as run

    i = {k: np.asarray(v) for k, v in inputs.items()}
    c = np.ascontiguousarray
    ctx = i["ctx_1024"]
    mask = i["mask_BxS2_bf1"].view(np.uint8)
    heads = lambda w, n: c(w.reshape(w.shape[0], n, 128).transpose(2, 1, 0))
    chunks = lambda w: c(w.reshape(2, 128, -1).transpose(1, 0, 2))
    w1 = np.concatenate([i["L1_ffn_we1"], i["L1_ffn_ws1"].reshape(256, 4, 128).transpose(1, 0, 2)])
    w3 = np.concatenate([i["L1_ffn_we3"], i["L1_ffn_ws3"].reshape(256, 4, 128).transpose(1, 0, 2)])
    w2 = np.concatenate([i["L1_ffn_we2"], i["L1_ffn_ws2"].reshape(4, 128, 256)])
    side = lambda w: w.reshape(-1, 2, 128, 128).transpose(0, 2, 1, 3).reshape(-1, 128, 256)
    arrays = {
        "x": c(i["x"].reshape(8, 112, 256).transpose(1, 0, 2)),
        "ctxT": c(ctx.transpose(2, 0, 1)),
        "ctxN": c(ctx.reshape(16, 12, 125, 128).transpose(0, 2, 1, 3)),
        "mask": c(mask),
        "mask_cols": c(mask.reshape(16, 12, 125).transpose(2, 0, 1)),
        "ident": np.eye(128, dtype=np.float32),
        "diag": np.repeat(np.eye(8, dtype=np.float32), 112, axis=1),
        "tri": np.tril(np.ones((16, 16), np.float32), -1).reshape(1, 16, 16),
        "wqT0": heads(i["L0_xattn_Wq"], 16), "wkT0": heads(i["L0_xattn_Wk"], 8), "wvT0": heads(i["L0_xattn_Wv"], 8),
        "wo0": c(i["L0_xattn_Wo"].reshape(16, 128, 256).transpose(1, 0, 2)),
        "factors": c(i["L0_ffn_factors"].reshape(8, 2, 128, 256).transpose(2, 1, 0, 3)),
        "bias": i["L0_ffn_bias"].reshape(1, 256),
        "wq1": chunks(i["L1_xattn_Wq"]), "wkT1": heads(i["L1_xattn_Wk"], 16), "wvT1": heads(i["L1_xattn_Wv"], 16),
        "wk1": c(i["L1_xattn_Wk"][:, 1536:]),
        "wo1": c(i["L1_xattn_Wo"].reshape(16, 128, 256).transpose(1, 0, 2)),
        "gains": c(np.stack([i["L1_xattn_gq"], i["L1_xattn_gk"]], axis=1)),
        "w_router": chunks(i["L1_ffn_w_router"]),
        "experts": c(np.concatenate([side(w1), side(w3), w2], axis=2)),
    }
    nc = bacc.Bacc("TRN2", target_bir_lowering=False, num_devices=1)
    a = namedtuple("Arrays", list(arrays))(*[
        nc.dram_tensor(f"in_{n}", v.shape, _mybir.dt.from_np(v.dtype), kind="ExternalInput").ap()
        for n, v in arrays.items()])
    out = nc.dram_tensor("out_x", (112, 8, 256), F32, kind="ExternalOutput").ap()
    build(nc, a, out)
    r = run(nc, [{f"in_{n}": v for n, v in arrays.items()}], core_ids=[0])
    return r.results[0]["out_x"].transpose(1, 0, 2).reshape(16, 56, 256)
```

```python
from collections import namedtuple
from contextlib import ExitStack

import concourse.bass as bass
from concourse import mybir

F32 = mybir.dt.float32
F32R = mybir.dt.float32r
BF16 = mybir.dt.bfloat16
U8 = mybir.dt.uint8
ALU = mybir.AluOpType
ACT = mybir.ActivationFunctionType
AX = mybir.AxisListType

B, QS, D = 16, 56, 256
S, C = 1500, 128
H, HD, G0 = 16, 128, 8
KT, NT = 125, 12
QW, HALF = H * QS, H * QS // 2
TT, NTT = 112, 8
KC = D // 128
RANK, E, HS = 8, 16, 512
NEXP = E + HS // 128
TOPK = 4
LN_EPS = 1e-5
RMS_EPS = 1e-5
MASKED = 32768.0
SCALE = float(HD) ** -0.5
MC, NMC = 500, 3
QBLK = 8
NG = 4
DVE_G = 3

STEPS = ["MMMMMA"] * 3 + ["MMMNNA"] * 3 + ["NNNNNA"] * 2 + ["TNNNNNA"] + ["NNNNNA"] * 3
SIDE = "".join(STEPS)
NSIDE = len(SIDE)
STEP_AT = [sum(len(x) for x in STEPS[:t]) for t in range(NT + 1)]
SIDE_V = sum(x != "A" for x in SIDE)
SIDE_A = SIDE.count("A")
assert (SIDE.count("M"), SIDE.count("N"), SIDE_A) == (QBLK * NMC, NT * DVE_G, NT) and NSIDE % 2 == 1


def need(eng, sem, value):
    if isinstance(value, int) and value <= 0:
        return
    eng.wait_ge(sem, value)


def side_number(k):
    return SIDE[:k].count(SIDE[k])


def side_done(s, batch, k):
    if SIDE[k] == "A":
        return s.side_act, SIDE_A * batch + SIDE[:k + 1].count("A")
    return s.side_dve, SIDE_V * batch + sum(x != "A" for x in SIDE[:k + 1])


def layer_norm_vector(dve, m, s):
    for j in range(NTT):
        dve.bn_stats(m.stats[:, j, :], m.x[:, j, :]).then_inc(s.ln_stats, 1)
    dve.wait_ge(s.ln_stats, NTT)
    for j in range(NTT):
        dve.bn_aggr(m.meanvar[:, j, :], m.stats[:, j, :]).then_inc(s.ln_aggr, 1)
    dve.wait_ge(s.ln_aggr, NTT)
    dve.tensor_scalar(m.vareps[:, :], m.meanvar[:, :, 1], LN_EPS, None, ALU.add).then_inc(s.ln_var, 1)
    dve.wait_ge(s.ln_std, 1)
    dve.reciprocal(m.rstd[:, :], m.std[:, :]).then_inc(s.ln_rstd, 1)
    dve.wait_ge(s.ln_rstd, 1)
    for j in range(NTT):
        dve.tensor_scalar(m.xn[:, j, :], m.x[:, j, :], m.meanvar[:, j, 0:1], m.rstd[:, j:j + 1],
                          ALU.subtract, ALU.mult).then_inc(s.xn, 1)


def layer_norm_scalar(act, m, s):
    act.wait_ge(s.ln_var, 1)
    act.activation(m.std[:, :], m.vareps[:, :], ACT.Sqrt).then_inc(s.ln_std, 1)


LN_SEMAPHORES = ["ln_stats", "ln_aggr", "ln_var", "ln_std", "ln_rstd", "xn"]


def semaphores(sem, tag, names):
    return namedtuple("Semaphores", names)(*[sem(f"{tag}_{n}") for n in names])


class Buffers:
    pass


class Banks:

    def __init__(self, jobs, sems, count=8):
        self.jobs, self.sems, self.count = jobs, sems, count

    def number(self, n):
        return sum(j[0] == self.jobs[n][0] for j in self.jobs[:n + 1])

    def wait_free(self, pe, n):
        if n >= self.count:
            pe.wait_ge(self.sems[self.jobs[n - self.count][0]], self.number(n - self.count))


def before_attention(nc, m, a, tag, sem):
    s = semaphores(sem, tag, LN_SEMAPHORES + ["ld_x", "ld_mask", "ld_const", "ld_w0", "ld_w1", "const", "ready", "on_act", "on_dve", "xnT",
                 "fold", "w_hi", "g_hi", "mcount"])
    jobs = [("act", "fold", i) for i in range(8)]
    jobs += [("dve", "gram", g) for g in range(DVE_G)]
    jobs += [("dve", "valid", 0)]
    jobs += [("act", "turn", i) for i in range(4)]
    jobs += [(("act", "dve")[i % 2], "query", i) for i in range(2 * H)]
    banks = Banks(jobs, {"act": s.on_act, "dve": s.on_dve})
    with ExitStack() as ctx:
        sb = lambda n, sh, dt: ctx.enter_context(nc.sbuf_tensor(f"{tag}_{n}", sh, dt))
        bk = [ctx.enter_context(nc.psum_tensor(f"{tag}_bk{i}", [128, 512], F32)) for i in range(8)]
        wqT = sb("wqT", [HD, H, D], F32)
        wkT0 = sb("wkT0", [HD, G0, C], F32)
        wkT1 = sb("wkT1", [HD, H, C], F32)
        wk1 = sb("wk1", [C, 512], F32)
        fold = sb("fold", [128, H, KC, C], F32)
        msum = sb("msum", [KT, B], F32)
        masku = sb("masku", [KT, B, NT], U8)
        maskf = sb("maskf", [KT, B, NT], F32)
        block = ctx.enter_context(nc.Block())

        @block.sync
        def _(sp):
            sp.dma_start(wqT[:, :, :], a.wqT0).then_inc(s.ld_w0, 16)
            sp.dma_start(wkT0[:, :, :], a.wkT0).then_inc(s.ld_w0, 16)
            sp.dma_start(m.x[:, :, :], a.x).then_inc(s.ld_x, 16)
            sp.dma_start(wkT1[:, :, :], a.wkT1).then_inc(s.ld_w1, 16)
            sp.dma_start(wk1[:, :], a.wk1).then_inc(s.ld_w1, 16)
            sp.dma_start(masku[:, :, :], a.mask_cols).then_inc(s.ld_mask, 16)
            sp.dma_start(m.ident[:, :], a.ident).then_inc(s.ld_const, 16)
            sp.dma_start(m.diag[:, :], a.diag).then_inc(s.ld_const, 16)
            sp.dma_start(m.row_of[:, :, :], a.row_of).then_inc(s.ld_const, 16)
            sp.dma_start(m.pick[:, :, :], a.pick).then_inc(s.ld_const, 16)

        @block.scalar
        def _(act):
            layer_norm_scalar(act, m, s)
            act.wait_ge(s.ld_w1, 32)
            act.activation(m.norm_hi[:, DVE_G * 512:], wk1[:, :], ACT.Copy).then_inc(s.w_hi, 1)
            for n, (who, kind, i) in enumerate(jobs):
                bank = bk[n % 8]
                if kind == "fold":
                    act.wait_ge(s.ready, n + 1)
                    act.activation(fold[:, 2 * i:2 * i + 2, :, :], bank[:, :], ACT.Copy, scale=SCALE).then_inc(s.on_act, 1)
                elif kind == "gram":
                    act.wait_ge(s.ready, n + 1)
                    act.activation(m.norm_hi[:, 512 * i:512 * i + 512], bank[:, :], ACT.Copy).then_inc(s.g_hi, 1)
                elif kind == "turn":
                    act.wait_ge(s.ready, n + 1)
                    act.activation(m.xnT[:, i // 2, HALF * (i % 2):HALF * (i % 2) + HALF], bank[:, 0:HALF],
                                   ACT.Copy).then_inc(s.on_act, 1)
                elif who == "act":
                    act.wait_ge(s.ready, n + 1)
                    h, half = i // 2, i % 2
                    act.activation(m.qs[:, 8 * half:8 * half + 8, h, :],
                                   bank[:, 0:HALF].rearrange("p (b q) -> p b q", q=QS), ACT.Copy).then_inc(s.on_act, 1)

        @block.vector
        def _(dve):
            dve.memset(m.ones[:, :], 1.0).then_inc(s.const, 1)
            dve.memset(m.ones8[:, :].bitcast(F32), 1.0).then_inc(s.const, 1)
            dve.memset(m.eps[:, :], RMS_EPS).then_inc(s.const, 1)
            dve.wait_ge(s.ld_x, 16)
            layer_norm_vector(dve, m, s)
            dve.wait_ge(s.ld_mask, 16)
            dve.tensor_scalar(m.mask_bias[:, :, :], masku[:, :, :], MASKED, -MASKED, ALU.mult, ALU.add).then_inc(s.const, 1)
            dve.tensor_copy(maskf[:, :, :], masku[:, :, :]).then_inc(s.mcount, 1)
            dve.wait_ge(s.mcount, 1)
            dve.tensor_reduce(msum[:, :], maskf[:, :, :], AX.X, ALU.add).then_inc(s.mcount, 1)
            dve.wait_ge(s.w_hi, 1)
            dve.tensor_tensor(m.norm_lo[:, DVE_G * 512:], wk1[:, :], m.norm_hi[:, DVE_G * 512:].bitcast(F32),
                              ALU.subtract).then_inc(s.const, 1)
            for n, (who, kind, i) in enumerate(jobs):
                bank = bk[n % 8]
                if who != "dve":
                    continue
                dve.wait_ge(s.ready, n + 1)
                if kind == "gram":
                    dve.wait_ge(s.g_hi, i + 1)
                    cols = slice(512 * i, 512 * i + 512)
                    dve.tensor_tensor(m.norm_lo[:, cols], bank[:, :], m.norm_hi[:, cols].bitcast(F32),
                                      ALU.subtract).then_inc(s.on_dve, 1)
                elif kind == "valid":
                    dve.tensor_scalar(m.valid[:, :], bank[:, 0:B], 1.0, None, ALU.min).then_inc(s.on_dve, 1)
                else:
                    h, half = i // 2, i % 2
                    dve.tensor_copy(m.qs[:, 8 * half:8 * half + 8, h, :],
                                    bank[:, 0:HALF].rearrange("p (b q) -> p b q", q=QS)).then_inc(s.on_dve, 1)

        @block.tensor
        def _(pe):
            for n, (who, kind, i) in enumerate(jobs):
                bank = bk[n % 8]
                banks.wait_free(pe, n)
                if kind == "fold":
                    if i == 0:
                        pe.wait_ge(s.ld_w0, 32)
                    for c in range(4):
                        h, kc = 2 * i + c // 2, c % 2
                        last = pe.matmul(bank[:, 128 * c:128 * c + 128], wqT[:, h, 128 * kc:128 * kc + 128],
                                         wkT0[:, h // 2, :], start=True, stop=True)
                elif kind == "gram":
                    if i == 0:
                        pe.wait_ge(s.ld_w1, 32)
                    for c in range(4):
                        h = 4 * i + c
                        last = pe.matmul(bank[:, 128 * c:128 * c + 128], wkT1[:, h, :], wkT1[:, h, :],
                                         start=True, stop=True)
                elif kind == "valid":
                    pe.wait_ge(s.mcount, 2)
                    pe.wait_ge(s.const, 1)
                    last = pe.matmul(bank[:, 0:B], m.ones[0:KT, :], msum[:, :], start=True, stop=True)
                elif kind == "turn":
                    if i == 0:
                        pe.wait_ge(s.ld_const, 64)
                        pe.wait_ge(s.xn, NTT)
                    for c in range(4):
                        j = 4 * (i % 2) + c
                        last = pe.transpose(bank[:, TT * c:TT * c + TT], m.xn[:, j, 128 * (i // 2):128 * (i // 2) + 128],
                                            m.ident[0:TT, 0:TT])
                else:
                    if i == 0:
                        pe.wait_ge(s.on_act, 12)
                    h, half = i // 2, i % 2
                    for kc in range(KC):
                        last = pe.matmul(bank[:, 0:HALF], fold[:, h, kc, :], m.xnT[:, kc, HALF * half:HALF * half + HALF],
                                         start=kc == 0, stop=kc == KC - 1)
                last.then_inc(s.ready, 1)


def attention(nc, m, a, tag, sem, first):
    s = semaphores(sem, tag, [
        "ld_land", "ld_nat", "ld_mask", "ctx_hi", "ctx_lo", "q_hi", "q_lo", "nat_hi", "nat_lo", "xq", "mask_row",
        "scores", "scaled", "probs", "p_hi", "p_lo0", "p_lo1", "pv", "acc", "den", "inv", "spread", "o_raw", "o_done",
        "side_pe", "side_dve", "side_act", "negmax", "rk_pre", "dve_passed", "pool_passed"])
    consumed = s.probs if first else s.scaled
    LAG = 1 if first else 2
    NP = 2 if first else 3
    POOL_LO = NT // 2 if first else 0
    with ExitStack() as ctx:
        sb = lambda n, sh, dt: ctx.enter_context(nc.sbuf_tensor(f"{tag}_{n}", sh, dt))
        psum = lambda n, sh: ctx.enter_context(nc.psum_tensor(f"{tag}_{n}", sh, F32))
        land = sb("land", [C, S], F32)
        chi = [sb(f"chi{i}", [C, S], F32R) for i in range(2)]
        clo = [sb(f"clo{i}", [C, S], F32R) for i in range(2)]
        nat = sb("nat", [KT, NT, C], F32)
        nhi = [sb(f"nhi{i}", [KT, NT, C], F32R) for i in range(2)]
        nlo = [sb(f"nlo{i}", [KT, NT, C], F32R) for i in range(2)]
        qhi = [sb(f"qhi{i}", [C, QW], F32R) for i in range(2)]
        qlo = [sb(f"qlo{i}", [C, QW], F32R) for i in range(2)]
        P = [sb(f"probs{i}", [KT, QW], F32) for i in range(NP)]
        phi = [sb(f"phi{i}", [KT, QW], F32R) for i in range(NP)]
        plo = [sb(f"plo{i}", [KT, QW], F32R) for i in range(NP)]
        acc = sb("acc", [KT, QW], F32)
        inv = sb("inv", [QBLK, TT], F32)
        if first:
            masku = sb("masku", [TT, S], U8)
            mrow = sb("mrow", [TT, S], BF16)
            mx = sb("mx", [TT, QBLK, NMC], F32)
            negmax = sb("negmax", [TT, QBLK], F32)
            shift = [sb(f"shift{i}", [QBLK, QW], F32R) for i in range(2)]
            msq = sb("msq", [KT, NT, 12], F32)
            msqa = sb("msqa", [KT, NT, 4], F32)
            side = [psum(f"side{i}", [128, 512]) for i in range(2)]
        else:
            scaled = [sb(f"scaled{i}", [KT, QW], F32) for i in range(2)]
            norm_banks = psum("norm", [128, 2, 512])
        slots = psum("slots", [128, 2, 2, 512])
        psO = psum("psO", [128, 2, 512])
        block = ctx.enter_context(nc.Block())

        def slot_of(par, t):
            return (par, 1 - par)[t] if first and t < 2 else (par + 1 + t) % 2 if first else t % 2

        def norm_slot(par):
            return slots[:, par, :, :] if first else norm_banks[:, :, :]

        def low_done(eng, b, t):
            if POOL_LO:
                eng.wait_ge((s.p_lo0, s.p_lo1)[t % 2], POOL_LO * b + t // 2 + 1)
            else:
                eng.wait_ge(s.p_lo1, NT * b + t + 1)

        def batches(eng, body):
            body(0, 0, True, True)
            body(1, 1, True, True)
            with eng.Fori(1, B // 2 - 1) as i:
                body(2 * i, 0, True, True)
                body(2 * i + 1, 1, True, True)
            body(B - 2, 0, True, False)
            body(B - 1, 1, False, False)

        def ahead(b, par, t, nxt):
            if t + LAG < NT:
                return [(b, par, t + LAG)]
            return [(b + 1, 1 - par, t + LAG - NT)] if nxt else []

        @block.sync
        def _(sp):
            def load_land(b):
                need(sp, s.ctx_lo, b)
                sp.dma_start(land[:, :], a.ctxT[:, bass.ds(b, 1), :]).then_inc(s.ld_land, 16)

            def load_nat(b, par):
                if first:
                    need(sp, s.side_dve, SIDE_V * b)
                else:
                    need(sp, s.nat_lo, b)
                sp.dma_start(nat[:, :, :], a.ctxN[bass.ds(b, 1), :, :, :]).then_inc(s.ld_nat, 16)

            def load_mask(b):
                need(sp, s.mask_row, b)
                sp.dma_start(masku[:, :], a.mask[bass.ds(b, 1), :].to_broadcast([TT, S])).then_inc(s.ld_mask, 16)

            def body(b, par, nxt, nxt2):
                if nxt:
                    load_nat(b + 1, 1 - par)
                if nxt2:
                    load_land(b + 2)
                    if first:
                        load_mask(b + 2)

            load_land(0)
            load_nat(0, 0)
            if first:
                load_mask(0)
            load_land(1)
            if first:
                load_mask(1)
            batches(sp, body)

        @block.scalar
        def _(act):
            def high_parts(b, par):
                act.wait_ge(s.ld_land, 16 * (b + 1))
                need(act, s.scores, NT * (b - 1))
                act.activation(chi[par][:, :], land[:, :], ACT.Copy).then_inc(s.ctx_hi, 1)
                act.activation(qhi[par][:, :], m.qs[:, bass.ds(b, 1), :, :].rearrange("p o h q -> p (o h q)"),
                               ACT.Copy).then_inc(s.q_hi, 1)

            def nat_high(b, par):
                act.wait_ge(s.ld_nat, 16 * (b + 1))
                need(act, s.pv, NT * (b - 1))
                act.activation(nhi[par][:, :, :], nat[:, :, :], ACT.Copy).then_inc(s.nat_hi, 1)

            def norms(b, par, k):
                t = side_number(k)
                act.wait_ge(s.side_pe, NSIDE * b + k + 1)
                if t == 0:
                    need(act, s.rk_pre, 2 * b)
                bank = side[(k + par) % 2]
                for c in range(4):
                    sq = bank[0:KT, 128 * c:128 * c + 128]
                    last = act.activation(sq, sq, ACT.Square, accum_out=msqa[:, t, c:c + 1])
                last.then_inc(s.side_act, 1)

            def exp(b, par, t):
                if first:
                    act.wait_ge(s.scores, NT * b + t + 1)
                    src = slots[0:KT, slot_of(par, t), :, 0:HALF]
                else:
                    act.wait_ge(s.scaled, NT * b + t + 1)
                    src = scaled[t % 2][:, :].rearrange("p (a c) -> p a c", a=2)
                need(act, s.pv, NT * b + t + 1 - NP)
                if t >= NP:
                    need(act, s.acc, (NT - 1) * b + max(1, t - NP))
                else:
                    need(act, s.acc, (NT - 1) * b + t + 1 - NP)
                dst = P[t % NP][:, :].rearrange("p (a c) -> p a c", a=2)
                if first:
                    bias = m.mask_bias[:, bass.ds(b, 1), t].rearrange("p o -> p o")
                    act.activation(dst, src, ACT.Exp, bias=bias).then_inc(s.probs, 1)
                else:
                    act.activation(dst, src, ACT.Exp).then_inc(s.probs, 1)
                act.wait_ge(s.probs, NT * b + t + 1)
                act.activation(phi[t % NP][:, :], P[t % NP][:, :], ACT.Copy).then_inc(s.p_hi, 1)

            def values_out(b):
                act.wait_ge(s.pv, NT * b + NT)
                dst = m.qs[:, bass.ds(b, 1), :, :].rearrange("p o (a h) q -> p (o a) (h q)", a=2)
                if first:
                    act.activation(dst, psO[:, :, 0:HALF], ACT.Copy, scale=m.valid[:, bass.ds(b, 1)]).then_inc(s.o_raw, 1)
                else:
                    act.activation(dst, psO[:, :, 0:HALF], ACT.Copy).then_inc(s.o_raw, 1)

            def body(b, par, nxt, nxt2):
                for t in range(NT):
                    if t == NT - LAG and nxt2:
                        high_parts(b + 2, par)
                    for tile in ahead(b, par, t, nxt):
                        exp(*tile)
                    if nxt and t == 1:
                        nat_high(b + 1, 1 - par)
                    if first and nxt:
                        for k in range(STEP_AT[t], STEP_AT[t + 1]):
                            if SIDE[k] == "A":
                                norms(b + 1, 1 - par, k)
                values_out(b)

            high_parts(0, 0)
            nat_high(0, 0)
            act.wait_ge(s.ctx_lo, 1)
            high_parts(1, 1)
            if first:
                for k in range(NSIDE):
                    if SIDE[k] == "A":
                        norms(0, 0, k)
            for t in range(LAG):
                exp(0, 0, t)
            batches(act, body)

        @block.gpsimd
        def _(pool):
            def low_parts(b, par):
                pool.wait_ge(s.ctx_hi, b + 1)
                pool.tensor_tensor(clo[par][:, :], land[:, :], chi[par][:, :].bitcast(F32), ALU.subtract).then_inc(s.ctx_lo, 1)
                if first:
                    pool.wait_ge(s.q_hi, b + 1)
                    pool.tensor_tensor(qlo[par][:, :], m.qs[:, bass.ds(b, 1), :, :].rearrange("p o h q -> p (o h q)"),
                                       qhi[par][:, :].bitcast(F32), ALU.subtract).then_inc(s.q_lo, 1)

            def nat_low(b, par):
                pool.wait_ge(s.nat_hi, b + 1)
                pool.tensor_tensor(nlo[par][:, :, :], nat[:, :, :], nhi[par][:, :, :].bitcast(F32),
                                   ALU.subtract).then_inc(s.nat_lo, 1)

            def mask_row(b):
                pool.wait_ge(s.ld_mask, 16 * (b + 1))
                if not (isinstance(b, int) and b == 0):
                    q, v = side_done(s, b - 1, SIDE.rindex("M"))
                    pool.wait_ge(q, v)
                pool.sem_inc(s.pool_passed, 1)
                pool.tensor_scalar(mrow[:, :], masku[:, :], MASKED, -MASKED, ALU.mult, ALU.add).then_inc(s.mask_row, 1)

            def prob_low(b, par, t):
                pool.wait_ge(s.p_hi, NT * b + t + 1)
                pool.tensor_tensor(plo[t % NP][:, :], P[t % NP][:, :], phi[t % NP][:, :].bitcast(F32),
                                   ALU.subtract).then_inc(s.p_lo0, 1)

            def add(b, par, t):
                pool.wait_ge(s.probs, NT * b + t + 1)
                if t == 1:
                    need(pool, s.den, b)
                    pool.tensor_tensor(acc[:, :], P[0][:, :], P[1][:, :], ALU.add).then_inc(s.acc, 1)
                else:
                    pool.wait_ge(s.acc, (NT - 1) * b + t - 1)
                    pool.tensor_tensor(acc[:, :], acc[:, :], P[t % NP][:, :], ALU.add).then_inc(s.acc, 1)

            def body(b, par, nxt, nxt2):
                for t in range(NT):
                    if POOL_LO and t % 2 == 0:
                        prob_low(b, par, t)
                    if t > 0:
                        add(b, par, t)
                    if t == 3 and nxt and first:
                        nat_low(b + 1, 1 - par)
                    if t == 8 and first and nxt2:
                        mask_row(b + 2)
                if nxt2:
                    low_parts(b + 2, par)

            low_parts(0, 0)
            if first:
                nat_low(0, 0)
                mask_row(0)
            low_parts(1, 1)
            if first:
                mask_row(1)
            batches(pool, body)

        @block.vector
        def _(dve):
            def max_chunk(b, par, k):
                i = side_number(k)
                j, c = i // NMC, i % NMC
                dve.wait_ge(s.side_pe, NSIDE * b + k + 1)
                if i == 0:
                    dve.wait_ge(s.mask_row, b + 1)
                    need(dve, s.negmax, b)
                bank = side[(k + par) % 2][0:TT, 0:MC]
                dve.sem_inc(s.dve_passed, 1)
                dve.tensor_tensor_reduce(bank, bank, mrow[:, MC * c:MC * c + MC], 1.0, -3.0e38, ALU.add, ALU.max,
                                         mx[:, j, c:c + 1]).then_inc(s.side_dve, 1)
                if i == QBLK * NMC - 1:
                    q, v = side_done(s, b, k)
                    dve.wait_ge(q, v)
                    dve.tensor_reduce(negmax[:, :], mx[:, :, :], AX.X, ALU.max, negate=True).then_inc(s.negmax, 1)

            def spread_shift(b, par, k):
                dve.wait_ge(s.side_pe, NSIDE * b + k + 1)
                need(dve, s.scores, NT * (b - 1))
                src = side[(k + par) % 2][0:QBLK, 0:TT].unsqueeze(1).to_broadcast([QBLK, QBLK, TT])
                dve.tensor_tensor(shift[par][:, :].rearrange("p (j c) -> p j c", c=TT), src,
                                  m.diag[:, :].rearrange("p (j c) -> p j c", c=TT), ALU.mult).then_inc(s.side_dve, 1)

            def norms(b, par, k):
                i = side_number(k)
                t, g = i // DVE_G, i % DVE_G
                if i == 0:
                    dve.wait_ge(s.nat_lo, b + 1)
                    dve.scalar_tensor_tensor(nat[:, :, :], nat[:, :, :], 2.0, nhi[par][:, :, :].bitcast(F32),
                                             ALU.mult, ALU.subtract).then_inc(s.xq, 1)
                    dve.wait_ge(s.xq, b + 1)
                    need(dve, s.rk_pre, 2 * b)
                dve.wait_ge(s.side_pe, NSIDE * b + k + 1)
                bank = side[(k + par) % 2]
                for c in range(4):
                    u = bank[0:KT, 128 * c:128 * c + 128]
                    last = dve.tensor_tensor_reduce(u, u, nat[:, t, :], 1.0, 0.0, ALU.mult, ALU.add,
                                                    msq[:, t, 4 * g + c:4 * g + c + 1])
                last.then_inc(s.side_dve, 1)

            def side_job(b, par, k):
                {"M": max_chunk, "N": norms, "T": spread_shift}[SIDE[k]](b, par, k)

            def norms_out(b):
                dve.wait_ge(s.side_dve, SIDE_V * (b + 1))
                dve.wait_ge(s.side_act, SIDE_A * (b + 1))
                dst = m.rk[:, bass.ds(b, 1), :, :].rearrange("p o t h -> p (o t) h")
                dve.tensor_scalar(dst[:, :, 0:12], msq[:, :, :], 1.0 / HD, RMS_EPS, ALU.mult, ALU.add).then_inc(s.rk_pre, 1)
                dve.tensor_scalar(dst[:, :, 12:16], msqa[:, :, :], 1.0 / HD, RMS_EPS, ALU.mult, ALU.add).then_inc(s.rk_pre, 1)

            def scale_scores(b, par, t):
                dve.wait_ge(s.scores, NT * b + t + 1)
                need(dve, s.probs, NT * b + t - 1)
                src = slots[0:KT, slot_of(par, t), :, 0:HALF].rearrange("p a (h q) -> p a h q", q=QS)
                rk = m.rk[:, bass.ds(b, 1), t, :].rearrange("p o (a h) -> p (o a) h", a=2).unsqueeze(3)
                dve.tensor_tensor(scaled[t % 2][:, :].rearrange("p (a h q) -> p a h q", a=2, q=QS), src,
                                  rk.to_broadcast([KT, 2, H // 2, QS]), ALU.mult).then_inc(s.scaled, 1)

            def prob_low(b, par, t):
                dve.wait_ge(s.p_hi, NT * b + t + 1)
                dve.tensor_tensor(plo[t % NP][:, :], P[t % NP][:, :], phi[t % NP][:, :].bitcast(F32),
                                  ALU.subtract).then_inc(s.p_lo1, 1)

            def nat_low(b, par):
                dve.wait_ge(s.nat_hi, b + 1)
                dve.tensor_tensor(nlo[par][:, :, :], nat[:, :, :], nhi[par][:, :, :].bitcast(F32),
                                  ALU.subtract).then_inc(s.nat_lo, 1)

            def query_low(b, par):
                dve.wait_ge(s.q_hi, b + 1)
                dve.tensor_tensor(qlo[par][:, :], m.qs[:, bass.ds(b, 1), :, :].rearrange("p o h q -> p (o h q)"),
                                  qhi[par][:, :].bitcast(F32), ALU.subtract).then_inc(s.q_lo, 1)

            def invert(b, par):
                dve.wait_ge(s.den, b + 1)
                dve.reciprocal(inv[:, :], norm_slot(par)[0:QBLK, 0, 0:TT]).then_inc(s.inv, 1)

            def normalise(b, par):
                dve.wait_ge(s.spread, b + 1)
                dve.wait_ge(s.o_raw, b + 1)
                o = m.qs[:, bass.ds(b, 1), :, :].rearrange("p o (a h) q -> p (o a) (h q)", a=2)
                dve.tensor_tensor(o, norm_slot(par)[:, :, 0:HALF], o, ALU.mult).then_inc(s.o_done, 1)

            def body(b, par, nxt, nxt2):
                start = isinstance(b, int) and b == 0
                for t in range(NT):
                    if not first:
                        for tile in ahead(b, par, t, nxt):
                            scale_scores(*tile)
                    if t == 0 and not start:
                        invert(b - 1, par)
                    if t == 1 and not start:
                        normalise(b - 1, par)
                    if POOL_LO:
                        if t % 2:
                            prob_low(b, par, t)
                    elif t < NT - 1:
                        prob_low(b, par, t + 1)
                    elif nxt:
                        prob_low(b + 1, 1 - par, 0)
                    if not first and nxt and t == 4:
                        nat_low(b + 1, 1 - par)
                    if first and nxt:
                        for k in range(STEP_AT[t], STEP_AT[t + 1]):
                            if SIDE[k] != "A":
                                side_job(b + 1, 1 - par, k)
                if not first and nxt2:
                    query_low(b + 2, par)
                if first and nxt:
                    norms_out(b + 1)

            if first:
                for k in range(NSIDE):
                    if SIDE[k] != "A":
                        side_job(0, 0, k)
                norms_out(0)
            else:
                nat_low(0, 0)
                query_low(0, 0)
                query_low(1, 1)
                for t in range(LAG):
                    scale_scores(0, 0, t)
                prob_low(0, 0, 0)
            batches(dve, body)
            invert(B - 1, 0)
            normalise(B - 1, 0)

        @block.tensor
        def _(pe):
            def scores_half(b, par, t, half):
                slot = slot_of(par, t)
                if half == 0:
                    if t == 0:
                        pe.wait_ge(s.ctx_lo, b + 1)
                        pe.wait_ge(s.q_lo, b + 1)
                        if first:
                            pe.wait_ge(*side_done(s, b, SIDE.index("T")))
                    if not first:
                        need(pe, consumed, NT * b + t - 1)
                    elif t < 3:
                        need(pe, consumed, NT * b + (t - 1 if t != 2 else 2))
                    elif t == 3:
                        need(pe, s.o_done, b)
                    else:
                        pe.wait_ge(consumed, NT * b + t - 1)
                keys = slice(KT * t, KT * t + KT)
                cols = slice(HALF * half, HALF * half + HALF)
                out = slots[0:KT, slot, half, 0:HALF]
                pe.matmul(out, clo[par][:, keys], qhi[par][:, cols], start=True, stop=False)
                pe.matmul(out, chi[par][:, keys], qlo[par][:, cols], start=False, stop=False)
                last = pe.matmul(out, chi[par][:, keys], qhi[par][:, cols], start=False, stop=not first)
                if first:
                    last = pe.matmul(out, m.ones8[:, :], shift[par][:, cols], start=False, stop=True)
                if half == 1:
                    last.then_inc(s.scores, 1)

            def values_half(b, par, t, half):
                if half == 0:
                    low_done(pe, b, t)
                    pe.wait_ge(s.p_hi, NT * b + t + 1)
                    if t == 0:
                        pe.wait_ge(s.nat_lo, b + 1)
                        need(pe, s.o_raw, b)
                cols = slice(HALF * half, HALF * half + HALF)
                out = psO[:, half, 0:HALF]
                pe.matmul(out, nlo[par][:, t, :], phi[t % NP][:, cols], start=t == 0, stop=False)
                pe.matmul(out, nhi[par][:, t, :], plo[t % NP][:, cols], start=False, stop=False)
                last = pe.matmul(out, nhi[par][:, t, :], phi[t % NP][:, cols], start=False, stop=t == NT - 1)
                if half == 1:
                    last.then_inc(s.pv, 1)

            def sums(b, par):
                pe.wait_ge(s.acc, (NT - 1) * (b + 1))
                if first:
                    pe.wait_ge(consumed, NT * B if isinstance(b, int) and b == B - 1 else NT * (b + 1) + 1)
                need(pe, s.o_done, b)
                for j in range(QBLK):
                    last = pe.matmul(norm_slot(par)[0:QBLK, 0, 0:TT], m.row_of[0:KT, j, :], acc[:, TT * j:TT * j + TT],
                                     start=j == 0, stop=j == QBLK - 1)
                last.then_inc(s.den, 1)

            def spread(b, par):
                pe.wait_ge(s.inv, b + 1)
                for j in range(QBLK):
                    last = pe.matmul(norm_slot(par)[:, j // 4, TT * (j % 4):TT * (j % 4) + TT], m.pick[:, j, :], inv[:, :],
                                     start=True, stop=True)
                last.then_inc(s.spread, 1)

            def side_job(b, par, k):
                kind, i = SIDE[k], side_number(k)
                bank = side[(k + par) % 2]
                if k == 0:
                    pe.wait_ge(s.ctx_hi, b + 1)
                    pe.wait_ge(s.q_hi, b + 1)
                if k >= 2:
                    pe.wait_ge(*side_done(s, b, k - 2))
                elif not (isinstance(b, int) and b == 0):
                    pe.wait_ge(*side_done(s, b - 1, k - 2 + NSIDE))
                if kind == "M":
                    j, c = i // NMC, i % NMC
                    last = pe.matmul(bank[0:TT, 0:MC], qhi[par][:, TT * j:TT * j + TT], chi[par][:, MC * c:MC * c + MC],
                                     start=True, stop=True)
                elif kind == "T":
                    pe.wait_ge(s.negmax, b + 1)
                    last = pe.transpose(bank[0:QBLK, 0:TT], negmax[:, :], m.ident[0:TT, 0:TT])
                else:
                    t, g = (i // DVE_G, i % DVE_G) if kind == "N" else (i, DVE_G)
                    keys, cols = slice(KT * t, KT * t + KT), slice(512 * g, 512 * g + 512)
                    if kind == "A":
                        if t == 0:
                            pe.wait_ge(s.ctx_lo, b + 1)
                        pe.matmul(bank[0:KT, :], clo[par][:, keys], m.norm_hi[:, cols], start=True, stop=False)
                    pe.matmul(bank[0:KT, :], chi[par][:, keys], m.norm_lo[:, cols], start=kind == "N", stop=False)
                    last = pe.matmul(bank[0:KT, :], chi[par][:, keys], m.norm_hi[:, cols], start=False, stop=True)
                last.then_inc(s.side_pe, 1)

            def body(b, par, nxt, nxt2):
                start = isinstance(b, int) and b == 0
                for t in range(NT):
                    jobs = list(range(STEP_AT[t], STEP_AT[t + 1])) if first and nxt else []

                    def side_jobs(count):
                        for k in jobs[:count]:
                            side_job(b + 1, 1 - par, k)
                        del jobs[:count]

                    for half in range(2):
                        for tile in ahead(b, par, t, nxt):
                            scores_half(*tile, half)
                        if half == 1 and t == 0 and not start:
                            sums(b - 1, par)
                        if half == 1 and t == 1 and not start:
                            spread(b - 1, par)
                        side_jobs(1 + half)
                    values_half(b, par, t, 0)
                    side_jobs(1)
                    values_half(b, par, t, 1)
                    side_jobs(len(jobs))

            if first:
                for k in range(NSIDE):
                    side_job(0, 0, k)
            for t in range(LAG):
                for half in range(2):
                    scores_half(0, 0, t, half)
            batches(pe, body)
            sums(B - 1, 0)
            spread(B - 1, 0)


def between_layers(nc, m, a, tag, sem):
    s1 = semaphores(sem, tag + "1", LN_SEMAPHORES)
    s2 = semaphores(sem, tag + "2", LN_SEMAPHORES)
    s = semaphores(sem, tag, ["ld_x", "ld_wv", "ld_wo", "ld_fac", "ld_bias", "ld_wq", "ld_wk", "ld_g", "ready", "on_act", "on_dve", "fac",
                 "gain", "rk_std", "rk_inv", "q", "sq", "ms", "std", "rinv", "qn", "qf", "q_out", "bias"])
    jobs = [("act", "vo", i) for i in range(8)]
    jobs += [("act", "outT", i) for i in range(4)]
    jobs += [("dve", "out", i) for i in range(4)]
    jobs += [("act", "turn", i) for i in range(4)]
    jobs += [("dve", "ffn", j) for j in range(NTT)]
    jobs += [("act", "turn2", i) for i in range(4)]
    banks = Banks(jobs, {"act": s.on_act, "dve": s.on_dve})
    with ExitStack() as ctx:
        sb = lambda n, sh, dt: ctx.enter_context(nc.sbuf_tensor(f"{tag}_{n}", sh, dt))
        bk = [ctx.enter_context(nc.psum_tensor(f"{tag}_bk{i}", [128, 512], F32)) for i in range(8)]
        wvT = sb("wvT", [HD, G0, C], F32)
        wo = sb("wo", [HD, H, D], F32)
        vo = sb("vo", [C, H, D], F32)
        yT = m.xnT
        fac = sb("fac", [128, KC, RANK, D], F32)
        fsum = sb("fsum", [128, KC, D], F32)
        bias = sb("bias", [TT, D], F32)
        wq = sb("wq", [128, KC, H * HD], F32)
        wkT = sb("wkT", [HD, H, C], F32)
        gains = sb("gains", [HD, 2], F32)
        gain = sb("gain", [HD, 1], F32)
        sq = [sb(f"sq{i}", [HD, HALF], F32) for i in range(2)]
        std = [sb(f"std{i}", [HD, HALF], F32) for i in range(2)]
        qn = [sb(f"qn{i}", [HD, HALF], F32) for i in range(2)]
        block = ctx.enter_context(nc.Block())
        NQ = 2 * H
        first_q = len(jobs)

        @block.sync
        def _(sp):
            sp.dma_start(wvT[:, :, :], a.wvT0).then_inc(s.ld_wv, 16)
            sp.dma_start(m.x[:, :, :], a.x).then_inc(s.ld_x, 16)
            sp.dma_start(wo[:, :, :], a.wo0).then_inc(s.ld_wo, 16)
            sp.dma_start(fac[:, :, :, :], a.factors).then_inc(s.ld_fac, 16)
            sp.dma_start(bias[:, :], a.bias.to_broadcast([TT, D])).then_inc(s.ld_bias, 16)
            sp.dma_start(wq[:, :, :], a.wq1).then_inc(s.ld_wq, 16)
            sp.dma_start(wkT[:, :, :], a.wkT1).then_inc(s.ld_wk, 16)
            sp.dma_start(gains[:, :], a.gains).then_inc(s.ld_g, 16)

        @block.scalar
        def _(act):
            for n, (who, kind, i) in enumerate(jobs):
                if kind == "turn" and i == 0:
                    layer_norm_scalar(act, m, s1)
                    act.activation(m.rk[:, :, :, :], m.rk[:, :, :, :], ACT.Sqrt).then_inc(s.rk_std, 1)
                if kind == "turn2" and i == 0:
                    layer_norm_scalar(act, m, s2)
                if who != "act":
                    continue
                bank = bk[n % 8]
                act.wait_ge(s.ready, n + 1)
                if kind == "vo":
                    act.activation(vo[:, 2 * i:2 * i + 2, :], bank[:, :], ACT.Copy).then_inc(s.on_act, 1)
                elif kind == "outT":
                    act.activation(yT[:, i // 2, HALF * (i % 2):HALF * (i % 2) + HALF], bank[:, 0:HALF],
                                   ACT.Copy).then_inc(s.on_act, 1)
                else:
                    act.activation(m.xnT[:, i // 2, HALF * (i % 2):HALF * (i % 2) + HALF], bank[:, 0:HALF],
                                   ACT.Copy).then_inc(s.on_act, 1)
            for n in range(NQ + 3):
                if n < NQ:
                    act.wait_ge(s.q, n + 1)
                    need(act, s.ms, n - 1)
                    act.activation(sq[n % 2][:, :], bk[n % 4][:, 0:HALF], ACT.Square).then_inc(s.sq, 1)
                if 1 <= n <= NQ:
                    act.wait_ge(s.ms, n)
                    need(act, s.rinv, n - 2)
                    act.activation(std[(n - 1) % 2][:, :], bk[4 + (n - 1) % 2][:, 0:HALF], ACT.Sqrt, bias=m.eps[:, 0:1],
                                   scale=1.0 / HD).then_inc(s.std, 1)
                if n >= 3:
                    k = n - 3
                    act.wait_ge(s.qf, k + 1)
                    act.activation(m.qs[:, 8 * (k % 2):8 * (k % 2) + 8, k // 2, :],
                                   bk[6 + k % 2][:, 0:HALF].rearrange("p (b q) -> p b q", q=QS), ACT.Copy).then_inc(s.q_out, 1)

        @block.vector
        def _(dve):
            dve.wait_ge(s.ld_x, 16)
            dve.wait_ge(s.ld_fac, 16)
            dve.tensor_reduce(fsum[:, :, :], fac[:, :, :, :].rearrange("p k r d -> p k d r"), AX.X, ALU.add).then_inc(s.fac, 1)
            dve.wait_ge(s.ld_g, 16)
            dve.tensor_scalar(gain[:, :], gains[:, 0:1], gains[:, 1:2], SCALE, ALU.mult, ALU.mult).then_inc(s.gain, 1)
            for n, (who, kind, i) in enumerate(jobs):
                bank = bk[n % 8]
                if kind == "turn" and i == 0:
                    dve.wait_ge(s.on_dve, 4)
                    layer_norm_vector(dve, m, s1)
                    dve.wait_ge(s.ld_bias, 16)
                    dve.wait_ge(s1.xn, NTT)
                    dve.tensor_tensor(m.x[:, :, :], m.x[:, :, :], bias[:, :].unsqueeze(1).to_broadcast([TT, NTT, D]),
                                      ALU.add).then_inc(s.bias, 1)
                    dve.wait_ge(s.rk_std, 1)
                    dve.reciprocal(m.rk[:, :, :, :], m.rk[:, :, :, :]).then_inc(s.rk_inv, 1)
                if kind == "turn2" and i == 0:
                    dve.wait_ge(s.on_dve, 4 + NTT)
                    layer_norm_vector(dve, m, s2)
                if who != "dve":
                    continue
                dve.wait_ge(s.ready, n + 1)
                if kind == "out":
                    dve.tensor_tensor(m.x[:, 2 * i:2 * i + 2, :], bank[0:TT, :].rearrange("p (j d) -> p j d", d=D),
                                      m.x[:, 2 * i:2 * i + 2, :], ALU.add).then_inc(s.on_dve, 1)
                else:
                    if i == 0:
                        dve.wait_ge(s.bias, 1)
                    dve.scalar_tensor_tensor(m.x[:, i, :], bank[0:TT, 0:D], float(RANK) ** -0.5, m.x[:, i, :],
                                             ALU.mult, ALU.add).then_inc(s.on_dve, 1)
            dve.wait_ge(s.gain, 1)
            for n in range(NQ):
                dve.wait_ge(s.std, n + 1)
                need(dve, s.qf, n - 1)
                dve.reciprocal(qn[n % 2][:, :], std[n % 2][:, :]).then_inc(s.rinv, 1)
                dve.wait_ge(s.rinv, n + 1)
                dve.scalar_tensor_tensor(qn[n % 2][:, :], bk[n % 4][:, 0:HALF], gain[:, 0:1], qn[n % 2][:, :],
                                         ALU.mult, ALU.mult).then_inc(s.qn, 1)

        @block.tensor
        def _(pe):
            for n, (who, kind, i) in enumerate(jobs):
                bank = bk[n % 8]
                banks.wait_free(pe, n)
                if kind == "vo":
                    if i == 0:
                        pe.wait_ge(s.ld_wv, 16)
                        pe.wait_ge(s.ld_wo, 16)
                    for c in range(2):
                        last = pe.matmul(bank[:, D * c:D * c + D], wvT[:, i, :], wo[:, 2 * i + c, :], start=True, stop=True)
                elif kind == "outT":
                    if i == 0:
                        pe.wait_ge(s.on_act, 8)
                    for h in range(H):
                        last = pe.matmul(bank[:, 0:HALF], vo[:, h, 128 * (i // 2):128 * (i // 2) + 128],
                                         m.qs[:, 8 * (i % 2):8 * (i % 2) + 8, h, :], start=h == 0, stop=h == H - 1)
                elif kind == "out":
                    if i == 0:
                        pe.wait_ge(s.on_act, 12)
                    for c in range(4):
                        j = 2 * i + c // 2
                        last = pe.transpose(bank[0:TT, 128 * c:128 * c + 128], yT[:, c % 2, TT * j:TT * j + TT], m.ident[:, :])
                elif kind in ("turn", "turn2"):
                    if i == 0:
                        pe.wait_ge(s1.xn if kind == "turn" else s2.xn, NTT)
                    for c in range(4):
                        j = 4 * (i % 2) + c
                        last = pe.transpose(bank[:, TT * c:TT * c + TT], m.xn[:, j, 128 * (i // 2):128 * (i // 2) + 128],
                                            m.ident[0:TT, 0:TT])
                else:
                    if i == 0:
                        pe.wait_ge(s.on_act, 16)
                        pe.wait_ge(s.fac, 1)
                    for kc in range(KC):
                        last = pe.matmul(bank[0:TT, 0:D], m.xnT[:, kc, TT * i:TT * i + TT], fsum[:, kc, :],
                                         start=kc == 0, stop=kc == KC - 1)
                last.then_inc(s.ready, 1)
            pe.wait_ge(s.on_act, 20)
            pe.wait_ge(s.on_dve, 4 + NTT)
            pe.wait_ge(s.ld_wq, 16)
            pe.wait_ge(s.ld_wk, 16)
            for n in range(NQ + 3):
                if n < NQ:
                    need(pe, s.qn, n - 3)
                    for kc in range(KC):
                        last = pe.matmul(bk[n % 4][:, 0:HALF], wq[:, kc, HD * (n // 2):HD * (n // 2) + HD],
                                         m.xnT[:, kc, HALF * (n % 2):HALF * (n % 2) + HALF], start=kc == 0, stop=kc == KC - 1)
                    last.then_inc(s.q, 1)
                if 1 <= n <= NQ:
                    pe.wait_ge(s.sq, n)
                    need(pe, s.std, n - 2)
                    pe.matmul(bk[4 + (n - 1) % 2][:, 0:HALF], m.ones[:, :], sq[(n - 1) % 2][:, :],
                              start=True, stop=True).then_inc(s.ms, 1)
                if n >= 3:
                    k = n - 3
                    pe.wait_ge(s.qn, k + 1)
                    need(pe, s.q_out, k - 1)
                    pe.matmul(bk[6 + k % 2][:, 0:HALF], wkT[:, k // 2, :], qn[k % 2][:, :], start=True, stop=True).then_inc(s.qf, 1)


def after_attention(nc, m, a, out, tag, sem):
    s = semaphores(sem, tag, LN_SEMAPHORES + ["ld_wv", "ld_wo", "ld_r", "ready", "on_act", "on_dve", "logit", "exp", "rt", "cw", "st",
                 "ld_e0", "ld_e1", "h1", "h3", "silu", "hid", "y", "add", "cwe", "st_out"])
    jobs = [("act", "vo", i) for i in range(8)]
    jobs += [("act", "outT", i) for i in range(4)]
    jobs += [("dve", "out", i) for i in range(4)]
    jobs += [("act", "turn", i) for i in range(4)]
    jobs += [("dve", "route", 0)]
    banks = Banks(jobs, {"act": s.on_act, "dve": s.on_dve})
    with ExitStack() as ctx:
        sb = lambda n, sh, dt: ctx.enter_context(nc.sbuf_tensor(f"{tag}_{n}", sh, dt))
        bk = [ctx.enter_context(nc.psum_tensor(f"{tag}_bk{i}", [128, 512], F32)) for i in range(8)]
        wvT = sb("wvT", [HD, H, C], F32)
        wo = sb("wo", [HD, H, D], F32)
        vo = sb("vo", [C, H, D], F32)
        yT = m.xnT
        wr = sb("wr", [128, KC, E], F32)
        tri = sb("tri", [TT, E, E], F32)
        lmax = sb("lmax", [TT, NTT], F32)
        lsub = sb("lsub", [TT, NTT, E], F32)
        ex = sb("ex", [TT, NTT, E], F32)
        cmp = sb("cmp", [TT, NTT, E, E], F32)
        rank = [sb(f"rank{i}", [TT, NTT, E], F32) for i in range(2)]
        sel = sb("sel", [TT, NTT, E], F32)
        top = sb("top", [TT, NTT], F32)
        rtop = sb("rtop", [TT, NTT], F32)
        cw = sb("cw", [TT, NTT, NEXP], F32)
        cwe = [sb(f"cwe{i}", [TT, NTT], F32) for i in range(2)]
        we = [sb(f"we{i}", [128, 2 * KC * 128 + D], F32) for i in range(2)]
        silu = [sb(f"silu{i}", [128, HALF], F32) for i in range(2)]
        hid = [sb(f"hid{i}", [128, QW], F32) for i in range(2)]
        block = ctx.enter_context(nc.Block())

        def experts(eng, body):
            body(0, 0)
            body(1, 1)
            with eng.Fori(1, NEXP // 2) as i:
                body(2 * i, 0)
                body(2 * i + 1, 1)

        @block.sync
        def _(sp):
            sp.dma_start(wvT[:, :, :], a.wvT1).then_inc(s.ld_wv, 16)
            sp.dma_start(wo[:, :, :], a.wo1).then_inc(s.ld_wo, 16)
            sp.dma_start(wr[:, :, :], a.w_router).then_inc(s.ld_r, 16)
            sp.dma_start(tri[:, :, :], a.tri.to_broadcast([TT, E, E])).then_inc(s.ld_r, 16)

            def body(e, par):
                need(sp, s.y, 4 * (e - 1))
                sp.dma_start(we[par][:, :], a.experts[bass.ds(e, 1), :, :]).then_inc((s.ld_e0, s.ld_e1)[par], 16)

            experts(sp, body)
            sp.wait_ge(s.add, NTT * NEXP)
            sp.dma_start(out, m.x[:, :, :]).then_inc(s.st_out, 16)
            sp.wait_ge(s.st_out, 16)

        @block.scalar
        def _(act):
            for n, (who, kind, i) in enumerate(jobs):
                if kind == "turn" and i == 0:
                    layer_norm_scalar(act, m, s)
                if who != "act":
                    continue
                bank = bk[n % 8]
                act.wait_ge(s.ready, n + 1)
                if kind == "vo":
                    act.activation(vo[:, 2 * i:2 * i + 2, :], bank[:, :], ACT.Copy).then_inc(s.on_act, 1)
                elif kind == "outT":
                    act.activation(yT[:, i // 2, HALF * (i % 2):HALF * (i % 2) + HALF], bank[:, 0:HALF],
                                   ACT.Copy).then_inc(s.on_act, 1)
                else:
                    act.activation(m.xnT[:, i // 2, HALF * (i % 2):HALF * (i % 2) + HALF], bank[:, 0:HALF],
                                   ACT.Copy).then_inc(s.on_act, 1)
            act.wait_ge(s.logit, 2)
            act.activation(ex[:, :, :], lsub[:, :, :], ACT.Exp).then_inc(s.exp, 1)

            def body(e, par):
                for half in range(2):
                    act.wait_ge(s.h1, 2 * e + half + 1)
                    need(act, s.hid, 2 * e + half - 1)
                    act.activation(silu[half][:, :], bk[half][:, 0:HALF], ACT.Silu).then_inc(s.silu, 1)

            experts(act, body)

        @block.vector
        def _(dve):
            for n, (who, kind, i) in enumerate(jobs):
                bank = bk[n % 8]
                if kind == "turn" and i == 0:
                    dve.wait_ge(s.on_dve, 4)
                    layer_norm_vector(dve, m, s)
                if who != "dve":
                    continue
                dve.wait_ge(s.ready, n + 1)
                if kind == "out":
                    dve.tensor_tensor(m.x[:, 2 * i:2 * i + 2, :], bank[0:TT, :].rearrange("p (j d) -> p j d", d=D),
                                      m.x[:, 2 * i:2 * i + 2, :], ALU.add).then_inc(s.on_dve, 1)
                else:
                    lg = bank[0:TT, 0:NTT * E].rearrange("p (j e) -> p j e", e=E)
                    dve.tensor_reduce(lmax[:, :], lg, AX.X, ALU.max).then_inc(s.logit, 1)
                    dve.wait_ge(s.logit, 1)
                    dve.tensor_tensor(lsub[:, :, :], lg, lmax[:, :].unsqueeze(2).to_broadcast([TT, NTT, E]),
                                      ALU.subtract).then_inc(s.logit, 1)
            dve.wait_ge(s.exp, 1)
            dve.wait_ge(s.ld_r, 32)
            other = ex[:, :, :].unsqueeze(2).to_broadcast([TT, NTT, E, E])
            own = ex[:, :, :].unsqueeze(3).to_broadcast([TT, NTT, E, E])
            dve.tensor_tensor(cmp[:, :, :, :], other, own, ALU.is_gt).then_inc(s.rt, 1)
            dve.wait_ge(s.rt, 1)
            dve.tensor_reduce(rank[0][:, :, :], cmp[:, :, :, :], AX.X, ALU.add).then_inc(s.rt, 1)
            dve.wait_ge(s.rt, 2)
            dve.tensor_tensor(cmp[:, :, :, :], other, own, ALU.is_equal).then_inc(s.rt, 1)
            dve.wait_ge(s.rt, 3)
            dve.tensor_tensor(cmp[:, :, :, :], cmp[:, :, :, :], tri[:, :, :].unsqueeze(1).to_broadcast([TT, NTT, E, E]),
                              ALU.mult).then_inc(s.rt, 1)
            dve.wait_ge(s.rt, 4)
            dve.tensor_reduce(rank[1][:, :, :], cmp[:, :, :, :], AX.X, ALU.add).then_inc(s.rt, 1)
            dve.wait_ge(s.rt, 5)
            dve.tensor_tensor(rank[0][:, :, :], rank[0][:, :, :], rank[1][:, :, :], ALU.add).then_inc(s.rt, 1)
            dve.wait_ge(s.rt, 6)
            dve.scalar_tensor_tensor(sel[:, :, :], rank[0][:, :, :], TOPK - 0.5, ex[:, :, :], ALU.is_lt, ALU.mult).then_inc(s.rt, 1)
            dve.wait_ge(s.rt, 7)
            dve.tensor_reduce(top[:, :], sel[:, :, :], AX.X, ALU.add).then_inc(s.rt, 1)
            dve.wait_ge(s.rt, 8)
            dve.reciprocal(rtop[:, :], top[:, :]).then_inc(s.rt, 1)
            dve.wait_ge(s.rt, 9)
            dve.scalar_tensor_tensor(cw[:, :, 0:E], sel[:, :, :], TOPK / (TOPK + 1.0),
                                     rtop[:, :].unsqueeze(2).to_broadcast([TT, NTT, E]), ALU.mult, ALU.mult).then_inc(s.cw, 1)
            dve.memset(cw[:, :, E:NEXP], 1.0 / (TOPK + 1.0)).then_inc(s.cw, 1)
            dve.wait_ge(s.cw, 2)

            def body(e, par):
                for half in range(2):
                    dve.wait_ge(s.silu, 2 * e + half + 1)
                    dve.wait_ge(s.h3, 2 * e + half + 1)
                    need(dve, s.y, 4 * (e - 1))
                    dve.tensor_tensor(hid[par][:, HALF * half:HALF * half + HALF], bk[2 + half][:, 0:HALF], silu[half][:, :],
                                      ALU.mult).then_inc(s.hid, 1)
                need(dve, s.add, NTT * (e - 1))
                dve.tensor_copy(cwe[par][:, :], cw[:, :, bass.ds(e, 1)].rearrange("p j o -> p (j o)")).then_inc(s.cwe, 1)
                dve.wait_ge(s.cwe, e + 1)
                need(dve, s.add, NTT * e)
                for j in range(NTT):
                    dve.wait_ge(s.y, 4 * e + j // 2 + 1)
                    dve.scalar_tensor_tensor(m.x[:, j, :], bk[4 + j // 2][0:TT, D * (j % 2):D * (j % 2) + D],
                                             cwe[par][:, j:j + 1], m.x[:, j, :], ALU.mult, ALU.add).then_inc(s.add, 1)

            experts(dve, body)

        @block.tensor
        def _(pe):
            for n, (who, kind, i) in enumerate(jobs):
                bank = bk[n % 8]
                banks.wait_free(pe, n)
                if kind == "vo":
                    if i == 0:
                        pe.wait_ge(s.ld_wv, 16)
                        pe.wait_ge(s.ld_wo, 16)
                    for c in range(2):
                        last = pe.matmul(bank[:, D * c:D * c + D], wvT[:, 2 * i + c, :], wo[:, 2 * i + c, :], start=True, stop=True)
                elif kind == "outT":
                    if i == 0:
                        pe.wait_ge(s.on_act, 8)
                    for h in range(H):
                        last = pe.matmul(bank[:, 0:HALF], vo[:, h, 128 * (i // 2):128 * (i // 2) + 128],
                                         m.qs[:, 8 * (i % 2):8 * (i % 2) + 8, h, :], start=h == 0, stop=h == H - 1)
                elif kind == "out":
                    if i == 0:
                        pe.wait_ge(s.on_act, 12)
                    for c in range(4):
                        j = 2 * i + c // 2
                        last = pe.transpose(bank[0:TT, 128 * c:128 * c + 128], yT[:, c % 2, TT * j:TT * j + TT], m.ident[:, :])
                elif kind == "turn":
                    if i == 0:
                        pe.wait_ge(s.xn, NTT)
                    for c in range(4):
                        j = 4 * (i % 2) + c
                        last = pe.transpose(bank[:, TT * c:TT * c + TT], m.xn[:, j, 128 * (i // 2):128 * (i // 2) + 128],
                                            m.ident[0:TT, 0:TT])
                else:
                    pe.wait_ge(s.on_act, 16)
                    pe.wait_ge(s.ld_r, 32)
                    for j in range(NTT):
                        for kc in range(KC):
                            last = pe.matmul(bank[0:TT, E * j:E * j + E], m.xnT[:, kc, TT * j:TT * j + TT], wr[:, kc, :],
                                             start=kc == 0, stop=kc == KC - 1)
                last.then_inc(s.ready, 1)
            pe.wait_ge(s.logit, 2)

            def body(e, par):
                pe.wait_ge((s.ld_e0, s.ld_e1)[par], 16 * (e // 2 + 1))
                w = we[par]
                for half in range(2):
                    need(pe, s.silu, 2 * e + half - 1)
                    for kc in range(KC):
                        last = pe.matmul(bk[half][:, 0:HALF], w[:, 128 * kc:128 * kc + 128],
                                         m.xnT[:, kc, HALF * half:HALF * half + HALF], start=kc == 0, stop=kc == KC - 1)
                    last.then_inc(s.h1, 1)
                    need(pe, s.hid, 2 * e + half - 1)
                    for kc in range(KC):
                        last = pe.matmul(bk[2 + half][:, 0:HALF], w[:, 256 + 128 * kc:384 + 128 * kc],
                                         m.xnT[:, kc, HALF * half:HALF * half + HALF], start=kc == 0, stop=kc == KC - 1)
                    last.then_inc(s.h3, 1)
                for j in range(NTT):
                    if j % 2 == 0:
                        pe.wait_ge(s.hid, 2 * e + (1 if j < 4 else 2))
                        need(pe, s.add, NTT * (e - 1) + j + 2)
                    last = pe.matmul(bk[4 + j // 2][0:TT, D * (j % 2):D * (j % 2) + D], hid[par][:, TT * j:TT * j + TT],
                                     w[:, 512:512 + D], start=True, stop=True)
                    if j % 2 == 1:
                        last.then_inc(s.y, 1)

            experts(pe, body)


def build(nc, a, out):
    with ExitStack() as ctx:
        sb = lambda n, sh, dt: ctx.enter_context(nc.sbuf_tensor(n, sh, dt))
        sem = lambda n: ctx.enter_context(nc.semaphore(n))
        m = Buffers()
        m.qs = sb("qs", [128, B, H, QS], F32)
        m.rk = sb("rk", [KT, B, NT, H], F32)
        m.ident = sb("ident", [128, 128], F32)
        m.ones = sb("ones", [128, 128], F32)
        m.row_of = sb("row_of", [128, QBLK, QBLK], F32)
        m.pick = sb("pick", [QBLK, QBLK, 128], F32)
        m.eps = sb("eps", [128, 1], F32)

        def with_norm_buffers(run, *args):
            with ExitStack() as inner:
                add = lambda n, sh: inner.enter_context(nc.sbuf_tensor(f"{args[0]}_{n}", sh, F32))
                if run is before_attention:
                    m.x = add("x", [TT, NTT, D])
                m.xn, m.xnT = add("xn", [TT, NTT, D]), add("xnT", [128, KC, QW])
                m.stats, m.meanvar = add("stats", [TT, NTT, 6]), add("meanvar", [TT, NTT, 2])
                m.vareps, m.std, m.rstd = add("vareps", [TT, NTT]), add("std", [TT, NTT]), add("rstd", [TT, NTT])
                run(*args[1:])

        with ExitStack() as only:
            for_first = lambda n, sh, dt: only.enter_context(nc.sbuf_tensor(n, sh, dt))
            m.ones8 = for_first("ones8", [QBLK, KT], F32R)
            m.diag = for_first("diag", [QBLK, QW], F32)
            m.mask_bias = for_first("mask_bias", [KT, B, NT], F32)
            m.valid = for_first("valid", [128, B], F32)
            m.norm_hi = for_first("norm_hi", [C, NG * 512], F32R)
            m.norm_lo = for_first("norm_lo", [C, NG * 512], F32R)
            with_norm_buffers(before_attention, "pre", nc, m, a, "pre", sem)
            attention(nc, m, a, "l0", sem, True)
        m.x = sb("x", [TT, NTT, D], F32)
        with_norm_buffers(between_layers, "mid", nc, m, a, "mid", sem)
        attention(nc, m, a, "l1", sem, False)
        with_norm_buffers(after_attention, "post", nc, m, a, out, "post", sem)


def kernel(**inputs):
    import numpy as np
    import concourse.bacc as bacc
    from concourse import mybir as _mybir
    from concourse.bass_utils import run_bass_kernel_spmd as run

    i = {k: np.asarray(v) for k, v in inputs.items()}
    c = np.ascontiguousarray
    ctx = i["ctx_1024"]
    mask = i["mask_BxS2_bf1"].view(np.uint8)
    heads = lambda w, n: c(w.reshape(w.shape[0], n, 128).transpose(2, 1, 0))
    chunks = lambda w: c(w.reshape(2, 128, -1).transpose(1, 0, 2))
    w1 = np.concatenate([i["L1_ffn_we1"], i["L1_ffn_ws1"].reshape(256, 4, 128).transpose(1, 0, 2)])
    w3 = np.concatenate([i["L1_ffn_we3"], i["L1_ffn_ws3"].reshape(256, 4, 128).transpose(1, 0, 2)])
    w2 = np.concatenate([i["L1_ffn_we2"], i["L1_ffn_ws2"].reshape(4, 128, 256)])
    side = lambda w: w.reshape(-1, 2, 128, 128).transpose(0, 2, 1, 3).reshape(-1, 128, 256)
    arrays = {
        "x": c(i["x"].reshape(8, 112, 256).transpose(1, 0, 2)),
        "ctxT": c(ctx.transpose(2, 0, 1)),
        "ctxN": c(ctx.reshape(16, 12, 125, 128).transpose(0, 2, 1, 3)),
        "mask": c(mask),
        "mask_cols": c(mask.reshape(16, 12, 125).transpose(2, 0, 1)),
        "ident": np.eye(128, dtype=np.float32),
        "diag": np.repeat(np.eye(8, dtype=np.float32), 112, axis=1),
        "row_of": c(np.broadcast_to(np.eye(8, dtype=np.float32), (128, 8, 8))),
        "pick": np.repeat(np.eye(8, dtype=np.float32)[:, :, None], 128, axis=2),
        "tri": np.tril(np.ones((16, 16), np.float32), -1).reshape(1, 16, 16),
        "wqT0": heads(i["L0_xattn_Wq"], 16), "wkT0": heads(i["L0_xattn_Wk"], 8), "wvT0": heads(i["L0_xattn_Wv"], 8),
        "wo0": c(i["L0_xattn_Wo"].reshape(16, 128, 256).transpose(1, 0, 2)),
        "factors": c(i["L0_ffn_factors"].reshape(8, 2, 128, 256).transpose(2, 1, 0, 3)),
        "bias": i["L0_ffn_bias"].reshape(1, 256),
        "wq1": chunks(i["L1_xattn_Wq"]), "wkT1": heads(i["L1_xattn_Wk"], 16), "wvT1": heads(i["L1_xattn_Wv"], 16),
        "wk1": c(i["L1_xattn_Wk"][:, 1536:]),
        "wo1": c(i["L1_xattn_Wo"].reshape(16, 128, 256).transpose(1, 0, 2)),
        "gains": c(np.stack([i["L1_xattn_gq"], i["L1_xattn_gk"]], axis=1)),
        "w_router": chunks(i["L1_ffn_w_router"]),
        "experts": c(np.concatenate([side(w1), side(w3), w2], axis=2)),
    }
    nc = bacc.Bacc("TRN2", target_bir_lowering=False, num_devices=1)
    a = namedtuple("Arrays", list(arrays))(*[
        nc.dram_tensor(f"in_{n}", v.shape, _mybir.dt.from_np(v.dtype), kind="ExternalInput").ap()
        for n, v in arrays.items()])
    out = nc.dram_tensor("out_x", (112, 8, 256), F32, kind="ExternalOutput").ap()
    build(nc, a, out)
    r = run(nc, [{f"in_{n}": v for n, v in arrays.items()}], core_ids=[0])
    return r.results[0]["out_x"].transpose(1, 0, 2).reshape(16, 56, 256)
```

```python
from collections import namedtuple
from contextlib import ExitStack

import concourse.bass as bass
from concourse import mybir

F32 = mybir.dt.float32
F32R = mybir.dt.float32r
BF16 = mybir.dt.bfloat16
U8 = mybir.dt.uint8
ALU = mybir.AluOpType
ACT = mybir.ActivationFunctionType
AX = mybir.AxisListType

B, QS, D = 16, 56, 256
S, C = 1500, 128
H, HD, G0 = 16, 128, 8
KT, NT = 125, 12
QW, HALF = H * QS, H * QS // 2
TT, NTT = 112, 8
KC = D // 128
RANK, E, HS = 8, 16, 512
NEXP = E + HS // 128
TOPK = 4
LN_EPS = 1e-5
RMS_EPS = 1e-5
MASKED = 32768.0
SCALE = float(HD) ** -0.5
MC, NMC = 500, 3
QBLK = 8
NG = 4
DVE_G = 3

STEPS = ["MMMMM"] * 2 + ["MMMMMA"] * 2 + ["MMMMNNA", "NNNNNA", "NNNNNAA", "TNNNNNA"] + ["NNNNNA"] * 2 + ["NNNNNAA", "NNNNA"]
SIDE = "".join(STEPS)
NSIDE = len(SIDE)
STEP_AT = [sum(len(x) for x in STEPS[:t]) for t in range(NT + 1)]
SIDE_V = sum(x != "A" for x in SIDE)
SIDE_A = SIDE.count("A")
ORDER = [("S", 0, 0), ("S", 0, 1), ("S", 1, 0), ("S", 1, 1), ("D", 0, 0), ("E", 0, 0), ("E", 0, 1)]
ORDER += [("S", t, half) for t in range(2, NT) for half in range(2)]
assert len(ORDER) % 3 == 0
assert (SIDE.count("M"), SIDE.count("N"), SIDE_A) == (QBLK * NMC, NT * DVE_G, NT)


def need(eng, sem, value):
    if isinstance(value, int) and value <= 0:
        return
    eng.wait_ge(sem, value)


def side_number(k):
    return SIDE[:k].count(SIDE[k])


def side_done(s, batch, k):
    if SIDE[k] == "A":
        return s.side_act, SIDE_A * batch + SIDE[:k + 1].count("A")
    return s.side_dve, SIDE_V * batch + sum(x != "A" for x in SIDE[:k + 1])


def layer_norm_vector(dve, m, s):
    for j in range(NTT):
        dve.bn_stats(m.stats[:, j, :], m.x[:, j, :]).then_inc(s.ln_stats, 1)
    dve.wait_ge(s.ln_stats, NTT)
    for j in range(NTT):
        dve.bn_aggr(m.meanvar[:, j, :], m.stats[:, j, :]).then_inc(s.ln_aggr, 1)
    dve.wait_ge(s.ln_aggr, NTT)
    dve.tensor_scalar(m.vareps[:, :], m.meanvar[:, :, 1], LN_EPS, None, ALU.add).then_inc(s.ln_var, 1)
    dve.wait_ge(s.ln_std, 1)
    dve.reciprocal(m.rstd[:, :], m.std[:, :]).then_inc(s.ln_rstd, 1)
    dve.wait_ge(s.ln_rstd, 1)
    for j in range(NTT):
        dve.tensor_scalar(m.xn[:, j, :], m.x[:, j, :], m.meanvar[:, j, 0:1], m.rstd[:, j:j + 1],
                          ALU.subtract, ALU.mult).then_inc(s.xn, 1)


def layer_norm_scalar(act, m, s):
    act.wait_ge(s.ln_var, 1)
    act.activation(m.std[:, :], m.vareps[:, :], ACT.Sqrt).then_inc(s.ln_std, 1)


LN_SEMAPHORES = ["ln_stats", "ln_aggr", "ln_var", "ln_std", "ln_rstd", "xn"]


def semaphores(sem, tag, names):
    return namedtuple("Semaphores", names)(*[sem(f"{tag}_{n}") for n in names])


class Buffers:
    pass


class Banks:

    def __init__(self, jobs, sems, count=8):
        self.jobs, self.sems, self.count = jobs, sems, count

    def number(self, n):
        return sum(j[0] == self.jobs[n][0] for j in self.jobs[:n + 1])

    def wait_free(self, pe, n):
        if n >= self.count:
            pe.wait_ge(self.sems[self.jobs[n - self.count][0]], self.number(n - self.count))


def before_attention(nc, m, a, tag, sem):
    s = semaphores(sem, tag, LN_SEMAPHORES + ["ld_x", "ld_mask", "ld_const", "ld_w0", "ld_w1", "const", "ready", "on_act", "on_dve", "xnT",
                 "fold", "w_hi", "g_hi", "mcount"])
    jobs = [("act", "fold", i) for i in range(8)]
    jobs += [("dve", "gram", g) for g in range(DVE_G)]
    jobs += [("dve", "valid", 0)]
    jobs += [("act", "turn", i) for i in range(4)]
    jobs += [(("act", "dve")[i % 2], "query", i) for i in range(2 * H)]
    banks = Banks(jobs, {"act": s.on_act, "dve": s.on_dve})
    with ExitStack() as ctx:
        sb = lambda n, sh, dt: ctx.enter_context(nc.sbuf_tensor(f"{tag}_{n}", sh, dt))
        bk = [ctx.enter_context(nc.psum_tensor(f"{tag}_bk{i}", [128, 512], F32)) for i in range(8)]
        wqT = sb("wqT", [HD, H, D], F32)
        wkT0 = sb("wkT0", [HD, G0, C], F32)
        wkT1 = sb("wkT1", [HD, H, C], F32)
        wk1 = sb("wk1", [C, 512], F32)
        fold = sb("fold", [128, H, KC, C], F32)
        msum = sb("msum", [KT, B], F32)
        masku = sb("masku", [KT, B, NT], U8)
        maskf = sb("maskf", [KT, B, NT], F32)
        block = ctx.enter_context(nc.Block())

        @block.sync
        def _(sp):
            sp.dma_start(wqT[:, :, :], a.wqT0).then_inc(s.ld_w0, 16)
            sp.dma_start(wkT0[:, :, :], a.wkT0).then_inc(s.ld_w0, 16)
            sp.dma_start(m.x[:, :, :], a.x).then_inc(s.ld_x, 16)
            sp.dma_start(wkT1[:, :, :], a.wkT1).then_inc(s.ld_w1, 16)
            sp.dma_start(wk1[:, :], a.wk1).then_inc(s.ld_w1, 16)
            sp.dma_start(masku[:, :, :], a.mask_cols).then_inc(s.ld_mask, 16)
            sp.dma_start(m.ident[:, :], a.ident).then_inc(s.ld_const, 16)
            sp.dma_start(m.diag[:, :], a.diag).then_inc(s.ld_const, 16)
            sp.dma_start(m.row_of[:, :, :], a.row_of).then_inc(s.ld_const, 16)
            sp.dma_start(m.pick[:, :, :], a.pick).then_inc(s.ld_const, 16)

        @block.scalar
        def _(act):
            layer_norm_scalar(act, m, s)
            act.wait_ge(s.ld_w1, 32)
            act.activation(m.norm_hi[:, DVE_G * 512:], wk1[:, :], ACT.Copy).then_inc(s.w_hi, 1)
            for n, (who, kind, i) in enumerate(jobs):
                bank = bk[n % 8]
                if kind == "fold":
                    act.wait_ge(s.ready, n + 1)
                    act.activation(fold[:, 2 * i:2 * i + 2, :, :], bank[:, :], ACT.Copy, scale=SCALE).then_inc(s.on_act, 1)
                elif kind == "gram":
                    act.wait_ge(s.ready, n + 1)
                    act.activation(m.norm_hi[:, 512 * i:512 * i + 512], bank[:, :], ACT.Copy).then_inc(s.g_hi, 1)
                elif kind == "turn":
                    act.wait_ge(s.ready, n + 1)
                    act.activation(m.xnT[:, i // 2, HALF * (i % 2):HALF * (i % 2) + HALF], bank[:, 0:HALF],
                                   ACT.Copy).then_inc(s.on_act, 1)
                elif who == "act":
                    act.wait_ge(s.ready, n + 1)
                    h, half = i // 2, i % 2
                    act.activation(m.qs[:, 8 * half:8 * half + 8, h, :],
                                   bank[:, 0:HALF].rearrange("p (b q) -> p b q", q=QS), ACT.Copy).then_inc(s.on_act, 1)

        @block.vector
        def _(dve):
            dve.memset(m.ones[:, :], 1.0).then_inc(s.const, 1)
            dve.memset(m.ones8[:, :].bitcast(F32), 1.0).then_inc(s.const, 1)
            dve.memset(m.eps[:, :], RMS_EPS).then_inc(s.const, 1)
            dve.wait_ge(s.ld_x, 16)
            layer_norm_vector(dve, m, s)
            dve.wait_ge(s.ld_mask, 16)
            dve.tensor_scalar(m.mask_bias[:, :, :], masku[:, :, :], MASKED, -MASKED, ALU.mult, ALU.add).then_inc(s.const, 1)
            dve.tensor_copy(maskf[:, :, :], masku[:, :, :]).then_inc(s.mcount, 1)
            dve.wait_ge(s.mcount, 1)
            dve.tensor_reduce(msum[:, :], maskf[:, :, :], AX.X, ALU.add).then_inc(s.mcount, 1)
            dve.wait_ge(s.w_hi, 1)
            dve.tensor_tensor(m.norm_lo[:, DVE_G * 512:], wk1[:, :], m.norm_hi[:, DVE_G * 512:].bitcast(F32),
                              ALU.subtract).then_inc(s.const, 1)
            for n, (who, kind, i) in enumerate(jobs):
                bank = bk[n % 8]
                if who != "dve":
                    continue
                dve.wait_ge(s.ready, n + 1)
                if kind == "gram":
                    dve.wait_ge(s.g_hi, i + 1)
                    cols = slice(512 * i, 512 * i + 512)
                    dve.tensor_tensor(m.norm_lo[:, cols], bank[:, :], m.norm_hi[:, cols].bitcast(F32),
                                      ALU.subtract).then_inc(s.on_dve, 1)
                elif kind == "valid":
                    dve.tensor_scalar(m.valid[:, :], bank[:, 0:B], 1.0, None, ALU.min).then_inc(s.on_dve, 1)
                else:
                    h, half = i // 2, i % 2
                    dve.tensor_copy(m.qs[:, 8 * half:8 * half + 8, h, :],
                                    bank[:, 0:HALF].rearrange("p (b q) -> p b q", q=QS)).then_inc(s.on_dve, 1)

        @block.tensor
        def _(pe):
            for n, (who, kind, i) in enumerate(jobs):
                bank = bk[n % 8]
                banks.wait_free(pe, n)
                if kind == "fold":
                    if i == 0:
                        pe.wait_ge(s.ld_w0, 32)
                    for c in range(4):
                        h, kc = 2 * i + c // 2, c % 2
                        last = pe.matmul(bank[:, 128 * c:128 * c + 128], wqT[:, h, 128 * kc:128 * kc + 128],
                                         wkT0[:, h // 2, :], start=True, stop=True)
                elif kind == "gram":
                    if i == 0:
                        pe.wait_ge(s.ld_w1, 32)
                    for c in range(4):
                        h = 4 * i + c
                        last = pe.matmul(bank[:, 128 * c:128 * c + 128], wkT1[:, h, :], wkT1[:, h, :],
                                         start=True, stop=True)
                elif kind == "valid":
                    pe.wait_ge(s.mcount, 2)
                    pe.wait_ge(s.const, 1)
                    last = pe.matmul(bank[:, 0:B], m.ones[0:KT, :], msum[:, :], start=True, stop=True)
                elif kind == "turn":
                    if i == 0:
                        pe.wait_ge(s.ld_const, 64)
                        pe.wait_ge(s.xn, NTT)
                    for c in range(4):
                        j = 4 * (i % 2) + c
                        last = pe.transpose(bank[:, TT * c:TT * c + TT], m.xn[:, j, 128 * (i // 2):128 * (i // 2) + 128],
                                            m.ident[0:TT, 0:TT])
                else:
                    if i == 0:
                        pe.wait_ge(s.on_act, 12)
                    h, half = i // 2, i % 2
                    for kc in range(KC):
                        last = pe.matmul(bank[:, 0:HALF], fold[:, h, kc, :], m.xnT[:, kc, HALF * half:HALF * half + HALF],
                                         start=kc == 0, stop=kc == KC - 1)
                last.then_inc(s.ready, 1)


def attention(nc, m, a, tag, sem, first):
    s = semaphores(sem, tag, [
        "ld_land", "ld_nat", "ld_mask", "ctx_hi", "ctx_lo", "q_hi", "q_lo", "nat_hi", "nat_lo", "xq", "mask_row",
        "scores", "scaled", "probs", "p_hi", "p_lo0", "p_lo1", "pv", "acc", "den", "inv", "spread", "o_raw", "o_done",
        "side_pe", "side_dve", "side_act", "negmax", "rk_pre", "dve_passed", "pool_passed",
        "act_passed"])
    LAG = 1 if first else 2
    NP = 2 if first else 3
    PIECES = 2 if first else 1
    POOL_LO = NT // 2 if first else 0
    with ExitStack() as ctx:
        sb = lambda n, sh, dt: ctx.enter_context(nc.sbuf_tensor(f"{tag}_{n}", sh, dt))
        psum = lambda n, sh: ctx.enter_context(nc.psum_tensor(f"{tag}_{n}", sh, F32))
        land = sb("land", [C, S], F32)
        chi = [sb(f"chi{i}", [C, S], F32R) for i in range(2)]
        clo = [sb(f"clo{i}", [C, S], F32R) for i in range(2)]
        nat = sb("nat", [KT, NT, C], F32)
        nhi = [sb(f"nhi{i}", [KT, NT, C], F32R) for i in range(2)]
        nlo = [sb(f"nlo{i}", [KT, NT, C], F32R) for i in range(2)]
        qhi = [sb(f"qhi{i}", [C, QW], F32R) for i in range(2)]
        qlo = [sb(f"qlo{i}", [C, QW], F32R) for i in range(2)]
        P = [sb(f"probs{i}", [KT, QW], F32) for i in range(NP)]
        phi = [sb(f"phi{i}", [KT, QW], F32R) for i in range(NP)]
        plo = [sb(f"plo{i}", [KT, QW], F32R) for i in range(NP)]
        acc = sb("acc", [KT, QW], F32)
        inv = sb("inv", [QBLK, TT], F32)
        if first:
            masku = sb("masku", [TT, S], U8)
            mrow = sb("mrow", [TT, S], BF16)
            mx = sb("mx", [TT, QBLK, NMC], F32)
            negmax = sb("negmax", [TT, QBLK], F32)
            shift = [sb(f"shift{i}", [QBLK, QW], F32R) for i in range(2)]
            msq = sb("msq", [KT, NT, 12], F32)
            msqa = sb("msqa", [KT, NT, 4], F32)
            side = [psum(f"side{i}", [128, 512]) for i in range(3)]
            slots = psum("slots", [128, 3, 512])
        else:
            scaled = [sb(f"scaled{i}", [KT, QW], F32) for i in range(2)]
            norm_banks = psum("norm", [128, 2, 512])
            slots = psum("slots", [128, 2, 2, 512])
        psO = psum("psO", [128, 2, 512])
        block = ctx.enter_context(nc.Block())

        def bank_of(kind, t, half):
            return slots[:, ORDER.index((kind, t, half)) % 3, :]

        def wait_bank(pe, b, kind, t, half):
            at = ORDER.index((kind, t, half)) - 3
            while True:
                if at < 0:
                    b, at = b - 1, at + len(ORDER)
                if isinstance(b, int) and b < 0:
                    return
                kind, t, half = ORDER[at]
                if kind == "S" and isinstance(b, int) and b == B:
                    at -= 3
                    continue
                if kind == "S":
                    return need(pe, s.probs, 2 * (NT * b + t) + half + 1)
                if not (isinstance(b, int) and b == 0):
                    return pe.wait_ge(*((s.inv, b) if kind == "D" else (s.o_done, 2 * b - 1 + half)))
                at -= 3

        def low_done(eng, b, t):
            if POOL_LO:
                eng.wait_ge((s.p_lo0, s.p_lo1)[t % 2], POOL_LO * b + t // 2 + 1)
            else:
                eng.wait_ge(s.p_lo1, NT * b + t + 1)

        def batches(eng, body):
            body(0, 0, True, True)
            body(1, 1, True, True)
            with eng.Fori(1, B // 2 - 1) as i:
                body(2 * i, 0, True, True)
                body(2 * i + 1, 1, True, True)
            body(B - 2, 0, True, False)
            body(B - 1, 1, False, False)

        def ahead(b, par, t, nxt):
            if t + LAG < NT:
                return [(b, par, t + LAG)]
            return [(b + 1, 1 - par, t + LAG - NT)] if nxt else []

        @block.sync
        def _(sp):
            def load_land(b):
                need(sp, s.ctx_lo, b)
                sp.dma_start(land[:, :], a.ctxT[:, bass.ds(b, 1), :]).then_inc(s.ld_land, 16)

            def load_nat(b, par):
                if first:
                    need(sp, s.side_dve, SIDE_V * b)
                else:
                    need(sp, s.nat_lo, b)
                sp.dma_start(nat[:, :, :], a.ctxN[bass.ds(b, 1), :, :, :]).then_inc(s.ld_nat, 16)

            def load_mask(b):
                need(sp, s.mask_row, b)
                sp.dma_start(masku[:, :], a.mask[bass.ds(b, 1), :].to_broadcast([TT, S])).then_inc(s.ld_mask, 16)

            def body(b, par, nxt, nxt2):
                if nxt:
                    load_nat(b + 1, 1 - par)
                if nxt2:
                    load_land(b + 2)
                    if first:
                        load_mask(b + 2)

            load_land(0)
            load_nat(0, 0)
            if first:
                load_mask(0)
            load_land(1)
            if first:
                load_mask(1)
            batches(sp, body)

        @block.scalar
        def _(act):
            def high_parts(b, par):
                act.wait_ge(s.ld_land, 16 * (b + 1))
                need(act, s.scores, PIECES * NT * (b - 1))
                act.activation(chi[par][:, :], land[:, :], ACT.Copy).then_inc(s.ctx_hi, 1)
                act.activation(qhi[par][:, :], m.qs[:, bass.ds(b, 1), :, :].rearrange("p o h q -> p (o h q)"),
                               ACT.Copy).then_inc(s.q_hi, 1)

            def nat_high(b, par):
                act.wait_ge(s.ld_nat, 16 * (b + 1))
                need(act, s.pv, NT * (b - 1))
                act.activation(nhi[par][:, :, :], nat[:, :, :], ACT.Copy).then_inc(s.nat_hi, 1)

            def norms(b, par, k):
                t = side_number(k)
                act.wait_ge(s.side_pe, NSIDE * b + k + 1)
                if t == 0:
                    need(act, s.rk_pre, 2 * b)
                bank = side[k % 3]
                for c in range(4):
                    sq = bank[0:KT, 128 * c:128 * c + 128]
                    last = act.activation(sq, sq, ACT.Square, accum_out=msqa[:, t, c:c + 1])
                last.then_inc(s.side_act, 1)

            def exp(b, par, t):
                need(act, s.pv, NT * b + t + 1 - NP)
                if t >= NP:
                    need(act, s.acc, (NT - 1) * b + max(1, t - NP))
                else:
                    need(act, s.acc, (NT - 1) * b + t + 1 - NP)
                for i in range(PIECES):
                    if first:
                        act.wait_ge(s.scores, 2 * (NT * b + t) + i + 1)
                        act.sem_inc(s.act_passed, 1)
                        bias = m.mask_bias[:, bass.ds(b, 1), t].rearrange("p o -> p o")
                        act.activation(P[t % NP][:, HALF * i:HALF * i + HALF], bank_of("S", t, i)[0:KT, 0:HALF], ACT.Exp,
                                       bias=bias).then_inc(s.probs, 1)
                    else:
                        act.wait_ge(s.scaled, NT * b + t + 1)
                        act.activation(P[t % NP][:, :], scaled[t % 2][:, :], ACT.Exp).then_inc(s.probs, 1)
                act.wait_ge(s.probs, PIECES * (NT * b + t + 1))
                act.activation(phi[t % NP][:, :], P[t % NP][:, :], ACT.Copy).then_inc(s.p_hi, 1)

            def values_out(b):
                act.wait_ge(s.pv, NT * b + NT)
                dst = m.qs[:, bass.ds(b, 1), :, :].rearrange("p o (a h) q -> p (o a) (h q)", a=2)
                if first:
                    act.activation(dst, psO[:, :, 0:HALF], ACT.Copy, scale=m.valid[:, bass.ds(b, 1)]).then_inc(s.o_raw, 1)
                else:
                    act.activation(dst, psO[:, :, 0:HALF], ACT.Copy).then_inc(s.o_raw, 1)

            def body(b, par, nxt, nxt2):
                for t in range(NT):
                    if t == NT - LAG and nxt2:
                        high_parts(b + 2, par)
                    for tile in ahead(b, par, t, nxt):
                        exp(*tile)
                    if nxt and t == 1:
                        nat_high(b + 1, 1 - par)
                    if first and nxt:
                        for k in range(STEP_AT[t], STEP_AT[t + 1]):
                            if SIDE[k] == "A":
                                norms(b + 1, 1 - par, k)
                values_out(b)

            high_parts(0, 0)
            nat_high(0, 0)
            act.wait_ge(s.ctx_lo, 1)
            high_parts(1, 1)
            if first:
                for k in range(NSIDE):
                    if SIDE[k] == "A":
                        norms(0, 0, k)
            for t in range(LAG):
                exp(0, 0, t)
            batches(act, body)

        @block.gpsimd
        def _(pool):
            def low_parts(b, par):
                pool.wait_ge(s.ctx_hi, b + 1)
                pool.tensor_tensor(clo[par][:, :], land[:, :], chi[par][:, :].bitcast(F32), ALU.subtract).then_inc(s.ctx_lo, 1)
                if first:
                    pool.wait_ge(s.q_hi, b + 1)
                    pool.tensor_tensor(qlo[par][:, :], m.qs[:, bass.ds(b, 1), :, :].rearrange("p o h q -> p (o h q)"),
                                       qhi[par][:, :].bitcast(F32), ALU.subtract).then_inc(s.q_lo, 1)

            def nat_low(b, par):
                pool.wait_ge(s.nat_hi, b + 1)
                pool.tensor_tensor(nlo[par][:, :, :], nat[:, :, :], nhi[par][:, :, :].bitcast(F32),
                                   ALU.subtract).then_inc(s.nat_lo, 1)

            def mask_row(b):
                pool.wait_ge(s.ld_mask, 16 * (b + 1))
                if not (isinstance(b, int) and b == 0):
                    q, v = side_done(s, b - 1, SIDE.rindex("M"))
                    pool.wait_ge(q, v)
                pool.sem_inc(s.pool_passed, 1)
                pool.tensor_scalar(mrow[:, :], masku[:, :], MASKED, -MASKED, ALU.mult, ALU.add).then_inc(s.mask_row, 1)

            def prob_low(b, par, t):
                pool.wait_ge(s.p_hi, NT * b + t + 1)
                pool.tensor_tensor(plo[t % NP][:, :], P[t % NP][:, :], phi[t % NP][:, :].bitcast(F32),
                                   ALU.subtract).then_inc(s.p_lo0, 1)

            def add(b, par, t):
                pool.wait_ge(s.probs, PIECES * (NT * b + t + 1))
                if t == 1:
                    need(pool, s.den, b)
                    pool.tensor_tensor(acc[:, :], P[0][:, :], P[1][:, :], ALU.add).then_inc(s.acc, 1)
                else:
                    pool.wait_ge(s.acc, (NT - 1) * b + t - 1)
                    pool.tensor_tensor(acc[:, :], acc[:, :], P[t % NP][:, :], ALU.add).then_inc(s.acc, 1)

            def body(b, par, nxt, nxt2):
                for t in range(NT):
                    if POOL_LO and t % 2 == 0:
                        prob_low(b, par, t)
                    if t > 0:
                        add(b, par, t)
                    if t == 0 and nxt:
                        low_parts(b + 1, 1 - par)
                    if t == 2 and nxt and first:
                        nat_low(b + 1, 1 - par)
                    if t == 8 and first and nxt2:
                        mask_row(b + 2)

            low_parts(0, 0)
            if first:
                nat_low(0, 0)
                mask_row(0)
                mask_row(1)
            batches(pool, body)

        @block.vector
        def _(dve):
            def max_chunk(b, par, k):
                i = side_number(k)
                j, c = i // NMC, i % NMC
                dve.wait_ge(s.side_pe, NSIDE * b + k + 1)
                if i == 0:
                    dve.wait_ge(s.mask_row, b + 1)
                    need(dve, s.negmax, b)
                bank = side[k % 3][0:TT, 0:MC]
                dve.sem_inc(s.dve_passed, 1)
                dve.tensor_tensor_reduce(bank, bank, mrow[:, MC * c:MC * c + MC], 1.0, -3.0e38, ALU.add, ALU.max,
                                         mx[:, j, c:c + 1]).then_inc(s.side_dve, 1)
                if i == QBLK * NMC - 1:
                    q, v = side_done(s, b, k)
                    dve.wait_ge(q, v)
                    dve.tensor_reduce(negmax[:, :], mx[:, :, :], AX.X, ALU.max, negate=True).then_inc(s.negmax, 1)

            def spread_shift(b, par, k):
                dve.wait_ge(s.side_pe, NSIDE * b + k + 1)
                need(dve, s.scores, 2 * NT * (b - 1))
                src = side[k % 3][0:QBLK, 0:TT].unsqueeze(1).to_broadcast([QBLK, QBLK, TT])
                dve.tensor_tensor(shift[par][:, :].rearrange("p (j c) -> p j c", c=TT), src,
                                  m.diag[:, :].rearrange("p (j c) -> p j c", c=TT), ALU.mult).then_inc(s.side_dve, 1)

            def norms(b, par, k):
                i = side_number(k)
                t, g = i // DVE_G, i % DVE_G
                if i == 0:
                    dve.wait_ge(s.nat_lo, b + 1)
                    dve.scalar_tensor_tensor(nat[:, :, :], nat[:, :, :], 2.0, nhi[par][:, :, :].bitcast(F32),
                                             ALU.mult, ALU.subtract).then_inc(s.xq, 1)
                    dve.wait_ge(s.xq, b + 1)
                    need(dve, s.rk_pre, 2 * b)
                dve.wait_ge(s.side_pe, NSIDE * b + k + 1)
                bank = side[k % 3]
                for c in range(4):
                    u = bank[0:KT, 128 * c:128 * c + 128]
                    last = dve.tensor_tensor_reduce(u, u, nat[:, t, :], 1.0, 0.0, ALU.mult, ALU.add,
                                                    msq[:, t, 4 * g + c:4 * g + c + 1])
                last.then_inc(s.side_dve, 1)

            def side_job(b, par, k):
                {"M": max_chunk, "N": norms, "T": spread_shift}[SIDE[k]](b, par, k)

            def norms_out(b):
                dve.wait_ge(s.side_dve, SIDE_V * (b + 1))
                dve.wait_ge(s.side_act, SIDE_A * (b + 1))
                dst = m.rk[:, bass.ds(b, 1), :, :].rearrange("p o t h -> p (o t) h")
                dve.tensor_scalar(dst[:, :, 0:12], msq[:, :, :], 1.0 / HD, RMS_EPS, ALU.mult, ALU.add).then_inc(s.rk_pre, 1)
                dve.tensor_scalar(dst[:, :, 12:16], msqa[:, :, :], 1.0 / HD, RMS_EPS, ALU.mult, ALU.add).then_inc(s.rk_pre, 1)

            def scale_scores(b, par, t):
                dve.wait_ge(s.scores, NT * b + t + 1)
                need(dve, s.probs, NT * b + t - 1)
                src = slots[0:KT, t % 2, :, 0:HALF].rearrange("p a (h q) -> p a h q", q=QS)
                rk = m.rk[:, bass.ds(b, 1), t, :].rearrange("p o (a h) -> p (o a) h", a=2).unsqueeze(3)
                dve.tensor_tensor(scaled[t % 2][:, :].rearrange("p (a h q) -> p a h q", a=2, q=QS), src,
                                  rk.to_broadcast([KT, 2, H // 2, QS]), ALU.mult).then_inc(s.scaled, 1)

            def prob_low(b, par, t):
                dve.wait_ge(s.p_hi, NT * b + t + 1)
                dve.tensor_tensor(plo[t % NP][:, :], P[t % NP][:, :], phi[t % NP][:, :].bitcast(F32),
                                  ALU.subtract).then_inc(s.p_lo1, 1)

            def nat_low(b, par):
                dve.wait_ge(s.nat_hi, b + 1)
                dve.tensor_tensor(nlo[par][:, :, :], nat[:, :, :], nhi[par][:, :, :].bitcast(F32),
                                  ALU.subtract).then_inc(s.nat_lo, 1)

            def query_low(b, par):
                dve.wait_ge(s.q_hi, b + 1)
                dve.tensor_tensor(qlo[par][:, :], m.qs[:, bass.ds(b, 1), :, :].rearrange("p o h q -> p (o h q)"),
                                  qhi[par][:, :].bitcast(F32), ALU.subtract).then_inc(s.q_lo, 1)

            def invert(b):
                dve.wait_ge(s.den, b + 1)
                src = bank_of("D", 0, 0) if first else norm_banks[:, 0, :]
                dve.reciprocal(inv[:, :], src[0:QBLK, 0:TT]).then_inc(s.inv, 1)

            def normalise(b):
                dve.wait_ge(s.o_raw, b + 1)
                o = m.qs[:, bass.ds(b, 1), :, :].rearrange("p o (a h) q -> p (o a) (h q)", a=2)
                if first:
                    for half in range(2):
                        dve.wait_ge(s.spread, 2 * b + half + 1)
                        dve.tensor_tensor(o[:, half, :], bank_of("E", 0, half)[:, 0:HALF], o[:, half, :],
                                          ALU.mult).then_inc(s.o_done, 1)
                else:
                    dve.wait_ge(s.spread, 2 * b + 2)
                    dve.tensor_tensor(o, norm_banks[:, :, 0:HALF], o, ALU.mult).then_inc(s.o_done, 1)

            def body(b, par, nxt, nxt2):
                start = isinstance(b, int) and b == 0
                for t in range(NT):
                    if not first:
                        for tile in ahead(b, par, t, nxt):
                            scale_scores(*tile)
                    if first and t == 0 and nxt:
                        side_job(b + 1, 1 - par, 0)
                    if t == 0 and not start:
                        invert(b - 1)
                    if t == 1 and not start:
                        normalise(b - 1)
                    if not first:
                        if t < NT - 1:
                            prob_low(b, par, t + 1)
                        elif nxt:
                            prob_low(b + 1, 1 - par, 0)
                        if nxt and t == 3:
                            nat_low(b + 1, 1 - par)
                        if nxt and t == 6:
                            query_low(b + 1, 1 - par)
                        continue
                    jobs = [k for k in range(STEP_AT[t], STEP_AT[t + 1]) if SIDE[k] != "A" and k > 0] if nxt else []
                    for k in jobs[:-2]:
                        side_job(b + 1, 1 - par, k)
                    if t % 2 == 0:
                        prob_low(b, par, t + 1)
                    for k in jobs[-2:]:
                        side_job(b + 1, 1 - par, k)
                if first and nxt:
                    norms_out(b + 1)

            if first:
                for k in range(NSIDE):
                    if SIDE[k] != "A":
                        side_job(0, 0, k)
                norms_out(0)
            else:
                nat_low(0, 0)
                query_low(0, 0)
                for t in range(LAG):
                    scale_scores(0, 0, t)
                prob_low(0, 0, 0)
            batches(dve, body)
            invert(B - 1)
            normalise(B - 1)

        @block.tensor
        def _(pe):
            def scores_half(b, par, t, half):
                if half == 0:
                    if t == 0:
                        pe.wait_ge(s.ctx_lo, b + 1)
                        pe.wait_ge(s.q_lo, b + 1)
                        if first:
                            pe.wait_ge(*side_done(s, b, SIDE.index("T")))
                    if not first:
                        need(pe, s.scaled, NT * b + t - 1)
                if first:
                    wait_bank(pe, b, "S", t, half)
                keys = slice(KT * t, KT * t + KT)
                cols = slice(HALF * half, HALF * half + HALF)
                out = (bank_of("S", t, half) if first else slots[:, t % 2, half, :])[0:KT, 0:HALF]
                pe.matmul(out, clo[par][:, keys], qhi[par][:, cols], start=True, stop=False)
                pe.matmul(out, chi[par][:, keys], qlo[par][:, cols], start=False, stop=False)
                last = pe.matmul(out, chi[par][:, keys], qhi[par][:, cols], start=False, stop=not first)
                if first:
                    last = pe.matmul(out, m.ones8[:, :], shift[par][:, cols], start=False, stop=True)
                if first or half == 1:
                    last.then_inc(s.scores, 1)

            def values_half(b, par, t, half):
                if half == 0:
                    low_done(pe, b, t)
                    pe.wait_ge(s.p_hi, NT * b + t + 1)
                    if t == 0:
                        pe.wait_ge(s.nat_lo, b + 1)
                        need(pe, s.o_raw, b)
                cols = slice(HALF * half, HALF * half + HALF)
                out = psO[:, half, 0:HALF]
                pe.matmul(out, nlo[par][:, t, :], phi[t % NP][:, cols], start=t == 0, stop=False)
                pe.matmul(out, nhi[par][:, t, :], plo[t % NP][:, cols], start=False, stop=False)
                last = pe.matmul(out, nhi[par][:, t, :], phi[t % NP][:, cols], start=False, stop=t == NT - 1)
                if half == 1:
                    last.then_inc(s.pv, 1)

            def sums(b):
                pe.wait_ge(s.acc, (NT - 1) * (b + 1))
                if first:
                    wait_bank(pe, b + 1, "D", 0, 0)
                    out = bank_of("D", 0, 0)
                else:
                    need(pe, s.o_done, b)
                    out = norm_banks[:, 0, :]
                for j in range(QBLK):
                    last = pe.matmul(out[0:QBLK, 0:TT], m.row_of[0:KT, j, :], acc[:, TT * j:TT * j + TT],
                                     start=j == 0, stop=j == QBLK - 1)
                last.then_inc(s.den, 1)

            def spread(b):
                pe.wait_ge(s.inv, b + 1)
                for half in range(2):
                    if first:
                        wait_bank(pe, b + 1, "E", 0, half)
                    out = bank_of("E", 0, half) if first else norm_banks[:, half, :]
                    for j in range(4):
                        last = pe.matmul(out[:, TT * j:TT * j + TT], m.pick[:, 4 * half + j, :], inv[:, :],
                                         start=True, stop=True)
                    last.then_inc(s.spread, 1)

            def side_job(b, par, k):
                kind, i = SIDE[k], side_number(k)
                bank = side[k % 3]
                if k == 0:
                    pe.wait_ge(s.ctx_hi, b + 1)
                    pe.wait_ge(s.q_hi, b + 1)
                if k >= 3:
                    pe.wait_ge(*side_done(s, b, k - 3))
                elif not (isinstance(b, int) and b == 0):
                    pe.wait_ge(*side_done(s, b - 1, max(j for j in range(NSIDE) if j % 3 == k)))
                if kind == "M":
                    j, c = i // NMC, i % NMC
                    last = pe.matmul(bank[0:TT, 0:MC], qhi[par][:, TT * j:TT * j + TT], chi[par][:, MC * c:MC * c + MC],
                                     start=True, stop=True)
                elif kind == "T":
                    pe.wait_ge(s.negmax, b + 1)
                    last = pe.transpose(bank[0:QBLK, 0:TT], negmax[:, :], m.ident[0:TT, 0:TT])
                else:
                    t, g = (i // DVE_G, i % DVE_G) if kind == "N" else (i, DVE_G)
                    keys, cols = slice(KT * t, KT * t + KT), slice(512 * g, 512 * g + 512)
                    if kind == "A":
                        if t == 0:
                            pe.wait_ge(s.ctx_lo, b + 1)
                        pe.matmul(bank[0:KT, :], clo[par][:, keys], m.norm_hi[:, cols], start=True, stop=False)
                    pe.matmul(bank[0:KT, :], chi[par][:, keys], m.norm_lo[:, cols], start=kind == "N", stop=False)
                    last = pe.matmul(bank[0:KT, :], chi[par][:, keys], m.norm_hi[:, cols], start=False, stop=True)
                last.then_inc(s.side_pe, 1)

            def body(b, par, nxt, nxt2):
                start = isinstance(b, int) and b == 0
                for t in range(NT):
                    jobs = list(range(STEP_AT[t], STEP_AT[t + 1])) if first and nxt else []

                    def side_jobs(count):
                        for k in jobs[:count]:
                            side_job(b + 1, 1 - par, k)
                        del jobs[:count]

                    if t == 1 and not start:
                        spread(b - 1)
                    for half in range(2):
                        for tile in ahead(b, par, t, nxt):
                            scores_half(*tile, half)
                        if half == 1 and t == 0 and not start:
                            sums(b - 1)
                        side_jobs(len(jobs) // (4 - half))
                    values_half(b, par, t, 0)
                    side_jobs(len(jobs) // 2)
                    values_half(b, par, t, 1)
                    side_jobs(len(jobs))

            if first:
                for k in range(NSIDE):
                    side_job(0, 0, k)
            for t in range(LAG):
                for half in range(2):
                    scores_half(0, 0, t, half)
            batches(pe, body)
            sums(B - 1)
            spread(B - 1)


def between_layers(nc, m, a, tag, sem):
    s1 = semaphores(sem, tag + "1", LN_SEMAPHORES)
    s2 = semaphores(sem, tag + "2", LN_SEMAPHORES)
    s = semaphores(sem, tag, ["ld_x", "ld_wv", "ld_wo", "ld_fac", "ld_bias", "ld_wq", "ld_wk", "ld_g", "ready", "on_act", "on_dve", "fac",
                 "gain", "rk_std", "rk_inv", "q", "sq", "ms", "std", "rinv", "qn", "qf", "q_out", "bias"])
    jobs = [("act", "vo", i) for i in range(8)]
    jobs += [("act", "outT", i) for i in range(4)]
    jobs += [("dve", "out", i) for i in range(4)]
    jobs += [("act", "turn", i) for i in range(4)]
    jobs += [("dve", "ffn", j) for j in range(NTT)]
    jobs += [("act", "turn2", i) for i in range(4)]
    banks = Banks(jobs, {"act": s.on_act, "dve": s.on_dve})
    with ExitStack() as ctx:
        sb = lambda n, sh, dt: ctx.enter_context(nc.sbuf_tensor(f"{tag}_{n}", sh, dt))
        bk = [ctx.enter_context(nc.psum_tensor(f"{tag}_bk{i}", [128, 512], F32)) for i in range(8)]
        wvT = sb("wvT", [HD, G0, C], F32)
        wo = sb("wo", [HD, H, D], F32)
        vo = sb("vo", [C, H, D], F32)
        yT = m.xnT
        fac = sb("fac", [128, KC, RANK, D], F32)
        fsum = sb("fsum", [128, KC, D], F32)
        bias = sb("bias", [TT, D], F32)
        wq = sb("wq", [128, KC, H * HD], F32)
        wkT = sb("wkT", [HD, H, C], F32)
        gains = sb("gains", [HD, 2], F32)
        gain = sb("gain", [HD, 1], F32)
        sq = [sb(f"sq{i}", [HD, HALF], F32) for i in range(2)]
        std = [sb(f"std{i}", [HD, HALF], F32) for i in range(2)]
        qn = [sb(f"qn{i}", [HD, HALF], F32) for i in range(2)]
        block = ctx.enter_context(nc.Block())
        NQ = 2 * H
        first_q = len(jobs)

        @block.sync
        def _(sp):
            sp.dma_start(wvT[:, :, :], a.wvT0).then_inc(s.ld_wv, 16)
            sp.dma_start(m.x[:, :, :], a.x).then_inc(s.ld_x, 16)
            sp.dma_start(wo[:, :, :], a.wo0).then_inc(s.ld_wo, 16)
            sp.dma_start(fac[:, :, :, :], a.factors).then_inc(s.ld_fac, 16)
            sp.dma_start(bias[:, :], a.bias.to_broadcast([TT, D])).then_inc(s.ld_bias, 16)
            sp.dma_start(wq[:, :, :], a.wq1).then_inc(s.ld_wq, 16)
            sp.dma_start(wkT[:, :, :], a.wkT1).then_inc(s.ld_wk, 16)
            sp.dma_start(gains[:, :], a.gains).then_inc(s.ld_g, 16)

        @block.scalar
        def _(act):
            for n, (who, kind, i) in enumerate(jobs):
                if kind == "turn" and i == 0:
                    layer_norm_scalar(act, m, s1)
                    act.activation(m.rk[:, :, :, :], m.rk[:, :, :, :], ACT.Sqrt).then_inc(s.rk_std, 1)
                if kind == "turn2" and i == 0:
                    layer_norm_scalar(act, m, s2)
                if who != "act":
                    continue
                bank = bk[n % 8]
                act.wait_ge(s.ready, n + 1)
                if kind == "vo":
                    act.activation(vo[:, 2 * i:2 * i + 2, :], bank[:, :], ACT.Copy).then_inc(s.on_act, 1)
                elif kind == "outT":
                    act.activation(yT[:, i // 2, HALF * (i % 2):HALF * (i % 2) + HALF], bank[:, 0:HALF],
                                   ACT.Copy).then_inc(s.on_act, 1)
                else:
                    act.activation(m.xnT[:, i // 2, HALF * (i % 2):HALF * (i % 2) + HALF], bank[:, 0:HALF],
                                   ACT.Copy).then_inc(s.on_act, 1)
            for n in range(NQ + 3):
                if n < NQ:
                    act.wait_ge(s.q, n + 1)
                    need(act, s.ms, n - 1)
                    act.activation(sq[n % 2][:, :], bk[n % 4][:, 0:HALF], ACT.Square).then_inc(s.sq, 1)
                if 1 <= n <= NQ:
                    act.wait_ge(s.ms, n)
                    need(act, s.rinv, n - 2)
                    act.activation(std[(n - 1) % 2][:, :], bk[4 + (n - 1) % 2][:, 0:HALF], ACT.Sqrt, bias=m.eps[:, 0:1],
                                   scale=1.0 / HD).then_inc(s.std, 1)
                if n >= 3:
                    k = n - 3
                    act.wait_ge(s.qf, k + 1)
                    act.activation(m.qs[:, 8 * (k % 2):8 * (k % 2) + 8, k // 2, :],
                                   bk[6 + k % 2][:, 0:HALF].rearrange("p (b q) -> p b q", q=QS), ACT.Copy).then_inc(s.q_out, 1)

        @block.vector
        def _(dve):
            dve.wait_ge(s.ld_x, 16)
            dve.wait_ge(s.ld_fac, 16)
            dve.tensor_reduce(fsum[:, :, :], fac[:, :, :, :].rearrange("p k r d -> p k d r"), AX.X, ALU.add).then_inc(s.fac, 1)
            dve.wait_ge(s.ld_g, 16)
            dve.tensor_scalar(gain[:, :], gains[:, 0:1], gains[:, 1:2], SCALE, ALU.mult, ALU.mult).then_inc(s.gain, 1)
            for n, (who, kind, i) in enumerate(jobs):
                bank = bk[n % 8]
                if kind == "turn" and i == 0:
                    dve.wait_ge(s.on_dve, 4)
                    layer_norm_vector(dve, m, s1)
                    dve.wait_ge(s.ld_bias, 16)
                    dve.wait_ge(s1.xn, NTT)
                    dve.tensor_tensor(m.x[:, :, :], m.x[:, :, :], bias[:, :].unsqueeze(1).to_broadcast([TT, NTT, D]),
                                      ALU.add).then_inc(s.bias, 1)
                    dve.wait_ge(s.rk_std, 1)
                    dve.reciprocal(m.rk[:, :, :, :], m.rk[:, :, :, :]).then_inc(s.rk_inv, 1)
                if kind == "turn2" and i == 0:
                    dve.wait_ge(s.on_dve, 4 + NTT)
                    layer_norm_vector(dve, m, s2)
                if who != "dve":
                    continue
                dve.wait_ge(s.ready, n + 1)
                if kind == "out":
                    dve.tensor_tensor(m.x[:, 2 * i:2 * i + 2, :], bank[0:TT, :].rearrange("p (j d) -> p j d", d=D),
                                      m.x[:, 2 * i:2 * i + 2, :], ALU.add).then_inc(s.on_dve, 1)
                else:
                    if i == 0:
                        dve.wait_ge(s.bias, 1)
                    dve.scalar_tensor_tensor(m.x[:, i, :], bank[0:TT, 0:D], float(RANK) ** -0.5, m.x[:, i, :],
                                             ALU.mult, ALU.add).then_inc(s.on_dve, 1)
            dve.wait_ge(s.gain, 1)
            for n in range(NQ):
                dve.wait_ge(s.std, n + 1)
                need(dve, s.qf, n - 1)
                dve.reciprocal(qn[n % 2][:, :], std[n % 2][:, :]).then_inc(s.rinv, 1)
                dve.wait_ge(s.rinv, n + 1)
                dve.scalar_tensor_tensor(qn[n % 2][:, :], bk[n % 4][:, 0:HALF], gain[:, 0:1], qn[n % 2][:, :],
                                         ALU.mult, ALU.mult).then_inc(s.qn, 1)

        @block.tensor
        def _(pe):
            for n, (who, kind, i) in enumerate(jobs):
                bank = bk[n % 8]
                banks.wait_free(pe, n)
                if kind == "vo":
                    if i == 0:
                        pe.wait_ge(s.ld_wv, 16)
                        pe.wait_ge(s.ld_wo, 16)
                    for c in range(2):
                        last = pe.matmul(bank[:, D * c:D * c + D], wvT[:, i, :], wo[:, 2 * i + c, :], start=True, stop=True)
                elif kind == "outT":
                    if i == 0:
                        pe.wait_ge(s.on_act, 8)
                    for h in range(H):
                        last = pe.matmul(bank[:, 0:HALF], vo[:, h, 128 * (i // 2):128 * (i // 2) + 128],
                                         m.qs[:, 8 * (i % 2):8 * (i % 2) + 8, h, :], start=h == 0, stop=h == H - 1)
                elif kind == "out":
                    if i == 0:
                        pe.wait_ge(s.on_act, 12)
                    for c in range(4):
                        j = 2 * i + c // 2
                        last = pe.transpose(bank[0:TT, 128 * c:128 * c + 128], yT[:, c % 2, TT * j:TT * j + TT], m.ident[:, :])
                elif kind in ("turn", "turn2"):
                    if i == 0:
                        pe.wait_ge(s1.xn if kind == "turn" else s2.xn, NTT)
                    for c in range(4):
                        j = 4 * (i % 2) + c
                        last = pe.transpose(bank[:, TT * c:TT * c + TT], m.xn[:, j, 128 * (i // 2):128 * (i // 2) + 128],
                                            m.ident[0:TT, 0:TT])
                else:
                    if i == 0:
                        pe.wait_ge(s.on_act, 16)
                        pe.wait_ge(s.fac, 1)
                    for kc in range(KC):
                        last = pe.matmul(bank[0:TT, 0:D], m.xnT[:, kc, TT * i:TT * i + TT], fsum[:, kc, :],
                                         start=kc == 0, stop=kc == KC - 1)
                last.then_inc(s.ready, 1)
            pe.wait_ge(s.on_act, 20)
            pe.wait_ge(s.on_dve, 4 + NTT)
            pe.wait_ge(s.ld_wq, 16)
            pe.wait_ge(s.ld_wk, 16)
            for n in range(NQ + 3):
                if n < NQ:
                    need(pe, s.qn, n - 3)
                    for kc in range(KC):
                        last = pe.matmul(bk[n % 4][:, 0:HALF], wq[:, kc, HD * (n // 2):HD * (n // 2) + HD],
                                         m.xnT[:, kc, HALF * (n % 2):HALF * (n % 2) + HALF], start=kc == 0, stop=kc == KC - 1)
                    last.then_inc(s.q, 1)
                if 1 <= n <= NQ:
                    pe.wait_ge(s.sq, n)
                    need(pe, s.std, n - 2)
                    pe.matmul(bk[4 + (n - 1) % 2][:, 0:HALF], m.ones[:, :], sq[(n - 1) % 2][:, :],
                              start=True, stop=True).then_inc(s.ms, 1)
                if n >= 3:
                    k = n - 3
                    pe.wait_ge(s.qn, k + 1)
                    need(pe, s.q_out, k - 1)
                    pe.matmul(bk[6 + k % 2][:, 0:HALF], wkT[:, k // 2, :], qn[k % 2][:, :], start=True, stop=True).then_inc(s.qf, 1)


def after_attention(nc, m, a, out, tag, sem):
    s = semaphores(sem, tag, LN_SEMAPHORES + ["ld_wv", "ld_wo", "ld_r", "ready", "on_act", "on_dve", "logit", "exp", "rt", "cw", "st",
                 "ld_e0", "ld_e1", "h1", "h3", "silu", "hid", "y", "add", "cwe", "st_out",
                 "x_hi", "x_lo", "w_hi", "w_lo", "h_hi", "h_lo"])
    jobs = [("act", "vo", i) for i in range(8)]
    jobs += [("act", "outT", i) for i in range(4)]
    jobs += [("dve", "out", i) for i in range(4)]
    jobs += [("act", "turn", i) for i in range(4)]
    jobs += [("dve", "route", 0)]
    banks = Banks(jobs, {"act": s.on_act, "dve": s.on_dve})
    with ExitStack() as ctx:
        sb = lambda n, sh, dt: ctx.enter_context(nc.sbuf_tensor(f"{tag}_{n}", sh, dt))
        bk = [ctx.enter_context(nc.psum_tensor(f"{tag}_bk{i}", [128, 512], F32)) for i in range(8)]
        wvT = sb("wvT", [HD, H, C], F32)
        wo = sb("wo", [HD, H, D], F32)
        vo = sb("vo", [C, H, D], F32)
        yT = m.xnT
        wr = sb("wr", [128, KC, E], F32)
        tri = sb("tri", [TT, E, E], F32)
        lmax = sb("lmax", [TT, NTT], F32)
        lsub = sb("lsub", [TT, NTT, E], F32)
        ex = sb("ex", [TT, NTT, E], F32)
        cmp = sb("cmp", [TT, NTT, E, E], F32)
        rank = [sb(f"rank{i}", [TT, NTT, E], F32) for i in range(2)]
        sel = sb("sel", [TT, NTT, E], F32)
        top = sb("top", [TT, NTT], F32)
        rtop = sb("rtop", [TT, NTT], F32)
        cw = sb("cw", [TT, NTT, NEXP], F32)
        cwe = [sb(f"cwe{i}", [TT, NTT], F32) for i in range(2)]
        we = [sb(f"we{i}", [128, 2 * KC * 128 + D], F32) for i in range(2)]
        silu = [sb(f"silu{i}", [128, HALF], F32) for i in range(2)]
        hid = [sb(f"hid{i}", [128, QW], F32) for i in range(2)]
        xhi, xlo = sb("xhi", [128, KC, QW], F32R), sb("xlo", [128, KC, QW], F32R)
        whi = [sb(f"whi{i}", [128, 2 * KC * 128 + D], F32R) for i in range(2)]
        wlo = [sb(f"wlo{i}", [128, 2 * KC * 128 + D], F32R) for i in range(2)]
        hhi = [sb(f"hhi{i}", [128, QW], F32R) for i in range(2)]
        hlo = [sb(f"hlo{i}", [128, QW], F32R) for i in range(2)]
        block = ctx.enter_context(nc.Block())

        def experts(eng, body):
            body(0, 0, True)
            body(1, 1, True)
            with eng.Fori(1, NEXP // 2 - 1) as i:
                body(2 * i, 0, True)
                body(2 * i + 1, 1, True)
            body(NEXP - 2, 0, True)
            body(NEXP - 1, 1, False)

        @block.sync
        def _(sp):
            sp.dma_start(wvT[:, :, :], a.wvT1).then_inc(s.ld_wv, 16)
            sp.dma_start(wo[:, :, :], a.wo1).then_inc(s.ld_wo, 16)
            sp.dma_start(wr[:, :, :], a.w_router).then_inc(s.ld_r, 16)
            sp.dma_start(tri[:, :, :], a.tri.to_broadcast([TT, E, E])).then_inc(s.ld_r, 16)

            def body(e, par, more):
                need(sp, s.w_lo, e - 1)
                sp.dma_start(we[par][:, :], a.experts[bass.ds(e, 1), :, :]).then_inc((s.ld_e0, s.ld_e1)[par], 16)

            experts(sp, body)
            sp.wait_ge(s.add, NTT * NEXP)
            sp.dma_start(out, m.x[:, :, :]).then_inc(s.st_out, 16)
            sp.wait_ge(s.st_out, 16)

        @block.scalar
        def _(act):
            for n, (who, kind, i) in enumerate(jobs):
                if kind == "turn" and i == 0:
                    layer_norm_scalar(act, m, s)
                if who != "act":
                    continue
                bank = bk[n % 8]
                act.wait_ge(s.ready, n + 1)
                if kind == "vo":
                    act.activation(vo[:, 2 * i:2 * i + 2, :], bank[:, :], ACT.Copy).then_inc(s.on_act, 1)
                elif kind == "outT":
                    act.activation(yT[:, i // 2, HALF * (i % 2):HALF * (i % 2) + HALF], bank[:, 0:HALF],
                                   ACT.Copy).then_inc(s.on_act, 1)
                else:
                    act.activation(m.xnT[:, i // 2, HALF * (i % 2):HALF * (i % 2) + HALF], bank[:, 0:HALF],
                                   ACT.Copy).then_inc(s.on_act, 1)
            act.wait_ge(s.logit, 2)
            act.activation(ex[:, :, :], lsub[:, :, :], ACT.Exp).then_inc(s.exp, 1)
            act.wait_ge(s.on_act, 16)
            act.activation(xhi[:, :, :], m.xnT[:, :, :], ACT.Copy).then_inc(s.x_hi, 1)

            def weights_high(e, par):
                act.wait_ge((s.ld_e0, s.ld_e1)[par], 16 * (e // 2 + 1))
                need(act, s.y, 4 * (e - 1))
                act.activation(whi[par][:, :], we[par][:, :], ACT.Copy).then_inc(s.w_hi, 1)

            weights_high(0, 0)

            def body(e, par, more):
                if more:
                    weights_high(e + 1, 1 - par)
                for half in range(2):
                    act.wait_ge(s.h1, 2 * e + half + 1)
                    need(act, s.hid, 2 * e + half - 1)
                    act.activation(silu[half][:, :], bk[half][:, 0:HALF], ACT.Silu).then_inc(s.silu, 1)
                    cols = slice(HALF * half, HALF * half + HALF)
                    need(act, s.y, 4 * (e - 1))
                    act.wait_ge(s.hid, 2 * e + half + 1)
                    act.activation(hhi[par][:, cols], hid[par][:, cols], ACT.Copy).then_inc(s.h_hi, 1)

            experts(act, body)

        @block.gpsimd
        def _(pool):
            pool.wait_ge(s.x_hi, 1)
            pool.tensor_tensor(xlo[:, :, :], m.xnT[:, :, :], xhi[:, :, :].bitcast(F32), ALU.subtract).then_inc(s.x_lo, 1)

            def body(e, par, more):
                need(pool, s.y, 4 * (e - 1))
                pool.wait_ge(s.w_hi, e + 1)
                pool.tensor_tensor(wlo[par][:, :], we[par][:, :], whi[par][:, :].bitcast(F32), ALU.subtract).then_inc(s.w_lo, 1)

            experts(pool, body)

        @block.vector
        def _(dve):
            for n, (who, kind, i) in enumerate(jobs):
                bank = bk[n % 8]
                if kind == "turn" and i == 0:
                    dve.wait_ge(s.on_dve, 4)
                    layer_norm_vector(dve, m, s)
                if who != "dve":
                    continue
                dve.wait_ge(s.ready, n + 1)
                if kind == "out":
                    dve.tensor_tensor(m.x[:, 2 * i:2 * i + 2, :], bank[0:TT, :].rearrange("p (j d) -> p j d", d=D),
                                      m.x[:, 2 * i:2 * i + 2, :], ALU.add).then_inc(s.on_dve, 1)
                else:
                    lg = bank[0:TT, 0:NTT * E].rearrange("p (j e) -> p j e", e=E)
                    dve.tensor_reduce(lmax[:, :], lg, AX.X, ALU.max).then_inc(s.logit, 1)
                    dve.wait_ge(s.logit, 1)
                    dve.tensor_tensor(lsub[:, :, :], lg, lmax[:, :].unsqueeze(2).to_broadcast([TT, NTT, E]),
                                      ALU.subtract).then_inc(s.logit, 1)
            dve.wait_ge(s.exp, 1)
            dve.wait_ge(s.ld_r, 32)
            other = ex[:, :, :].unsqueeze(2).to_broadcast([TT, NTT, E, E])
            own = ex[:, :, :].unsqueeze(3).to_broadcast([TT, NTT, E, E])
            dve.tensor_tensor(cmp[:, :, :, :], other, own, ALU.is_gt).then_inc(s.rt, 1)
            dve.wait_ge(s.rt, 1)
            dve.tensor_reduce(rank[0][:, :, :], cmp[:, :, :, :], AX.X, ALU.add).then_inc(s.rt, 1)
            dve.wait_ge(s.rt, 2)
            dve.tensor_tensor(cmp[:, :, :, :], other, own, ALU.is_equal).then_inc(s.rt, 1)
            dve.wait_ge(s.rt, 3)
            dve.tensor_tensor(cmp[:, :, :, :], cmp[:, :, :, :], tri[:, :, :].unsqueeze(1).to_broadcast([TT, NTT, E, E]),
                              ALU.mult).then_inc(s.rt, 1)
            dve.wait_ge(s.rt, 4)
            dve.tensor_reduce(rank[1][:, :, :], cmp[:, :, :, :], AX.X, ALU.add).then_inc(s.rt, 1)
            dve.wait_ge(s.rt, 5)
            dve.tensor_tensor(rank[0][:, :, :], rank[0][:, :, :], rank[1][:, :, :], ALU.add).then_inc(s.rt, 1)
            dve.wait_ge(s.rt, 6)
            dve.scalar_tensor_tensor(sel[:, :, :], rank[0][:, :, :], TOPK - 0.5, ex[:, :, :], ALU.is_lt, ALU.mult).then_inc(s.rt, 1)
            dve.wait_ge(s.rt, 7)
            dve.tensor_reduce(top[:, :], sel[:, :, :], AX.X, ALU.add).then_inc(s.rt, 1)
            dve.wait_ge(s.rt, 8)
            dve.reciprocal(rtop[:, :], top[:, :]).then_inc(s.rt, 1)
            dve.wait_ge(s.rt, 9)
            dve.scalar_tensor_tensor(cw[:, :, 0:E], sel[:, :, :], TOPK / (TOPK + 1.0),
                                     rtop[:, :].unsqueeze(2).to_broadcast([TT, NTT, E]), ALU.mult, ALU.mult).then_inc(s.cw, 1)
            dve.memset(cw[:, :, E:NEXP], 1.0 / (TOPK + 1.0)).then_inc(s.cw, 1)
            dve.wait_ge(s.cw, 2)

            def body(e, par, more):
                for half in range(2):
                    dve.wait_ge(s.silu, 2 * e + half + 1)
                    dve.wait_ge(s.h3, 2 * e + half + 1)
                    need(dve, s.h_lo, 2 * (e - 1))
                    dve.tensor_tensor(hid[par][:, HALF * half:HALF * half + HALF], bk[2 + half][:, 0:HALF], silu[half][:, :],
                                      ALU.mult).then_inc(s.hid, 1)
                    cols = slice(HALF * half, HALF * half + HALF)
                    need(dve, s.y, 4 * (e - 1))
                    dve.wait_ge(s.h_hi, 2 * e + half + 1)
                    dve.tensor_tensor(hlo[par][:, cols], hid[par][:, cols], hhi[par][:, cols].bitcast(F32),
                                      ALU.subtract).then_inc(s.h_lo, 1)
                need(dve, s.add, NTT * (e - 1))
                dve.tensor_copy(cwe[par][:, :], cw[:, :, bass.ds(e, 1)].rearrange("p j o -> p (j o)")).then_inc(s.cwe, 1)
                dve.wait_ge(s.cwe, e + 1)
                need(dve, s.add, NTT * e)
                for j in range(NTT):
                    dve.wait_ge(s.y, 4 * e + j // 2 + 1)
                    dve.scalar_tensor_tensor(m.x[:, j, :], bk[4 + j // 2][0:TT, D * (j % 2):D * (j % 2) + D],
                                             cwe[par][:, j:j + 1], m.x[:, j, :], ALU.mult, ALU.add).then_inc(s.add, 1)

            experts(dve, body)

        @block.tensor
        def _(pe):
            for n, (who, kind, i) in enumerate(jobs):
                bank = bk[n % 8]
                banks.wait_free(pe, n)
                if kind == "vo":
                    if i == 0:
                        pe.wait_ge(s.ld_wv, 16)
                        pe.wait_ge(s.ld_wo, 16)
                    for c in range(2):
                        last = pe.matmul(bank[:, D * c:D * c + D], wvT[:, 2 * i + c, :], wo[:, 2 * i + c, :], start=True, stop=True)
                elif kind == "outT":
                    if i == 0:
                        pe.wait_ge(s.on_act, 8)
                    for h in range(H):
                        last = pe.matmul(bank[:, 0:HALF], vo[:, h, 128 * (i // 2):128 * (i // 2) + 128],
                                         m.qs[:, 8 * (i % 2):8 * (i % 2) + 8, h, :], start=h == 0, stop=h == H - 1)
                elif kind == "out":
                    if i == 0:
                        pe.wait_ge(s.on_act, 12)
                    for c in range(4):
                        j = 2 * i + c // 2
                        last = pe.transpose(bank[0:TT, 128 * c:128 * c + 128], yT[:, c % 2, TT * j:TT * j + TT], m.ident[:, :])
                elif kind == "turn":
                    if i == 0:
                        pe.wait_ge(s.xn, NTT)
                    for c in range(4):
                        j = 4 * (i % 2) + c
                        last = pe.transpose(bank[:, TT * c:TT * c + TT], m.xn[:, j, 128 * (i // 2):128 * (i // 2) + 128],
                                            m.ident[0:TT, 0:TT])
                else:
                    pe.wait_ge(s.on_act, 16)
                    pe.wait_ge(s.ld_r, 32)
                    for j in range(NTT):
                        for kc in range(KC):
                            last = pe.matmul(bank[0:TT, E * j:E * j + E], m.xnT[:, kc, TT * j:TT * j + TT], wr[:, kc, :],
                                             start=kc == 0, stop=kc == KC - 1)
                last.then_inc(s.ready, 1)
            pe.wait_ge(s.logit, 2)
            pe.wait_ge(s.x_lo, 1)

            def body(e, par, more):
                pe.wait_ge(s.w_lo, e + 1)
                for half in range(2):
                    tokens = slice(HALF * half, HALF * half + HALF)
                    for which, bank, made, free in ((0, bk[half], s.h1, s.silu), (1, bk[2 + half], s.h3, s.hid)):
                        need(pe, free, 2 * e + half - 1)
                        for kc in range(KC):
                            rows = slice(256 * which + 128 * kc, 256 * which + 128 * kc + 128)
                            pe.matmul(bank[:, 0:HALF], wlo[par][:, rows], xhi[:, kc, tokens], start=kc == 0, stop=False)
                            pe.matmul(bank[:, 0:HALF], whi[par][:, rows], xlo[:, kc, tokens], start=False, stop=False)
                            last = pe.matmul(bank[:, 0:HALF], whi[par][:, rows], xhi[:, kc, tokens],
                                             start=False, stop=kc == KC - 1)
                        last.then_inc(made, 1)
                for j in range(NTT):
                    if j % 2 == 0:
                        pe.wait_ge(s.h_lo, 2 * e + (1 if j < 4 else 2))
                        need(pe, s.add, NTT * (e - 1) + j + 2)
                    y = bk[4 + j // 2][0:TT, D * (j % 2):D * (j % 2) + D]
                    tokens = slice(TT * j, TT * j + TT)
                    pe.matmul(y, hlo[par][:, tokens], whi[par][:, 512:512 + D], start=True, stop=False)
                    pe.matmul(y, hhi[par][:, tokens], wlo[par][:, 512:512 + D], start=False, stop=False)
                    last = pe.matmul(y, hhi[par][:, tokens], whi[par][:, 512:512 + D], start=False, stop=True)
                    if j % 2 == 1:
                        last.then_inc(s.y, 1)

            experts(pe, body)


def build(nc, a, out):
    with ExitStack() as ctx:
        sb = lambda n, sh, dt: ctx.enter_context(nc.sbuf_tensor(n, sh, dt))
        sem = lambda n: ctx.enter_context(nc.semaphore(n))
        m = Buffers()
        m.qs = sb("qs", [128, B, H, QS], F32)
        m.rk = sb("rk", [KT, B, NT, H], F32)
        m.ident = sb("ident", [128, 128], F32)
        m.ones = sb("ones", [128, 128], F32)
        m.row_of = sb("row_of", [128, QBLK, QBLK], F32)
        m.pick = sb("pick", [QBLK, QBLK, 128], F32)
        m.eps = sb("eps", [128, 1], F32)

        def with_norm_buffers(run, *args):
            with ExitStack() as inner:
                add = lambda n, sh: inner.enter_context(nc.sbuf_tensor(f"{args[0]}_{n}", sh, F32))
                if run is before_attention:
                    m.x = add("x", [TT, NTT, D])
                m.xn, m.xnT = add("xn", [TT, NTT, D]), add("xnT", [128, KC, QW])
                m.stats, m.meanvar = add("stats", [TT, NTT, 6]), add("meanvar", [TT, NTT, 2])
                m.vareps, m.std, m.rstd = add("vareps", [TT, NTT]), add("std", [TT, NTT]), add("rstd", [TT, NTT])
                run(*args[1:])

        with ExitStack() as only:
            for_first = lambda n, sh, dt: only.enter_context(nc.sbuf_tensor(n, sh, dt))
            m.ones8 = for_first("ones8", [QBLK, KT], F32R)
            m.diag = for_first("diag", [QBLK, QW], F32)
            m.mask_bias = for_first("mask_bias", [KT, B, NT], F32)
            m.valid = for_first("valid", [128, B], F32)
            m.norm_hi = for_first("norm_hi", [C, NG * 512], F32R)
            m.norm_lo = for_first("norm_lo", [C, NG * 512], F32R)
            with_norm_buffers(before_attention, "pre", nc, m, a, "pre", sem)
            attention(nc, m, a, "l0", sem, True)
        m.x = sb("x", [TT, NTT, D], F32)
        with_norm_buffers(between_layers, "mid", nc, m, a, "mid", sem)
        attention(nc, m, a, "l1", sem, False)
        with_norm_buffers(after_attention, "post", nc, m, a, out, "post", sem)


def kernel(**inputs):
    import numpy as np
    import concourse.bacc as bacc
    from concourse import mybir as _mybir
    from concourse.bass_utils import run_bass_kernel_spmd as run

    i = {k: np.asarray(v) for k, v in inputs.items()}
    c = np.ascontiguousarray
    ctx = i["ctx_1024"]
    mask = i["mask_BxS2_bf1"].view(np.uint8)
    heads = lambda w, n: c(w.reshape(w.shape[0], n, 128).transpose(2, 1, 0))
    chunks = lambda w: c(w.reshape(2, 128, -1).transpose(1, 0, 2))
    w1 = np.concatenate([i["L1_ffn_we1"], i["L1_ffn_ws1"].reshape(256, 4, 128).transpose(1, 0, 2)])
    w3 = np.concatenate([i["L1_ffn_we3"], i["L1_ffn_ws3"].reshape(256, 4, 128).transpose(1, 0, 2)])
    w2 = np.concatenate([i["L1_ffn_we2"], i["L1_ffn_ws2"].reshape(4, 128, 256)])
    side = lambda w: w.reshape(-1, 2, 128, 128).transpose(0, 2, 1, 3).reshape(-1, 128, 256)
    arrays = {
        "x": c(i["x"].reshape(8, 112, 256).transpose(1, 0, 2)),
        "ctxT": c(ctx.transpose(2, 0, 1)),
        "ctxN": c(ctx.reshape(16, 12, 125, 128).transpose(0, 2, 1, 3)),
        "mask": c(mask),
        "mask_cols": c(mask.reshape(16, 12, 125).transpose(2, 0, 1)),
        "ident": np.eye(128, dtype=np.float32),
        "diag": np.repeat(np.eye(8, dtype=np.float32), 112, axis=1),
        "row_of": c(np.broadcast_to(np.eye(8, dtype=np.float32), (128, 8, 8))),
        "pick": np.repeat(np.eye(8, dtype=np.float32)[:, :, None], 128, axis=2),
        "tri": np.tril(np.ones((16, 16), np.float32), -1).reshape(1, 16, 16),
        "wqT0": heads(i["L0_xattn_Wq"], 16), "wkT0": heads(i["L0_xattn_Wk"], 8), "wvT0": heads(i["L0_xattn_Wv"], 8),
        "wo0": c(i["L0_xattn_Wo"].reshape(16, 128, 256).transpose(1, 0, 2)),
        "factors": c(i["L0_ffn_factors"].reshape(8, 2, 128, 256).transpose(2, 1, 0, 3)),
        "bias": i["L0_ffn_bias"].reshape(1, 256),
        "wq1": chunks(i["L1_xattn_Wq"]), "wkT1": heads(i["L1_xattn_Wk"], 16), "wvT1": heads(i["L1_xattn_Wv"], 16),
        "wk1": c(i["L1_xattn_Wk"][:, 1536:]),
        "wo1": c(i["L1_xattn_Wo"].reshape(16, 128, 256).transpose(1, 0, 2)),
        "gains": c(np.stack([i["L1_xattn_gq"], i["L1_xattn_gk"]], axis=1)),
        "w_router": chunks(i["L1_ffn_w_router"]),
        "experts": c(np.concatenate([side(w1), side(w3), w2], axis=2)),
    }
    nc = bacc.Bacc("TRN2", target_bir_lowering=False, num_devices=1)
    a = namedtuple("Arrays", list(arrays))(*[
        nc.dram_tensor(f"in_{n}", v.shape, _mybir.dt.from_np(v.dtype), kind="ExternalInput").ap()
        for n, v in arrays.items()])
    out = nc.dram_tensor("out_x", (112, 8, 256), F32, kind="ExternalOutput").ap()
    build(nc, a, out)
    r = run(nc, [{f"in_{n}": v for n, v in arrays.items()}], core_ids=[0])
    return r.results[0]["out_x"].transpose(1, 0, 2).reshape(16, 56, 256)
```
